# Optimizing a Trainium2 kernel written in Bass

```python
import numpy as np
import jax
import jax.numpy as jnp

def _softmax(x, axis=-1):
    return jax.nn.softmax(x, axis=axis)

def _gelu(x):
    return jax.nn.gelu(x, approximate=True)

def _silu(x):
    return jax.nn.silu(x)

def _sigmoid(x):
    return jax.nn.sigmoid(x)

def _layernorm(x, axis=-1, eps=1e-05):
    m = jnp.mean(x, axis=axis, keepdims=True)
    v = jnp.var(x, axis=axis, keepdims=True)
    return (x - m) / jnp.sqrt(v + eps)

def _scatter_add(tgt, idx, src, axis=0):
    return tgt.at[idx].add(src)

def _segment_sum(src, seg, n):
    return jax.ops.segment_sum(src, seg, n)
kernel_name = 'mk_prb_d1_jaxref_r8_ddc4ce'

def setup_inputs(seed: int=0):
    np.random.seed(seed)
    _w = jnp.asarray

    def _L0_attn_setup():
        import jax, jax.numpy as jnp
        import numpy as np
        DIM, HEADS = (128, 16)
        B, N = (2, 256)
        key = jax.random.key(seed)
        ks = jax.random.split(key, 8)
        d = DIM // HEADS
        return {'x': jax.random.normal(ks[0], (B, N, DIM), dtype=jnp.float32), 'w_qkv': jax.random.normal(ks[1], (DIM, 3 * DIM), dtype=jnp.float32) * DIM ** (-0.5), 'w_out': jax.random.normal(ks[2], (DIM, DIM), dtype=jnp.float32) * DIM ** (-0.5), 'b_out': jnp.zeros((DIM,), dtype=jnp.float32), 'void_q': jax.random.normal(ks[3], (1, HEADS, 1, d), dtype=jnp.float32), 'void_k': jax.random.normal(ks[4], (1, HEADS, 1, d), dtype=jnp.float32), 'void_v': jax.random.normal(ks[5], (1, HEADS, 1, d), dtype=jnp.float32), 'attention_trace': jax.random.uniform(ks[6], (HEADS, 1, 1), dtype=jnp.float32), 'temperature_factor': jax.random.normal(ks[7], (HEADS, 1, 1), dtype=jnp.float32)}
    _L0_attn_in = _L0_attn_setup()

    def _L0_ffn_setup():
        import jax, jax.numpy as jnp
        import numpy as np
        DIM = 128
        DEPTH = 6
        HEADS = 16
        DIM_HEAD = 64
        WINDOW = 32
        INNER = HEADS * DIM_HEAD
        DIM_INNER = int(DIM * 4 * 2 / 3)
        QK_SCALE = 8.0

        def shift_tokens(t):
            a, s = jnp.split(t, 2, -1)
            s = jnp.pad(s, ((0, 0), (1, 0), (0, 0)))[:, :-1]
            return jnp.concatenate([a, s], -1)

        def l2norm(t):
            return t / jnp.maximum(jnp.linalg.norm(t, axis=-1, keepdims=True), 1e-12)

        def rotate_half(x):
            x1, x2 = jnp.split(x, 2, -1)
            return jnp.concatenate([-x2, x1], -1)

        def rotary_tables(n):
            half = jnp.arange(0, DIM_HEAD, 2, dtype=jnp.float32)
            inv_freq = 1.0 / 10000.0 ** (half / DIM_HEAD)
            t = jnp.arange(n, dtype=jnp.float32)
            freqs = t[:, None] * inv_freq[None, :]
            freqs = jnp.concatenate([freqs, freqs], -1)
            base_scale = (half + 0.4 * DIM_HEAD) / (1.4 * DIM_HEAD)
            power = (t - n // 2) / (WINDOW // 2)
            scale = base_scale[None, :] ** power[:, None]
            scale = jnp.concatenate([scale, scale], -1)
            return (freqs, scale)

        def local_attention(q, k, v):
            b, h, n, d = q.shape
            w = WINDOW
            nw = n // w
            bq = q.reshape(b, h, nw, w, d)
            bk = k.reshape(b, h, nw, w, d)
            bv = v.reshape(b, h, nw, w, d)

            def look(t):
                p = jnp.pad(t, ((0, 0), (0, 0), (1, 0), (0, 0), (0, 0)))
                return jnp.concatenate([p[:, :, :nw], p[:, :, 1:]], axis=3)
            bk2, bv2 = (look(bk), look(bv))
            seq = jnp.arange(n).reshape(nw, w)
            seq_p = jnp.pad(seq, ((1, 0), (0, 0)), constant_values=-1)
            jt = jnp.concatenate([seq_p[:nw], seq_p[1:]], axis=1)
            it = seq[:, :, None]
            jb = jt[:, None, :]
            mask = (it < jb) | (it > jb + w) | (jb == -1)
            sim = jnp.einsum('bhwie,bhwje->bhwij', bq, bk2) * QK_SCALE
            sim = jnp.where(mask, -jnp.finfo(sim.dtype).max, sim)
            attn = jax.nn.softmax(sim, -1)
            out = jnp.einsum('bhwij,bhwje->bhwie', attn, bv2)
            return out.reshape(b, h, n, d)

        def attn_layer(x, Wqkv, qs, ksc, Wo):
            b, n, _ = x.shape
            qkv = x @ Wqkv
            q, k, v = jnp.split(qkv, 3, -1)
            sh = lambda t: t.reshape(b, n, HEADS, DIM_HEAD).transpose(0, 2, 1, 3)
            q, k, v = (sh(q), sh(k), sh(v))
            q = l2norm(q) * qs
            k = l2norm(k) * ksc
            freqs, scale = rotary_tables(n)
            cos, sin = (jnp.cos(freqs), jnp.sin(freqs))
            q = q * cos * scale + rotate_half(q) * sin * scale
            inv = 1.0 / scale
            k = k * cos * inv + rotate_half(k) * sin * inv
            out = local_attention(q, k, v)
            out = out.transpose(0, 2, 1, 3).reshape(b, n, INNER)
            return out @ Wo

        def ffn_layer(x, g, bln, W1, b1, W2, b2):
            mu = x.mean(-1, keepdims=True)
            var = ((x - mu) ** 2).mean(-1, keepdims=True)
            xn = (x - mu) / jnp.sqrt(var + 1e-05) * g + bln
            hg = xn @ W1 + b1
            a, gate = jnp.split(hg, 2, -1)
            return a * jax.nn.gelu(gate, approximate=False) @ W2 + b2
        key = jax.random.key(seed)
        ks = jax.random.split(key, 8)
        B, N = (2, 256)
        init = lambda k, shape: jax.random.normal(k, shape, jnp.float32) * 0.02
        return {'x': jax.random.normal(ks[0], (B, N, DIM), jnp.float32), 'Wqkv': init(ks[1], (DEPTH, DIM, 3 * INNER)), 'q_scale': jnp.ones((DEPTH, DIM_HEAD), jnp.float32), 'k_scale': jnp.ones((DEPTH, DIM_HEAD), jnp.float32), 'Wo': init(ks[2], (DEPTH, INNER, DIM)), 'ln_g': jnp.ones((DEPTH, DIM), jnp.float32), 'ln_b': jnp.zeros((DEPTH, DIM), jnp.float32), 'W1': init(ks[3], (DEPTH, DIM, 2 * DIM_INNER)), 'b1': jnp.zeros((DEPTH, 2 * DIM_INNER), jnp.float32), 'W2': init(ks[4], (DEPTH, DIM_INNER, DIM)), 'b2': jnp.zeros((DEPTH, DIM), jnp.float32)}
    _L0_ffn_in = _L0_ffn_setup()
    _d = {'L0_attn_x': _L0_attn_in['x'], 'L0_attn_w_qkv': _L0_attn_in['w_qkv'], 'L0_attn_w_out': _L0_attn_in['w_out'], 'L0_attn_b_out': _L0_attn_in['b_out'], 'L0_attn_void_q': _L0_attn_in['void_q'], 'L0_attn_void_k': _L0_attn_in['void_k'], 'L0_attn_void_v': _L0_attn_in['void_v'], 'L0_attn_attention_trace': _L0_attn_in['attention_trace'], 'L0_attn_temperature_factor': _L0_attn_in['temperature_factor'], 'L0_ffn_Wqkv': _L0_ffn_in['Wqkv'], 'L0_ffn_q_scale': _L0_ffn_in['q_scale'], 'L0_ffn_k_scale': _L0_ffn_in['k_scale'], 'L0_ffn_Wo': _L0_ffn_in['Wo'], 'L0_ffn_ln_g': _L0_ffn_in['ln_g'], 'L0_ffn_ln_b': _L0_ffn_in['ln_b'], 'L0_ffn_W1': _L0_ffn_in['W1'], 'L0_ffn_b1': _L0_ffn_in['b1'], 'L0_ffn_W2': _L0_ffn_in['W2'], 'L0_ffn_b2': _L0_ffn_in['b2']}
    _x0 = _d['L0_attn_x']
    _d['L0_attn_x'] = jax.random.normal(jax.random.fold_in(jax.random.key(seed), 1), (8, 256, 128), dtype=_x0.dtype)
    del _x0
    return _d

def reference(L0_attn_x, L0_attn_w_qkv, L0_attn_w_out, L0_attn_b_out, L0_attn_void_q, L0_attn_void_k, L0_attn_void_v, L0_attn_attention_trace, L0_attn_temperature_factor, L0_ffn_Wqkv, L0_ffn_q_scale, L0_ffn_k_scale, L0_ffn_Wo, L0_ffn_ln_g, L0_ffn_ln_b, L0_ffn_W1, L0_ffn_b1, L0_ffn_W2, L0_ffn_b2):

    def _L0_attn_ref(x, w_qkv, w_out, b_out, void_q, void_k, void_v, attention_trace, temperature_factor):
        import jax, jax.numpy as jnp
        import numpy as np
        DIM, HEADS = (128, 16)
        B, N = (2, 256)
        b, n, dim = x.shape
        h = void_q.shape[1]
        d = dim // h
        qkv = x @ w_qkv
        q, k, v = jnp.split(qkv, 3, axis=-1)

        def to_heads(t):
            return t.reshape(b, n, h, d).transpose(0, 2, 1, 3)
        q, k, v = (to_heads(q), to_heads(k), to_heads(v))
        q = jnp.concatenate([q, jnp.broadcast_to(void_q, (b, h, 1, d))], axis=2)
        k = jnp.concatenate([k, jnp.broadcast_to(void_k, (b, h, 1, d))], axis=2)
        v = jnp.concatenate([v, jnp.broadcast_to(void_v, (b, h, 1, d))], axis=2)
        dots = jnp.einsum('bhid,bhjd->bhij', q, k) * dim ** (-0.5)
        dots = dots.at[:, :, n, n].add(10.0)
        temperature = jnp.maximum(1.0 + jnp.abs(attention_trace) * temperature_factor, 1.0)
        attn = jax.nn.softmax(dots / temperature, axis=-1)
        out = jnp.einsum('bhij,bhjd->bhid', attn, v)[:, :, :n, :]
        out = out.transpose(0, 2, 1, 3).reshape(b, n, dim)
        return out @ w_out + b_out

    def _L0_ffn_ref(x, Wqkv, q_scale, k_scale, Wo, ln_g, ln_b, W1, b1, W2, b2):
        import jax, jax.numpy as jnp
        import numpy as np
        DIM = 128
        DEPTH = 6
        HEADS = 16
        DIM_HEAD = 64
        WINDOW = 32
        INNER = HEADS * DIM_HEAD
        DIM_INNER = int(DIM * 4 * 2 / 3)
        QK_SCALE = 8.0

        def shift_tokens(t):
            a, s = jnp.split(t, 2, -1)
            s = jnp.pad(s, ((0, 0), (1, 0), (0, 0)))[:, :-1]
            return jnp.concatenate([a, s], -1)

        def l2norm(t):
            return t / jnp.maximum(jnp.linalg.norm(t, axis=-1, keepdims=True), 1e-12)

        def rotate_half(x):
            x1, x2 = jnp.split(x, 2, -1)
            return jnp.concatenate([-x2, x1], -1)

        def rotary_tables(n):
            half = jnp.arange(0, DIM_HEAD, 2, dtype=jnp.float32)
            inv_freq = 1.0 / 10000.0 ** (half / DIM_HEAD)
            t = jnp.arange(n, dtype=jnp.float32)
            freqs = t[:, None] * inv_freq[None, :]
            freqs = jnp.concatenate([freqs, freqs], -1)
            base_scale = (half + 0.4 * DIM_HEAD) / (1.4 * DIM_HEAD)
            power = (t - n // 2) / (WINDOW // 2)
            scale = base_scale[None, :] ** power[:, None]
            scale = jnp.concatenate([scale, scale], -1)
            return (freqs, scale)

        def local_attention(q, k, v):
            b, h, n, d = q.shape
            w = WINDOW
            nw = n // w
            bq = q.reshape(b, h, nw, w, d)
            bk = k.reshape(b, h, nw, w, d)
            bv = v.reshape(b, h, nw, w, d)

            def look(t):
                p = jnp.pad(t, ((0, 0), (0, 0), (1, 0), (0, 0), (0, 0)))
                return jnp.concatenate([p[:, :, :nw], p[:, :, 1:]], axis=3)
            bk2, bv2 = (look(bk), look(bv))
            seq = jnp.arange(n).reshape(nw, w)
            seq_p = jnp.pad(seq, ((1, 0), (0, 0)), constant_values=-1)
            jt = jnp.concatenate([seq_p[:nw], seq_p[1:]], axis=1)
            it = seq[:, :, None]
            jb = jt[:, None, :]
            mask = (it < jb) | (it > jb + w) | (jb == -1)
            sim = jnp.einsum('bhwie,bhwje->bhwij', bq, bk2) * QK_SCALE
            sim = jnp.where(mask, -jnp.finfo(sim.dtype).max, sim)
            attn = jax.nn.softmax(sim, -1)
            out = jnp.einsum('bhwij,bhwje->bhwie', attn, bv2)
            return out.reshape(b, h, n, d)

        def attn_layer(x, Wqkv, qs, ksc, Wo):
            b, n, _ = x.shape
            qkv = x @ Wqkv
            q, k, v = jnp.split(qkv, 3, -1)
            sh = lambda t: t.reshape(b, n, HEADS, DIM_HEAD).transpose(0, 2, 1, 3)
            q, k, v = (sh(q), sh(k), sh(v))
            q = l2norm(q) * qs
            k = l2norm(k) * ksc
            freqs, scale = rotary_tables(n)
            cos, sin = (jnp.cos(freqs), jnp.sin(freqs))
            q = q * cos * scale + rotate_half(q) * sin * scale
            inv = 1.0 / scale
            k = k * cos * inv + rotate_half(k) * sin * inv
            out = local_attention(q, k, v)
            out = out.transpose(0, 2, 1, 3).reshape(b, n, INNER)
            return out @ Wo

        def ffn_layer(x, g, bln, W1, b1, W2, b2):
            mu = x.mean(-1, keepdims=True)
            var = ((x - mu) ** 2).mean(-1, keepdims=True)
            xn = (x - mu) / jnp.sqrt(var + 1e-05) * g + bln
            hg = xn @ W1 + b1
            a, gate = jnp.split(hg, 2, -1)
            return a * jax.nn.gelu(gate, approximate=False) @ W2 + b2
        for i in range(DEPTH):
            x = attn_layer(shift_tokens(x), Wqkv[i], q_scale[i], k_scale[i], Wo[i]) + x
            x = ffn_layer(shift_tokens(x), ln_g[i], ln_b[i], W1[i], b1[i], W2[i], b2[i]) + x
        return x
    x = L0_attn_x
    xn = _layernorm(x, axis=-1)
    x = x + _L0_attn_ref(xn, L0_attn_w_qkv, L0_attn_w_out, L0_attn_b_out, L0_attn_void_q, L0_attn_void_k, L0_attn_void_v, L0_attn_attention_trace, L0_attn_temperature_factor) + _L0_ffn_ref(xn, L0_ffn_Wqkv, L0_ffn_q_scale, L0_ffn_k_scale, L0_ffn_Wo, L0_ffn_ln_g, L0_ffn_ln_b, L0_ffn_W1, L0_ffn_b1, L0_ffn_W2, L0_ffn_b2)
    return x

_drawn_inputs = setup_inputs


def setup_inputs(seed=0):
    import zlib

    import numpy as np

    out = dict(_drawn_inputs(seed))
    spreads = {'L0_attn_b_out': (0.0, 0.517),
     'L0_ffn_q_scale': (1.0, 0.6),
     'L0_ffn_k_scale': (1.0, 0.6),
     'L0_ffn_ln_g': (1.0, 0.6),
     'L0_ffn_ln_b': (0.0, 0.8),
     'L0_ffn_b1': (0.0, 0.8),
     'L0_ffn_b2': (0.0, 0.1)}
    factors = {'L0_attn_void_k': 8.0,
     'L0_attn_void_v': 8.0,
     'L0_attn_attention_trace': 64.0,
     'L0_attn_temperature_factor': 8.0,
     'L0_ffn_W1': 3.641,
     'L0_ffn_W2': 3.574}
    for name, (base, spread) in spreads.items():
        noise = np.random.default_rng([zlib.crc32(name.encode()), seed]).standard_normal(out[name].shape)
        drawn = base * np.exp(spread * noise) if base else spread * noise
        out[name] = jnp.asarray(drawn.astype(out[name].dtype))
    for name, factor in factors.items():
        out[name] = (out[name] * factor).astype(out[name].dtype)
    return out
```

```python
from contextlib import ExitStack

import numpy as np
import concourse.bass as bass
from concourse import mybir

F32 = mybir.dt.float32
F32R = mybir.dt.float32r
BF16 = mybir.dt.bfloat16
ALU = mybir.AluOpType
ACT = mybir.ActivationFunctionType
AX_X = mybir.AxisListType.X

P = 128
B, N, D = 8, 256, 128
TT = N // P
TILES = B * TT
GH, GD = 16, 8
NK = N + 1
GU = TT * GH // 2
DEPTH, H, DH, WIN = 6, 16, 64, 32
INNER = H * DH
NG = 4
HG = H // NG
GC = HG * DH
PR = HG // 2
NW = P // WIN
ITERS = DEPTH * B
FI = int(D * 4 * 2 / 3)
FCH = [(0, 128), (128, 128), (256, FI - 256)]
QKV = 3 * INNER
PIECE = QKV // B
NORM_G = 2.0 ** 10
NVEC = 9


def shape_constants():
    half = np.arange(0, DH, 2, dtype=np.float32)
    inv_freq = (1.0 / 10000.0 ** (half / DH)).astype(np.float32)
    t = np.arange(N, dtype=np.float32)
    freqs = t[:, None] * inv_freq[None, :]
    freqs = np.concatenate([freqs, freqs], -1).astype(np.float64)
    base = (half.astype(np.float64) + 0.4 * DH) / (1.4 * DH)
    power = (t.astype(np.float64) - N // 2) / (WIN // 2)
    scale = base[None, :] ** power[:, None]
    scale = np.concatenate([scale, scale], -1)
    sign = np.where(np.arange(DH) < DH // 2, -1.0, 1.0)
    cos, sin = np.cos(freqs), np.sin(freqs) * sign
    q_gain = 8.0
    rot = np.zeros((P, 2, TT, 2, DH))
    for k, trig in enumerate((cos, sin)):
        for tt in range(TT):
            rows = slice(tt * P, (tt + 1) * P)
            rot[:, k, tt, 0] = trig[rows] * scale[rows] * q_gain * NORM_G
            rot[:, k, tt, 1] = trig[rows] / scale[rows] * NORM_G
    mask = np.zeros((P, HG, TT, 2 * WIN))
    qi = (np.arange(P) % WIN)[:, None]
    w = (np.arange(P) // WIN)[:, None]
    j = np.arange(2 * WIN)[None, :]
    for tt in range(TT):
        bad = (j - WIN > qi) | (qi > j) | ((w + tt * NW == 0) & (j < WIN))
        mask[:, :, tt] = np.where(bad, -1e30, 0.0)[:, None, :]
    head_of = np.arange(P)[:, None] // GD == np.arange(GH)[None, :]
    return {
        "c_ident": np.eye(P, dtype=np.float32),
        "c_rot": rot.reshape(P, -1).astype(np.float32),
        "c_mask": mask.reshape(P, -1).astype(np.float32),
        "c_head": head_of.astype(np.float32),
        "c_spread": np.ascontiguousarray(head_of.T).astype(np.float32),
    }


def bass_dual_attention(nc: bass.Bass, A: dict, out: bass.AP):
    with ExitStack() as ctx:
        def sb(name, shape, dt=F32):
            return ctx.enter_context(nc.sbuf_tensor(name, shape, dt))

        PS = ctx.enter_context(nc.psum_tensor("PS", [P, 8, 512], F32))

        ident = sb("ident", [P, P])
        ident_bf = sb("ident_bf", [P, P], BF16)
        mask_bf = sb("mask_bf", [P, 512], BF16)
        head_col = sb("head_col", [P, GH])
        spread = sb("spread", [GH, P])
        mean_mat = sb("mean_mat", [P, P])
        rot = sb("rot", [P, DEPTH * 2 * TT * 2 * DH])
        vec_all = sb("vec_all", [P, DEPTH * NVEC])
        vec = sb("vec", [P, NVEC])
        x_tok = sb("x_tok", [P, TILES * D])
        xT = sb("xT", [P, B * (N + 1)])
        stat = sb("stat", [P, 4, TILES])
        wg = sb("wg", [P, 3 * D])
        wgo = sb("wgo", [P, D])
        bo = sb("bo", [P, D])
        temp = sb("temp", [GH, 6])
        qscale = sb("qscale", [P, 1])
        voidk = sb("voidk", [P, 1])
        voidv = sb("voidv", [P, GH, GD + 1])
        gq = sb("gq", [P, N])
        gk = sb("gk", [P, N])
        xg = sb("xg", [P, N])
        gv = sb("gv", [P, TT, GH, 32])
        gmx = sb("gmx", [P, 2, 2])
        gpv = sb("gpv", [P, 2 * TT * GH])
        gden = sb("gden", [P, TT * GH])
        gatt = sb("gatt", [P, TT, D])
        gattT = sb("gattT", [P, N])
        w_raw = sb("w_raw", [P, 2 * QKV])
        wh = sb("wh", [P, 2, 3, INNER], F32R)
        wl = sb("wl", [P, 2, 3, INNER], F32R)
        xh = sb("xh", [P, N], F32R)
        xl = sb("xl", [P, N], F32R)
        rmx = sb("rmx", [P, 2, TT * HG])
        rsum = sb("rsum", [P, 2, TT * HG])
        rinv = sb("rinv", [P, 2, TT * HG])
        ss = sb("ss", [P, 16])
        ssm = sb("ssm", [P, 2, 16])
        ssl = sb("ssl", [P, 2, 16])
        guess = sb("guess", [P, 2, 16])
        one_half = sb("one_half", [P, 16])
        newton = sb("newton", [P, 3, 16])
        rn = sb("rn", [P, 2, 16])
        wo = sb("wo", [P, INNER // P, D])
        w1 = sb("w1", [P, 2 * FI])
        w2 = sb("w2", [P, 3, D])
        x1 = sb("x1", [P, N])
        xs2 = sb("xs2", [P, N])
        xc = sb("xc", [P, N])
        xc2 = sb("xc2", [P, N])
        var = sb("var", [P, N])
        rs = sb("rs", [P, N])
        xn = sb("xn", [P, N])
        hT = sb("hT", [P, 3, N])

        arena = sb("arena", [P, 17280])
        taken = [0]

        def part(n):
            taken[0] += n
            return arena[:, taken[0] - n:taken[0]]

        gkz = part(2 * GH * NK)
        sq_tok = arena[:, taken[0]:taken[0] + TILES * D]
        gp = part(4 * 2 * NK).rearrange("p (u e k) -> p u e k", u=4, e=2)
        gpT = part(2 * 512).rearrange("p (u n) -> p u n", u=2)
        goT = part(2 * N).rearrange("p (u n) -> p u n", u=2)
        gtok = part(TT * GH * (GD + 1)).rearrange("p (h d) -> p h d", d=GD + 1)
        gacc = part(TT * GH * (GD + 1)).rearrange("p (h d) -> p h d", d=GD + 1)
        xc_tok = part(TILES * D)
        mask_f = part(512)
        rot_base = part(2 * TT * 2 * DH).rearrange("p (k t n) -> p k t n", k=2, t=TT)
        gains = part(DEPTH * 2 * DH).rearrange("p (l n) -> p l n", l=DEPTH)
        gains_sw = part(DEPTH * 2 * DH).rearrange("p (l n) -> p l n", l=DEPTH)
        taken[0] = 0
        sq = part(1024)
        t1 = part(2048).rearrange("p (u n) -> p u n", u=2)
        t2 = part(1024)
        qn = part(2048).rearrange("p (u n) -> p u n", u=2)
        qT = part(1024).rearrange("p (u a n) -> p u a n", u=2, a=PR)
        kz = part(4 * PR * (N + WIN)).rearrange("p (u a e n) -> p u a e n", u=2, a=PR, e=2)
        v = part(2048).rearrange("p (g t n) -> p g t n", g=NG, t=TT)
        pr = part(1024).rearrange("p (u h t k) -> p u h t k", u=2, t=TT, h=HG)
        pT0 = part(HG * (P + WIN)).rearrange("p (h n) -> p h n", h=HG)
        pT1 = part(HG * P).rearrange("p (h n) -> p h n", h=HG)
        oT = part(2048).rearrange("p (c n) -> p c n", c=2 * NG)
        hg = part(3 * 512).rearrange("p (c n) -> p c n", c=3)

        wh_flat = wh[:, :, :, :].rearrange("p u a n -> p (u a n)")
        wl_flat = wl[:, :, :, :].rearrange("p u a n -> p (u a n)")

        names = """ld_x ld_const ld_gw ld_vec ld_raw ld_wo ld_w1 ld_w2 st_out
        vec_clear zeroed cleared ones_set mask_set temp_set spread_mm qscale_set voidk_set ln_step ln_guess ln_sq xn_t state_set rot_set
        g_k_mm g_k g_kz g_q_mm g_q g_x g_v_mm g_v g_s g_mx g_sub g_exp g_void g_pt g_pT g_o g_oT g_tok g_tokev g_num g_acc
        g_den g_att g_attT_mm g_attT g_y g_res
        split_hi split_lo xh_set xl_set s_qk s_v sq_set v_set ss_set ssm_set ssl_set guess_set nw1_set nw2_set nw3_set rn_set t1_set t2_set add_set qn_set
        tq_mm tk_mm qT_set kz_set s_mm mx_set sub_set exp_set sum_set inv_set pn_set pt_mm pT_set o_mm o_set
        f_y f_x1 f_xs2 f_mean f_xc f_sq f_var f_ve f_ln f_guess f_n1 f_n2 f_rs f_xr f_xn f_vec f_hg f_hgc f_gate f_h f_y2
        o_t o_add""".split()
        S = {n: ctx.enter_context(nc.semaphore(n)) for n in names}
        block = ctx.enter_context(nc.Block())

        def unit(i, g, back=0):
            return i + (g - back) // NG, (g - back) % NG

        def done(i, g, back=0):
            return i * NG + (g - back + 1)

        def live(i):
            return not isinstance(i, int) or 0 <= i < ITERS

        def layer_of(i):
            if isinstance(i, int):
                return i // B
            return nc.s_assert_within(i >> 3, 0, DEPTH - 1, skip_runtime_bounds_check_because="iterations end before ITERS")

        def wait(eng, name, value):
            if not isinstance(value, int) or value > 0:
                eng.wait_ge(S[name], value)

        def sweep(eng, body):
            body(0)
            body(1)
            body(2)
            with eng.Fori(3, ITERS) as i:
                body(i)
            body(ITERS)
            body(ITERS + 1)

        def gunit(b, c, back=0):
            return b + (c - back) // GU, (c - back) % GU

        def gdone(b, c, back=0):
            return b * GU + (c - back + 1)

        def glive(b):
            return not isinstance(b, int) or 0 <= b < B

        def gsweep(eng, body):
            body(0)
            body(1)
            with eng.Fori(2, B) as b:
                body(b)
            body(B)

        def state(rows, b, shift):
            return xT[rows, bass.ds(b * (N + 1) + 1 - shift, N)]

        lower, upper = slice(0, D // 2), slice(D // 2, D)

        @block.sync
        def _(sp):
            x_t = A["L0_attn_x"].rearrange("b (t p) d -> p (b t) d", p=P)
            xt3 = x_tok[:, :].rearrange("p (a d) -> p a d", d=D)
            sp.dma_start(xt3[:, :, :], x_t[:, :, :]).then_inc(S["ld_x"], 16)
            sp.dma_start(ident[:, :], A["c_ident"]).then_inc(S["ld_const"], 16)
            sp.dma_start(head_col[:, :], A["c_head"]).then_inc(S["ld_const"], 16)
            sp.dma_start(spread[:, :], A["c_spread"]).then_inc(S["ld_const"], 16)
            sp.dma_start(rot_base.rearrange("p a b c -> p (a b c)"), A["c_rot"]).then_inc(S["ld_const"], 16)
            sp.dma_start(mask_f, A["c_mask"]).then_inc(S["ld_const"], 16)
            sp.dma_start(wg[:, :], A["L0_attn_w_qkv"]).then_inc(S["ld_gw"], 16)
            sp.dma_start(wgo[:, :], A["L0_attn_w_out"]).then_inc(S["ld_gw"], 16)
            sp.dma_start(temp[:, 0:1], A["L0_attn_attention_trace"].rearrange("h a b -> h (a b)")).then_inc(S["ld_gw"], 16)
            sp.dma_start(temp[:, 1:2], A["L0_attn_temperature_factor"].rearrange("h a b -> h (a b)")).then_inc(S["ld_gw"], 16)
            sp.dma_start(voidk[:, :], A["L0_attn_void_k"].rearrange("a h b d -> (a h b d)").rearrange("(p o) -> p o", o=1)).then_inc(S["ld_gw"], 16)
            vv_src = A["L0_attn_void_v"].rearrange("a h b d -> (a b) h d")
            sp.dma_start(voidv[:, :, 0:GD], vv_src.to_broadcast([P, GH, GD])).then_inc(S["ld_gw"], 16)
            sp.dma_start(bo[:, :], A["L0_attn_b_out"].rearrange("(a d) -> a d", a=1).to_broadcast([P, D])).then_inc(S["ld_gw"], 16)
            sp.dma_start(w_raw[:, 0:QKV], A["L0_ffn_Wqkv"][0]).then_inc(S["ld_raw"], 16)
            hd = DH // 2
            for k, name in enumerate(("L0_ffn_q_scale", "L0_ffn_k_scale")):
                a = A[name].rearrange("(o l) d -> o l d", o=1)
                c = k * DH
                sp.dma_start(gains[:, :, c:c + DH], a.to_broadcast([P, DEPTH, DH])).then_inc(S["ld_vec"], 16)
                sp.dma_start(gains_sw[:, :, c:c + hd], a[:, :, hd:DH].to_broadcast([P, DEPTH, hd])).then_inc(S["ld_vec"], 16)
                sp.dma_start(gains_sw[:, :, c + hd:c + DH], a[:, :, 0:hd].to_broadcast([P, DEPTH, hd])).then_inc(S["ld_vec"], 16)
            vv = vec_all[:, :].rearrange("p (l v) -> p l v", v=NVEC)
            sp.wait_ge(S["vec_clear"], 1)
            with nc.allow_non_contiguous_dma(reason="small vectors"):
                def column(n, k, src):
                    sp.dma_start(vv[0:n, :, k:k + 1], src.rearrange("l (p o) -> p l o", o=1)).then_inc(S["ld_vec"], 16)

                column(P, 0, A["L0_ffn_ln_g"])
                column(P, 1, A["L0_ffn_ln_b"])
                for c, (c0, cn) in enumerate(FCH):
                    for half in range(2):
                        column(cn, 2 + 3 * half + c, A["L0_ffn_b1"][:, half * FI + c0:half * FI + c0 + cn])
                column(P, 8, A["L0_ffn_b2"])

            def load_wo(l):
                sp.dma_start(wo[:, :, :], A["L0_ffn_Wo"][l].rearrange("(c p) n -> p c n", p=P)).then_inc(S["ld_wo"], 16)

            def load_w1(l):
                sp.dma_start(w1[:, :], A["L0_ffn_W1"][l]).then_inc(S["ld_w1"], 16)

            def load_w2(l):
                sp.dma_start(w2[:, 0:2, :], A["L0_ffn_W2"][l][0:2 * P, :].rearrange("(c p) n -> p c n", p=P)).then_inc(S["ld_w2"], 16)
                sp.dma_start(w2[0:FCH[2][1], 2, :], A["L0_ffn_W2"][l][2 * P:FI, :]).then_inc(S["ld_w2"], 16)

            load_wo(0)
            load_w1(0)
            load_w2(0)
            sp.wait_ge(S["ld_raw"], 16)
            sp.dma_start(w_raw[:, QKV:2 * QKV], A["L0_ffn_Wqkv"][1]).then_inc(S["ld_raw"], 16)
            for l in range(1, DEPTH):
                c = (l + 1) % 2 * QKV
                sp.wait_ge(S["ld_raw"], 16 * (l + 1))
                sp.wait_ge(S["split_lo"], 1 + B * (l - 1))
                sp.dma_start(w_raw[:, c:c + QKV], A["L0_ffn_Wqkv"][(l + 1) % DEPTH]).then_inc(S["ld_raw"], 16)
                sp.wait_ge(S["f_y"], B * l)
                load_wo(l)
                sp.wait_ge(S["f_hg"], 3 * B * l)
                load_w1(l)
                sp.wait_ge(S["f_y2"], B * l)
                load_w2(l)
            o_t = out.rearrange("b (t p) d -> p (b t) d", p=P)
            for q in range(4):
                sp.wait_ge(S["o_add"], q + 1)
                sp.dma_start(o_t[:, 4 * q:4 * q + 4, :], xt3[:, 4 * q:4 * q + 4, :]).then_inc(S["st_out"], 16)
            sp.wait_ge(S["st_out"], 64)

        @block.gpsimd
        def _(pool):
            pool.memset(vec_all[:, :], 0.0).then_inc(S["vec_clear"], 1)
            pool.memset(mean_mat[:, :], 1.0 / D)
            pool.memset(one_half[:, :], 1.5)
            pool.memset(xT[:, :], 0.0)
            pool.memset(xs2[:, :], 0.0)
            pool.memset(gv[:, :, :, :], 0.0).then_inc(S["zeroed"], 1)
            pool.wait_ge(S["zeroed"], 1)
            pool.memset(gv[:, :, :, GD:GD + 1], 1.0)
            pool.memset(voidv[:, :, GD:GD + 1], 1.0).then_inc(S["ones_set"], 1)
            pool.wait_ge(S["ld_const"], 16 * 5)
            pool.wait_ge(S["ld_gw"], 16 * 7)
            gkz3 = gkz.rearrange("p (u k) -> p u k", k=NK)
            for u in range(2):
                last = pool.tensor_tensor(gkz3[:, u * GH:(u + 1) * GH, N], head_col[:, :],
                                          voidk[:, 0:1].to_broadcast([P, GH]), ALU.mult)
            last.then_inc(S["voidk_set"], 1)

            def spread_keys(b):
                pool.wait_ge(S["g_k"], b + 1)
                wait(pool, "g_s", (b - 1) * GU)
                u = b & 1
                for h0 in range(0, GH, 4):
                    dst = gkz[:, bass.ds(u * (GH * NK) + h0 * NK, 4 * NK)].rearrange("p (h k) -> p h k", h=4)
                    last = pool.tensor_tensor(
                        dst[:, :, 0:N], gk[:, :].unsqueeze(1).to_broadcast([P, 4, N]),
                        head_col[:, h0:h0 + 4].unsqueeze(2).to_broadcast([P, 4, N]), ALU.mult)
                last.then_inc(S["g_kz"], 1)

            spread_keys(0)

            def g_body(b):
                for c in range(GU):
                    j, cj = gunit(b, c, 1)
                    if glive(j):
                        pool.wait_ge(S["g_exp"], gdone(b, c, 1))
                        h0, t = cj // 2 * 2, cj % 2
                        wait(pool, "g_num", j - 1)
                        pool.tensor_copy(gpv[:, bass.ds((j & 1) * (TT * GH) + t * GH + h0, 2)], gp[:, cj % 4, :, N]).then_inc(S["g_void"], 1)
                    if c == GU // 2 and glive(b) and (not isinstance(b, int) or b + 1 < B):
                        spread_keys(b + 1)

            g_body(0)
            g_body(1)
            with pool.Fori(2, B - 1) as b:
                g_body(b)
            g_body(B - 1)
            g_body(B)

            pool.wait_ge(S["ld_vec"], 16 * 15)
            rot3 = rot[:, :].rearrange("p (l k t n) -> p l k t n", l=DEPTH, k=2, t=TT)
            for l in range(DEPTH):
                for k, gain in enumerate((gains, gains_sw)):
                    last = pool.tensor_tensor(rot3[:, l, k], rot_base[:, k, :, :],
                                              gain[:, l, :].unsqueeze(1).to_broadcast([P, TT, 2 * DH]), ALU.mult)
            last.then_inc(S["rot_set"], 1)
            pool.wait_ge(S["g_res"], B)
            pool.wait_ge(S["g_void"], GU * B)
            pool.memset(kz[:, :, :, :, :], 0.0)
            pool.memset(pT0[:, :, :], 0.0)
            pool.memset(pT1[:, :, :], 0.0).then_inc(S["cleared"], 1)

            def body(i):
                for g in range(NG):
                    j, gj = unit(i, g, 2)
                    if live(j):
                        k = gj % 2
                        p2 = pr[:, k].rearrange("p h t k -> p (h t) k")
                        pool.wait_ge(S["inv_set"], done(i, g, 2))
                        pool.tensor_tensor(p2, p2, rinv[:, k, :].unsqueeze(2).to_broadcast([P, TT * HG, 2 * WIN]),
                                           ALU.mult).then_inc(S["pn_set"], 1)
                    if live(i):
                        k = g % 2
                        pool.wait_ge(S["t2_set"], done(i, g))
                        pool.tensor_tensor(t1[:, k, :], t1[:, k, :], t2, ALU.add).then_inc(S["add_set"], 1)
                        pool.wait_ge(S["ssm_set"], done(i, g))
                        pool.wait_ge(S["guess_set"], done(i, g))
                        pool.tensor_tensor(newton[:, 0, :], guess[:, k, :], guess[:, k, :], ALU.mult).then_inc(S["nw1_set"], 1)
                        pool.wait_ge(S["nw1_set"], done(i, g))
                        pool.tensor_tensor(newton[:, 1, :], newton[:, 0, :], ssm[:, k, :], ALU.mult).then_inc(S["nw2_set"], 1)
                        pool.wait_ge(S["nw2_set"], done(i, g))
                        pool.tensor_tensor(newton[:, 2, :], newton[:, 1, :], one_half[:, :], ALU.add).then_inc(S["nw3_set"], 1)
                        pool.wait_ge(S["nw3_set"], done(i, g))
                        pool.tensor_tensor(rn[:, k, :], newton[:, 2, :], guess[:, k, :], ALU.mult).then_inc(S["rn_set"], 1)
                        pool.wait_ge(S["add_set"], done(i, g))
                        pool.wait_ge(S["rn_set"], done(i, g))
                        wait(pool, "tk_mm", done(i, g, 2))
                        pool.tensor_tensor(
                            qn[:, k, :].rearrange("p (u d) -> p u d", d=DH), t1[:, k, :].rearrange("p (u d) -> p u d", d=DH),
                            rn[:, k, :].unsqueeze(2).to_broadcast([P, 16, DH]), ALU.mult).then_inc(S["qn_set"], 1)
                    if g == 2 and live(i):
                        c0 = (((i >> 3) + 1) & 1) * QKV + (i & 7) * PIECE
                        pool.wait_ge(S["split_hi"], i + 2)
                        pool.tensor_tensor(wl_flat[:, bass.ds(c0, PIECE)], w_raw[:, bass.ds(c0, PIECE)],
                                           wh_flat[:, bass.ds(c0, PIECE)].bitcast(F32), ALU.subtract).then_inc(S["split_lo"], 1)

            sweep(pool, body)

        @block.scalar
        def _(act):
            act.wait_ge(S["ln_step"], 3)
            act.activation(sq_tok, xc_tok, ACT.Square).then_inc(S["ln_sq"], 1)
            act.wait_ge(S["ln_step"], 6)
            act.activation(stat[:, 1, :], stat[:, 3, :], ACT.Ln).then_inc(S["ln_guess"], 1)
            act.wait_ge(S["ln_guess"], 1)
            act.activation(stat[:, 0, :], stat[:, 1, :], ACT.Exp, scale=-0.5).then_inc(S["ln_guess"], 1)
            act.wait_ge(S["ld_raw"], 16)
            act.activation(wh_flat[:, 0:QKV], w_raw[:, 0:QKV], ACT.Copy).then_inc(S["split_hi"], 1)
            act.wait_ge(S["zeroed"], 1)
            xT3 = xT[:, :].rearrange("p (b n) -> p b n", b=B)
            for b in range(B):
                act.wait_ge(S["xn_t"], b // 2 + 1)
                act.activation(xT3[:, b, 1:], PS[:, b // 2, (b % 2) * N:(b % 2 + 1) * N], ACT.Copy).then_inc(S["state_set"], 1)

            def take_keys(b):
                act.wait_ge(S["g_k_mm"], b + 1)
                wait(act, "g_kz", b)
                act.activation(gk[:, :], PS[:, 7, 0:N], ACT.Copy).then_inc(S["g_k"], 1)

            take_keys(0)

            def g_body(b, more=True):
                for c in range(GU):
                    if glive(b) and c == 0:
                        act.wait_ge(S["g_q_mm"], b + 1)
                        act.wait_ge(S["qscale_set"], 1)
                        act.activation(gq[:, :], PS[:, 7, 0:N], ACT.Copy, scale=qscale[:, 0:1]).then_inc(S["g_q"], 1)
                        wait(act, "g_v_mm", b)
                        act.activation(xg[:, :], state(slice(0, P), b, 0), ACT.Copy).then_inc(S["g_x"], 1)
                    if glive(b) and c == 3:
                        act.wait_ge(S["g_v_mm"], b + 1)
                        wait(act, "g_o", b * GU)
                        if isinstance(b, int) and b == 0:
                            act.wait_ge(S["ones_set"], 1)
                        act.activation(gv[:, :, :, 0:GD], PS[:, 7, 0:N].rearrange("p (t h d) -> p t h d", t=TT, h=GH), ACT.Copy).then_inc(S["g_v"], 1)
                    j, cj = gunit(b, c, 1)
                    if glive(j):
                        act.wait_ge(S["g_sub"], gdone(b, c, 1))
                        act.activation(gp[:, cj % 4], gp[:, cj % 4], ACT.Exp).then_inc(S["g_exp"], 1)
                    j, cj = gunit(b, c, 2)
                    if glive(j):
                        act.wait_ge(S["g_pt"], gdone(b, c, 2))
                        wait(act, "g_o", gdone(b, c, 4))
                        act.activation(gpT[:, cj % 2], PS[:, 4, :], ACT.Copy).then_inc(S["g_pT"], 1)
                    j, cj = gunit(b, c, 3)
                    if glive(j) and cj % 4 == 3:
                        n = cj // 4
                        act.wait_ge(S["g_o"], gdone(b, c, 3))
                        wait(act, "g_tok", 4 * j + n - 1)
                        act.activation(goT[:, n % 2, :], PS[:, 5, 0:N], ACT.Copy).then_inc(S["g_oT"], 1)
                    if c == 6 and glive(b - 1):
                        act.wait_ge(S["g_attT_mm"], b)
                        act.activation(gattT[:, :], PS[:, 7, 0:N], ACT.Copy).then_inc(S["g_attT"], 1)
                    if c == 9 and glive(b) and more:
                        take_keys(b + 1)

            g_body(0)
            g_body(1)
            with act.Fori(2, B - 1) as b:
                g_body(b)
            g_body(B - 1, more=False)
            g_body(B)

            def lead_state(i):
                b = i & (B - 1)
                act.activation(xh[lower, :], state(lower, b, 0), ACT.Copy)
                act.activation(xh[upper, :], state(upper, b, 1), ACT.Copy).then_inc(S["xh_set"], 1)

            lead_state(0)
            act.wait_ge(S["cleared"], 1)

            def body(i):
                for g in range(NG):
                    j, gj = unit(i, g, 2)
                    if live(j):
                        k = gj % 2
                        act.wait_ge(S["sub_set"], done(i, g, 2))
                        act.activation(pr[:, k].rearrange("p h t k -> p (h t k)"), pr[:, k].rearrange("p h t k -> p (h t k)"),
                                       ACT.Exp).then_inc(S["exp_set"], 1)
                    if g == 0 and live(i - 2):
                        act.wait_ge(S["f_ve"], i - 1)
                        act.activation(rs[:, :], var[:, :], ACT.Ln).then_inc(S["f_ln"], 1)
                        act.wait_ge(S["f_ln"], i - 1)
                        act.activation(rs[:, :], rs[:, :], ACT.Exp, scale=-0.5).then_inc(S["f_guess"], 1)
                    if g == 3 and live(i - 1):
                        act.wait_ge(S["f_x1"], i)
                        wait(act, "f_xc", i - 1)
                        act.activation(xs2[lower, :], x1[lower, :], ACT.Copy)
                        act.activation(xs2[upper, 1:], x1[upper, 0:N - 1], ACT.Copy).then_inc(S["f_xs2"], 1)
                    if live(i):
                        act.wait_ge(S["s_qk"], done(i, g))
                        wait(act, "ss_set", done(i, g, 1))
                        for t in range(TT):
                            act.activation(sq[:, t * 512:(t + 1) * 512], PS[:, t, :], ACT.Square).then_inc(S["sq_set"], 1)
                        act.wait_ge(S["s_v"], done(i, g))
                        wait(act, "o_mm", done(i, g, 4))
                        act.activation(v[:, g].rearrange("p t n -> p (t n)"), PS[:, 2, :], ACT.Copy).then_inc(S["v_set"], 1)
                    j, gj = unit(i, g, 1)
                    if live(j):
                        k = gj % 2
                        act.wait_ge(S["tq_mm"], done(i, g, 1))
                        wait(act, "s_mm", done(i, g, 3))
                        act.activation(qT[:, k].rearrange("p a n -> p (a n)"), PS[:, 3, :], ACT.Copy).then_inc(S["qT_set"], 1)
                        act.wait_ge(S["tk_mm"], done(i, g, 1))
                        kt = PS[:, 4, :].rearrange("p (a n) -> p a n", a=PR)
                        act.activation(kz[0:DH, k, :, 0, WIN:], kt[0:DH], ACT.Copy)
                        act.activation(kz[DH:P, k, :, 1, WIN:], kt[DH:P], ACT.Copy).then_inc(S["kz_set"], 1)
                    if live(i):
                        act.wait_ge(S["ssm_set"], done(i, g))
                        act.activation(ssl[:, g % 2, :], ssm[:, g % 2, :], ACT.Ln, scale=-2.0).then_inc(S["ssl_set"], 1)
                        act.wait_ge(S["ssl_set"], done(i, g))
                        wait(act, "rn_set", done(i, g, 2))
                        act.activation(guess[:, g % 2, :], ssl[:, g % 2, :], ACT.Exp, scale=-0.5).then_inc(S["guess_set"], 1)
                    if g == 3 and live(i - 1):
                        act.wait_ge(S["f_xc"], i)
                        act.activation(xc2[:, :], xc[:, :], ACT.Square).then_inc(S["f_sq"], 1)
                    if g == 3 and (not isinstance(i, int) or i + 1 < ITERS) and live(i):
                        act.wait_ge(S["s_v"], done(i, 3))
                        act.wait_ge(S["state_set"], i + 2)
                        lead_state(i + 1)
                    j, gj = unit(i, g, 2)
                    if live(j):
                        act.wait_ge(S["pt_mm"], done(i, g, 2))
                        wait(act, "o_mm", done(i, g, 3))
                        src = PS[:, 6, :].rearrange("p (h n) -> p h n", h=HG)
                        for t in range(TT):
                            dst = (pT0, pT1)[t]
                            for w in range(NW):
                                k0, s0, q0 = (w - 1) * WIN, t * 2 * WIN, w * WIN
                                if w == 0:
                                    moves = [(s0 + WIN, WIN, dst, 0, 0)] + [(s0, WIN, pT0, P - WIN, P)] * t
                                elif k0 % (2 * WIN) == 0:
                                    moves = [(s0, 2 * WIN, dst, k0, q0)]
                                else:
                                    moves = [(s0, WIN, dst, k0, q0), (s0 + WIN, WIN, dst, k0 + WIN, q0)]
                                for r, n, to, d0, c0 in moves:
                                    last = act.activation(to[d0:d0 + n, :, c0:c0 + WIN], src[r:r + n, :, q0:q0 + WIN], ACT.Copy)
                        last.then_inc(S["pT_set"], 1)
                    if g == 1 and live(i - 2):
                        for c, (_, n) in enumerate(FCH):
                            act.wait_ge(S["f_hgc"], 3 * (i - 2) + c + 1)
                            act.activation(hg[0:n, c, N:], hg[0:n, c, N:], ACT.Gelu, bias=vec[0:n, 5 + c:6 + c]).then_inc(S["f_gate"], 1)
                    j, gj = unit(i, g, 2)
                    if live(j):
                        act.wait_ge(S["o_mm"], done(i, g, 2))
                        if gj == 0:
                            wait(act, "f_y", j)
                        act.activation(oT[:, 2 * gj:2 * gj + 2, :].rearrange("p c n -> p (c n)"), PS[:, 2, :], ACT.Copy).then_inc(S["o_set"], 1)
                    if g == 1 and live(i):
                        c0 = (((i >> 3) + 1) & 1) * QKV + (i & 7) * PIECE
                        act.wait_ge(S["ld_raw"], 16 * ((i >> 3) + 2))
                        act.activation(wh_flat[:, bass.ds(c0, PIECE)], w_raw[:, bass.ds(c0, PIECE)], ACT.Copy).then_inc(S["split_hi"], 1)

            sweep(act, body)

        @block.vector
        def _(dve):
            dve.wait_ge(S["ld_gw"], 16 * 7)
            dve.tensor_scalar(temp[:, 3:4], temp[:, 0:1], -1.0, None, ALU.mult).then_inc(S["temp_set"], 1)
            dve.wait_ge(S["temp_set"], 1)
            dve.tensor_tensor(temp[:, 2:3], temp[:, 0:1], temp[:, 3:4], ALU.max).then_inc(S["temp_set"], 1)
            dve.wait_ge(S["temp_set"], 2)
            dve.tensor_tensor(temp[:, 3:4], temp[:, 2:3], temp[:, 1:2], ALU.mult).then_inc(S["temp_set"], 1)
            dve.wait_ge(S["temp_set"], 3)
            dve.tensor_scalar(temp[:, 4:5], temp[:, 3:4], 1.0, 1.0, ALU.add, ALU.max).then_inc(S["temp_set"], 1)
            dve.wait_ge(S["temp_set"], 4)
            dve.reciprocal(temp[:, 5:6], temp[:, 4:5]).then_inc(S["temp_set"], 1)
            x3 = x_tok[:, :].rearrange("p (a d) -> p a d", d=D)
            xc3 = xc_tok.rearrange("p (a d) -> p a d", d=D)
            dve.wait_ge(S["ld_x"], 16)
            dve.tensor_reduce(stat[:, 0, :], x3, AX_X, ALU.add).then_inc(S["ln_step"], 1)
            dve.wait_ge(S["ln_step"], 1)
            dve.tensor_scalar(stat[:, 1, :], stat[:, 0, :], 1.0 / D, None, ALU.mult).then_inc(S["ln_step"], 1)
            dve.wait_ge(S["ln_step"], 2)
            dve.tensor_tensor(xc3, x3, stat[:, 1, :].unsqueeze(2).to_broadcast([P, TILES, D]), ALU.subtract).then_inc(S["ln_step"], 1)
            dve.tensor_tensor(x3, x3, bo[:, :].unsqueeze(1).to_broadcast([P, TILES, D]), ALU.add).then_inc(S["ln_step"], 1)
            dve.wait_ge(S["ln_sq"], 1)
            dve.tensor_reduce(stat[:, 2, :], sq_tok.rearrange("p (a d) -> p a d", d=D), AX_X, ALU.add).then_inc(S["ln_step"], 1)
            dve.wait_ge(S["ln_step"], 5)
            dve.tensor_scalar(stat[:, 3, :], stat[:, 2, :], 1.0 / D, 1e-5, ALU.mult, ALU.add).then_inc(S["ln_step"], 1)
            dve.wait_ge(S["ln_guess"], 2)
            dve.scalar_tensor_tensor(out=stat[:, 1, :], in0=stat[:, 0, :], scalar=-0.5, in1=stat[:, 0, :], op0=ALU.mult, op1=ALU.mult).then_inc(S["ln_step"], 1)
            dve.wait_ge(S["ln_step"], 7)
            dve.tensor_tensor(stat[:, 2, :], stat[:, 1, :], stat[:, 3, :], ALU.mult).then_inc(S["ln_step"], 1)
            dve.wait_ge(S["ln_step"], 8)
            dve.scalar_tensor_tensor(out=stat[:, 1, :], in0=stat[:, 2, :], scalar=1.5, in1=stat[:, 0, :], op0=ALU.add, op1=ALU.mult).then_inc(S["ln_step"], 1)
            dve.wait_ge(S["ln_step"], 9)
            dve.tensor_tensor(xc3, xc3, stat[:, 1, :].unsqueeze(2).to_broadcast([P, TILES, D]), ALU.mult).then_inc(S["ln_step"], 1)
            dve.wait_ge(S["spread_mm"], 1)
            dve.tensor_scalar(qscale[:, :], PS[:, 7, 0:1], float(D) ** -0.5, None, ALU.mult).then_inc(S["qscale_set"], 1)
            dve.wait_ge(S["ld_const"], 16 * 5)
            dve.tensor_copy(ident_bf[:, :], ident[:, :])
            dve.tensor_copy(mask_bf[:, :], mask_f).then_inc(S["mask_set"], 1)
            dve.wait_ge(S["split_hi"], 1)
            dve.tensor_tensor(wl_flat[:, 0:QKV], w_raw[:, 0:QKV], wh_flat[:, 0:QKV].bitcast(F32), ALU.subtract).then_inc(S["split_lo"], 1)

            def g_body(b):
                for c in range(GU):
                    if glive(b):
                        bank = 2 * (c % 2)
                        dve.wait_ge(S["g_s"], gdone(b, c))
                        wait(dve, "g_sub", gdone(b, c, 2))
                        dve.tensor_reduce(gmx[:, c % 2, :], PS[:, bank:bank + 2, 0:NK], AX_X, ALU.max).then_inc(S["g_mx"], 1)
                        dve.wait_ge(S["g_mx"], gdone(b, c))
                        wait(dve, "g_pt", gdone(b, c, 4))
                        wait(dve, "g_void", gdone(b, c, 4))
                        dve.tensor_tensor(gp[:, c % 4], PS[:, bank:bank + 2, 0:NK],
                                          gmx[:, c % 2, :].unsqueeze(2).to_broadcast([P, 2, NK]), ALU.subtract).then_inc(S["g_sub"], 1)
                    j, cj = gunit(b, c, 6)
                    if glive(j) and cj % 4 == 3:
                        n = cj // 4
                        dve.wait_ge(S["g_tok"], 4 * j + n + 1)
                        if n == 0:
                            wait(dve, "g_acc", j)
                        dve.tensor_copy(gtok.rearrange("p (t h) d -> p t h d", t=TT)[:, :, 4 * n:4 * n + 4, :],
                                        PS[:, 6, 0:N].rearrange("p (t h d) -> p t h d", t=TT, h=4)[:, :, :, 0:GD + 1]).then_inc(S["g_tokev"], 1)
                    if c == 5 and glive(b - 1):
                        f = b - 1
                        dve.wait_ge(S["g_void"], b * GU)
                        void = gpv[:, bass.ds((f & 1) * (TT * GH), TT * GH)]
                        dve.tensor_tensor(
                            gacc.rearrange("p (t h) d -> p t h d", t=TT),
                            void.rearrange("p (t h) -> p t h", t=TT).unsqueeze(3).to_broadcast([P, TT, GH, GD + 1]),
                            voidv[:, :, :].unsqueeze(1).to_broadcast([P, TT, GH, GD + 1]), ALU.mult).then_inc(S["g_num"], 1)
                        dve.wait_ge(S["g_num"], b)
                        dve.wait_ge(S["g_tokev"], 4 * b)
                        dve.tensor_tensor(gacc[:, :, :], gacc[:, :, :], gtok[:, :, :], ALU.add).then_inc(S["g_acc"], 1)
                        dve.wait_ge(S["g_acc"], b)
                        dve.reciprocal(gden[:, :], gacc[:, :, GD]).then_inc(S["g_den"], 1)
                        dve.wait_ge(S["g_den"], b)
                        wait(dve, "g_attT_mm", b - 1)
                        dve.tensor_tensor(gatt[:, :, :].rearrange("p t (h d) -> p (t h) d", h=GH), gacc[:, :, 0:GD],
                                          gden[:, :].unsqueeze(2).to_broadcast([P, TT * GH, GD]), ALU.mult).then_inc(S["g_att"], 1)
                    if c == 8 and glive(b - 1):
                        rows = x_tok[:, bass.ds((b - 1) * (TT * D), TT * D)]
                        dve.wait_ge(S["g_y"], b)
                        dve.tensor_tensor(rows, rows, PS[:, 7, 0:N], ALU.add).then_inc(S["g_res"], 1)

            gsweep(dve, g_body)

            def trail_state(i):
                b = i & (B - 1)
                dve.wait_ge(S["xh_set"], i + 1)
                dve.tensor_tensor(xl[lower, :], state(lower, b, 0), xh[lower, :].bitcast(F32), ALU.subtract)
                dve.tensor_tensor(xl[upper, :], state(upper, b, 1), xh[upper, :].bitcast(F32), ALU.subtract).then_inc(S["xl_set"], 1)

            trail_state(0)
            dve.wait_ge(S["rot_set"], 1)
            ROT = TT * 2 * DH

            def body(i):
                for g in range(NG):
                    j, gj = unit(i, g, 2)
                    if live(j):
                        k = gj % 2
                        s3 = PS[:, 5, :].rearrange("p (u k) -> p u k", k=2 * WIN)
                        dve.wait_ge(S["s_mm"], done(i, g, 2))
                        dve.tensor_reduce(rmx[:, k, :], s3, AX_X, ALU.max).then_inc(S["mx_set"], 1)
                        dve.wait_ge(S["mx_set"], done(i, g, 2))
                        wait(dve, "pt_mm", done(i, g, 4))
                        dve.tensor_tensor(pr[:, k].rearrange("p h t k -> p (h t) k"), s3,
                                          rmx[:, k, :].unsqueeze(2).to_broadcast([P, TT * HG, 2 * WIN]), ALU.subtract).then_inc(S["sub_set"], 1)
                    if g == 3 and live(i - 2):
                        f = i - 2
                        dve.wait_ge(S["f_y2"], f + 1)
                        if live(i - 1):
                            dve.wait_ge(S["f_y"], f + 2)
                        new = xT[:, bass.ds((f & 7) * (N + 1) + 1, N)]
                        dve.scalar_tensor_tensor(out=new, in0=PS[:, 7, 0:N], scalar=vec[:, 8:9], in1=x1[:, :],
                                                 op0=ALU.add, op1=ALU.add).then_inc(S["state_set"], 1)
                    if g == 3 and live(i - 1):
                        f = i - 1
                        dve.wait_ge(S["f_y"], f + 1)
                        dve.wait_ge(S["state_set"], B + f)
                        dve.tensor_tensor(x1[:, :], PS[:, 7, N:2 * N], xT[:, bass.ds((f & 7) * (N + 1) + 1, N)], ALU.add).then_inc(S["f_x1"], 1)
                    if g == 0 and live(i - 2):
                        f = i - 2
                        dve.tensor_copy(vec[:, :], vec_all[:, bass.ds(layer_of(f) * NVEC, NVEC)]).then_inc(S["f_vec"], 1)
                        dve.wait_ge(S["f_var"], f + 1)
                        wait(dve, "f_hg", 3 * f)
                        dve.tensor_scalar(var[:, :], PS[:, 7, N:2 * N], 1e-5, None, ALU.add).then_inc(S["f_ve"], 1)

                    def normalise():
                        f = i - 2
                        dve.wait_ge(S["f_guess"], f + 1)
                        dve.scalar_tensor_tensor(out=xn[:, :], in0=rs[:, :], scalar=-0.5, in1=rs[:, :], op0=ALU.mult, op1=ALU.mult).then_inc(S["f_n1"], 1)
                        dve.wait_ge(S["f_n1"], f + 1)
                        dve.tensor_tensor(var[:, :], xn[:, :], var[:, :], ALU.mult).then_inc(S["f_n2"], 1)
                        dve.wait_ge(S["f_n2"], f + 1)
                        dve.scalar_tensor_tensor(out=rs[:, :], in0=var[:, :], scalar=1.5, in1=rs[:, :], op0=ALU.add, op1=ALU.mult).then_inc(S["f_rs"], 1)
                        dve.wait_ge(S["f_rs"], f + 1)
                        dve.tensor_tensor(var[:, :], xc[:, :], rs[:, :], ALU.mult).then_inc(S["f_xr"], 1)
                        dve.wait_ge(S["f_xr"], f + 1)
                        dve.wait_ge(S["f_vec"], f + 1)
                        dve.tensor_scalar(xn[:, :], var[:, :], vec[:, 0:1], vec[:, 1:2], ALU.mult, ALU.add).then_inc(S["f_xn"], 1)

                    def take_hidden(c):
                        n = FCH[c][1]
                        dve.wait_ge(S["f_hg"], 3 * (i - 2) + c + 1)
                        wait(dve, "f_h", 3 * (i - 2))
                        dve.tensor_copy(hg[0:n, c, :], PS[0:n, 7, :]).then_inc(S["f_hgc"], 1)

                    if g == 1 and live(i - 2):
                        take_hidden(1)
                    k = g % 2
                    if live(i):
                        dve.wait_ge(S["s_qk"], done(i, g))
                        wait(dve, "qn_set", done(i, g, 2))
                        qk4 = PS[:, 0:2, :].rearrange("p t (q h d) -> p (t q) h d", q=2, h=HG)
                        layer = layer_of(i)
                        cos = rot[:, bass.ds(layer * (2 * ROT), ROT)].rearrange("p (u d) -> p u d", d=DH)
                        sin = rot[:, bass.ds(layer * (2 * ROT) + ROT, ROT)].rearrange("p (u d) -> p u d", d=DH)
                        t4 = t1[:, k].rearrange("p (u h d) -> p u h d", u=4, h=HG)
                        for t in range(TT):
                            dve.wait_ge(S["sq_set"], TT * (done(i, g) - 1) + t + 1)
                            u2 = slice(2 * t, 2 * t + 2)
                            last = dve.tensor_tensor(t4[:, u2], qk4[:, u2], cos[:, u2].unsqueeze(2).to_broadcast([P, 2, HG, DH]), ALU.mult)
                        last.then_inc(S["t1_set"], 1)
                    j, gj = unit(i, g, 2)
                    if live(j):
                        kj = gj % 2
                        dve.wait_ge(S["exp_set"], done(i, g, 2))
                        dve.tensor_reduce(rsum[:, kj, :], pr[:, kj].rearrange("p h t k -> p (h t) k"), AX_X, ALU.add).then_inc(S["sum_set"], 1)
                        dve.wait_ge(S["sum_set"], done(i, g, 2))
                        dve.reciprocal(rinv[:, kj, :], rsum[:, kj, :]).then_inc(S["inv_set"], 1)
                    if live(i):
                        dve.wait_ge(S["sq_set"], TT * done(i, g))
                        dve.tensor_reduce(ss[:, :], sq.rearrange("p (u d) -> p u d", d=DH), AX_X, ALU.add).then_inc(S["ss_set"], 1)
                        dve.wait_ge(S["ss_set"], done(i, g))
                        wait(dve, "nw2_set", done(i, g, 2))
                        dve.tensor_scalar(ssm[:, k, :], ss[:, :], 1e-24, -0.5 * NORM_G ** 2, ALU.max, ALU.mult).then_inc(S["ssm_set"], 1)
                    if g == 0 and live(i - 2):
                        normalise()
                    if live(i):
                        hd = DH // 2
                        wait(dve, "add_set", done(i, g, 1))
                        o4 = t2.rearrange("p (u h d) -> p u h d", u=4, h=HG)
                        for lo, hi in ((0, hd), (hd, 0)):
                            last = dve.tensor_tensor(o4[:, :, :, lo:lo + hd], qk4[:, :, :, hi:hi + hd],
                                                     sin[:, :, lo:lo + hd].unsqueeze(2).to_broadcast([P, 4, HG, hd]), ALU.mult)
                        last.then_inc(S["t2_set"], 1)
                    if g == 0 and live(i - 2):
                        take_hidden(0)
                    if g == 1 and live(i - 2):
                        take_hidden(2)
                    if g == 2 and live(i - 2):
                        f = i - 2
                        for c, (_, n) in enumerate(FCH):
                            dve.wait_ge(S["f_gate"], 3 * f + c + 1)
                            wait(dve, "f_y2", f)
                            dve.scalar_tensor_tensor(out=hT[0:n, c, :], in0=hg[0:n, c, 0:N], scalar=vec[0:n, 2 + c:3 + c], in1=hg[0:n, c, N:],
                                                     op0=ALU.add, op1=ALU.mult).then_inc(S["f_h"], 1)
                    if g == 3 and live(i - 1):
                        f = i - 1
                        dve.wait_ge(S["f_mean"], f + 1)
                        dve.wait_ge(S["f_xs2"], f + 1)
                        dve.tensor_tensor(xc[:, :], xs2[:, :], PS[:, 7, 0:N], ALU.subtract).then_inc(S["f_xc"], 1)
                    if g == 3 and live(i) and (not isinstance(i, int) or i + 1 < ITERS):
                        trail_state(i + 1)

            sweep(dve, body)
            for q in range(4):
                dve.wait_ge(S["o_t"], q + 1)
                rows = x_tok[:, 4 * q * D:4 * (q + 1) * D]
                dve.tensor_tensor(rows, rows, PS[:, q, :], ALU.add).then_inc(S["o_add"], 1)

        @block.tensor
        def _(pe):
            pe.wait_ge(S["ld_const"], 16 * 5)
            pe.wait_ge(S["temp_set"], 5)
            pe.matmul(PS[:, 7, 0:1], spread[:, :], temp[:, 5:6], start=True, stop=True).then_inc(S["spread_mm"], 1)
            pe.wait_ge(S["ln_step"], 10)
            for q in range(4):
                for a in range(4):
                    c = (4 * q + a) * D
                    last = pe.transpose(PS[:, q, a * P:(a + 1) * P], xc_tok[:, c:c + D], ident[:, :])
                last.then_inc(S["xn_t"], 1)
            misc = PS[:, 7, 0:N]

            def g_keys(b):
                pe.matmul(misc, wg[:, D:2 * D], state(slice(0, P), b, 0), start=True, stop=True).then_inc(S["g_k_mm"], 1)

            pe.wait_ge(S["state_set"], B)
            pe.wait_ge(S["ld_gw"], 16 * 7)
            pe.wait_ge(S["qscale_set"], 1)
            g_keys(0)

            def g_body(b, more=True):
                for c in range(GU):
                    if glive(b) and c == 0:
                        wait(pe, "g_k", b + 1)
                        pe.matmul(misc, wg[:, 0:D], state(slice(0, P), b, 0), start=True, stop=True).then_inc(S["g_q_mm"], 1)
                        pe.wait_ge(S["g_q"], b + 1)
                        pe.wait_ge(S["g_kz"], b + 1)
                        pe.wait_ge(S["voidk_set"], 1)
                    if glive(b):
                        wait(pe, "g_sub", gdone(b, c, 2))
                        for e in range(2):
                            h = c // 2 * 2 + e
                            keys = gkz[:, bass.ds((b & 1) * (GH * NK) + h * NK, NK)]
                            t = c % 2
                            last = pe.matmul(PS[:, 2 * (c % 2) + e, 0:NK], gq[:, t * P:(t + 1) * P], keys, start=True, stop=True)
                        last.then_inc(S["g_s"], 1)
                    if glive(b) and c == 1:
                        pe.wait_ge(S["g_x"], b + 1)
                        for t in range(TT):
                            last = pe.matmul(PS[:, 7, t * P:(t + 1) * P], xg[:, t * P:(t + 1) * P], wg[:, 2 * D:3 * D], start=True, stop=True)
                        last.then_inc(S["g_v_mm"], 1)
                    j, cj = gunit(b, c, 2)
                    if glive(j):
                        pe.wait_ge(S["g_exp"], gdone(b, c, 2))
                        wait(pe, "g_pT", gdone(b, c, 3))
                        for e in range(2):
                            for kt in range(TT):
                                n = 2 * e + kt
                                last = pe.transpose(PS[:, 4, n * P:(n + 1) * P], gp[:, cj % 4, e, kt * P:(kt + 1) * P], ident[:, :])
                        last.then_inc(S["g_pt"], 1)
                    j, cj = gunit(b, c, 3)
                    if glive(j):
                        n, pair, t = cj // 4, cj // 2 % 2, cj % 2
                        pe.wait_ge(S["g_pT"], gdone(b, c, 3))
                        if cj == 0:
                            pe.wait_ge(S["g_v"], j + 1)
                        if cj % 4 == 0:
                            wait(pe, "g_oT", 4 * j + n)
                        for kt in range(TT):
                            for e in range(2):
                                h = cj // 2 * 2 + e
                                r = 32 * (2 * pair + e)
                                last = pe.matmul(PS[r:r + 32, 5, t * P:(t + 1) * P], gv[:, kt, h, :],
                                                 gpT[:, cj % 2, (2 * e + kt) * P:(2 * e + kt + 1) * P],
                                                 start=(kt == 0), stop=(kt == 1), skip_group_check=True)
                        last.then_inc(S["g_o"], 1)
                    j, cj = gunit(b, c, 5)
                    if glive(j) and cj % 4 == 3:
                        n = cj // 4
                        pe.wait_ge(S["g_oT"], 4 * j + n + 1)
                        wait(pe, "g_tokev", 4 * j + n)
                        for t in range(TT):
                            last = pe.transpose(PS[:, 6, t * P:(t + 1) * P], goT[:, n % 2, t * P:(t + 1) * P], ident[:, :])
                        last.then_inc(S["g_tok"], 1)
                    if c == 6 and glive(b - 1):
                        pe.wait_ge(S["g_att"], b)
                        if glive(b):
                            pe.wait_ge(S["g_v"], b + 1)
                        for t in range(TT):
                            last = pe.transpose(PS[:, 7, t * P:(t + 1) * P], gatt[:, t, :], ident[:, :])
                        last.then_inc(S["g_attT_mm"], 1)
                    if c == 7 and glive(b - 1):
                        pe.wait_ge(S["g_attT"], b)
                        for t in range(TT):
                            last = pe.matmul(PS[:, 7, t * P:(t + 1) * P], gattT[:, t * P:(t + 1) * P], wgo[:, :], start=True, stop=True)
                        last.then_inc(S["g_y"], 1)
                    if c == 9 and glive(b) and more:
                        wait(pe, "g_res", b)
                        pe.wait_ge(S["g_v"], b + 1)
                        g_keys(b + 1)

            g_body(0)
            g_body(1)
            with pe.Fori(2, B - 1) as b:
                g_body(b)
            g_body(B - 1, more=False)
            g_body(B)

            pe.wait_ge(S["mask_set"], 1)

            def body(i):
                for g in range(NG):
                    if live(i):
                        if g == 0:
                            pe.wait_ge(S["xl_set"], i + 1)
                            pe.wait_ge(S["split_lo"], 1 + (i >> 3) * B)
                        if isinstance(i, int) and i == 0 and g == 0:
                            pe.wait_ge(S["g_res"], B)
                            pe.wait_ge(S["g_void"], GU * B)
                        u = (i >> 3) & 1
                        parts = ((xh, wh), (xh, wl), (xl, wh))
                        wait(pe, "t2_set", done(i, g, 1))
                        for t in range(TT):
                            for n, (x, w) in enumerate(parts):
                                last = pe.matmul(PS[:, t, :], x[:, t * P:(t + 1) * P], w[:, bass.ds(u, 1), 0:2, g * GC:(g + 1) * GC].squeeze(1),
                                                 start=(n == 0), stop=(n == 2))
                        last.then_inc(S["s_qk"], 1)
                        wait(pe, "v_set", done(i, g, 1))
                        wait(pe, "o_set", done(i, g, 3))
                        for t in range(TT):
                            for n, (x, w) in enumerate(parts):
                                last = pe.matmul(PS[:, 2, t * GC:(t + 1) * GC], x[:, t * P:(t + 1) * P], w[:, bass.ds(u, 1), 2, g * GC:(g + 1) * GC].squeeze(1),
                                                 start=(n == 0), stop=(n == 2))
                        last.then_inc(S["s_v"], 1)
                    j, gj = unit(i, g, 1)
                    if live(j):
                        k = gj % 2
                        pe.wait_ge(S["qn_set"], done(i, g, 1))
                        for q, (free, mm) in enumerate((("qT_set", "tq_mm"), ("kz_set", "tk_mm"))):
                            wait(pe, free, done(i, g, 2))
                            for a in range(PR):
                                for t in range(TT):
                                    c = (t * 2 + q) * GC + a * P
                                    last = pe.transpose(PS[:, 3 + q, a * N + t * P:a * N + (t + 1) * P], qn[:, k, c:c + P], ident[:, :])
                            last.then_inc(S[mm], 1)
                    if g == 0 and live(i - 2):
                        hidden(i - 2, 0)
                    if g == 1 and live(i - 2):
                        hidden(i - 2, 2)
                    if g == 3 and live(i - 1):
                        f = i - 1
                        pe.wait_ge(S["f_xs2"], f + 1)
                        pe.wait_ge(S["state_set"], B + f)
                        pe.matmul(PS[:, 7, 0:N], mean_mat[:, :], xs2[:, :], start=True, stop=True).then_inc(S["f_mean"], 1)
                    j, gj = unit(i, g, 2)
                    if live(j):
                        k = gj % 2
                        pe.wait_ge(S["pn_set"], done(i, g, 2))
                        wait(pe, "pT_set", done(i, g, 3))
                        for h in range(HG):
                            last = pe.transpose(PS[:, 6, h * P:(h + 1) * P], pr[:, k, h].rearrange("p t k -> p (t k)"), ident[:, :])
                        last.then_inc(S["pt_mm"], 1)
                    j, gj = unit(i, g, 1)
                    if live(j):
                        k = gj % 2
                        pe.wait_ge(S["qT_set"], done(i, g, 1))
                        pe.wait_ge(S["kz_set"], done(i, g, 1))
                        wait(pe, "sub_set", done(i, g, 2))
                        scores = PS[:, 5, :].rearrange("p (h t k) -> p h t k", h=HG, t=TT)
                        pe.matmul(PS[:, 5, :], ident_bf[:, :], mask_bf[:, :], start=True, stop=False, skip_group_check=True)
                        for t in range(TT):
                            for a in range(PR):
                                for w in range(NW):
                                    q0, k0 = t * P + w * WIN, (t * NW + w) * WIN
                                    last = pe.matmul(scores[w * WIN:(w + 1) * WIN, 2 * a:2 * a + 2, t, :], qT[:, k, a, q0:q0 + WIN],
                                                     kz[:, k, a, :, k0:k0 + 2 * WIN], start=False, stop=True, skip_group_check=True)
                        last.then_inc(S["s_mm"], 1)
                    j, gj = unit(i, g, 2)
                    if live(j):
                        pe.wait_ge(S["pT_set"], done(i, g, 2))
                        if live(i):
                            pe.wait_ge(S["v_set"], done(i, g))
                        wait(pe, "o_set", done(i, g, 3))
                        for a in range(PR):
                            for t, q0, probs in ((0, 0, pT0), (1, P, pT1)):
                                for e in range(2):
                                    h = 2 * a + e
                                    n = probs.shape[2]
                                    last = pe.matmul(PS[e * DH:(e + 1) * DH, 2, a * N + q0:a * N + q0 + n],
                                                     v[:, gj, t, h * DH:(h + 1) * DH], probs[:, h, :],
                                                     start=(t == 0), stop=(t == 1), skip_group_check=True)
                        last.then_inc(S["o_mm"], 1)
                    if g == 0 and live(i - 2):
                        hidden(i - 2, 1)
                    if g == 2 and live(i - 2):
                        f = i - 2
                        pe.wait_ge(S["f_h"], 3 * (f + 1))
                        pe.wait_ge(S["ld_w2"], 32 * ((f >> 3) + 1))
                        for c, (_, n) in enumerate(FCH):
                            last = pe.matmul(PS[:, 7, 0:N], w2[0:n, c, :], hT[0:n, c, :], start=(c == 0), stop=(c == 2))
                        last.then_inc(S["f_y2"], 1)
                    if g == 2 and live(i - 1):
                        f = i - 1
                        pe.wait_ge(S["o_set"], 4 * (f + 1))
                        pe.wait_ge(S["ld_wo"], 16 * ((f >> 3) + 1))
                        wait(pe, "f_hgc", 3 * f)
                        for c in range(INNER // P):
                            last = pe.matmul(PS[:, 7, N:2 * N], wo[:, c, :], oT[:, c, :], start=(c == 0), stop=(c == INNER // P - 1))
                        last.then_inc(S["f_y"], 1)
                    if g == 3 and live(i - 1):
                        f = i - 1
                        pe.wait_ge(S["f_sq"], f + 1)
                        pe.matmul(PS[:, 7, N:2 * N], mean_mat[:, :], xc2[:, :], start=True, stop=True).then_inc(S["f_var"], 1)

            def hidden(f, c):
                c0, n = FCH[c]
                pe.wait_ge(S["f_xn"], f + 1)
                pe.wait_ge(S["ld_w1"], 16 * ((f >> 3) + 1))
                wait(pe, "f_hgc", 3 * f + c)
                for half in range(2):
                    w0 = half * FI + c0
                    last = pe.matmul(PS[0:n, 7, half * N:(half + 1) * N], w1[:, w0:w0 + n], xn[:, :], start=True, stop=True)
                last.then_inc(S["f_hg"], 1)

            sweep(pe, body)
            pe.wait_ge(S["state_set"], B + ITERS)
            for q in range(4):
                for a in range(4):
                    b, t = (4 * q + a) // TT, a % TT
                    c = b * (N + 1) + 1 + t * P
                    last = pe.transpose(PS[:, q, a * P:(a + 1) * P], xT[:, c:c + P], ident[:, :])
                last.then_inc(S["o_t"], 1)


_INS = ["L0_attn_x", "L0_attn_w_qkv", "L0_attn_w_out", "L0_attn_b_out", "L0_attn_void_q", "L0_attn_void_k",
        "L0_attn_void_v", "L0_attn_attention_trace", "L0_attn_temperature_factor", "L0_ffn_Wqkv", "L0_ffn_q_scale",
        "L0_ffn_k_scale", "L0_ffn_Wo", "L0_ffn_ln_g", "L0_ffn_ln_b", "L0_ffn_W1", "L0_ffn_b1", "L0_ffn_W2", "L0_ffn_b2"]


def kernel(**inputs):
    import concourse.bacc as _bacc
    from concourse.bass_utils import run_bass_kernel_spmd as _run

    nc = _bacc.Bacc("TRN2", target_bir_lowering=False, num_devices=1)
    given = {name: np.ascontiguousarray(inputs[name]) for name in _INS if name != "L0_attn_void_q"}
    given.update(shape_constants())
    arrays, aps = {}, {}
    for name, a in given.items():
        arrays[f"in_{name}"] = a
        aps[name] = nc.dram_tensor(f"in_{name}", a.shape, mybir.dt.from_np(a.dtype), kind="ExternalInput").ap()
    result = nc.dram_tensor("result", (B, N, D), F32, kind="ExternalOutput").ap()
    bass_dual_attention(nc, aps, result)
    r = _run(nc, [arrays], core_ids=[0])
    return r.results[0]["result"]
```

```python
from contextlib import ExitStack

import numpy as np
import concourse.bass as bass
from concourse import mybir

F32 = mybir.dt.float32
F32R = mybir.dt.float32r
BF16 = mybir.dt.bfloat16
ALU = mybir.AluOpType
ACT = mybir.ActivationFunctionType
AX_X = mybir.AxisListType.X

P = 128
B, N, D = 8, 256, 128
TT = N // P
TILES = B * TT
GH, GD = 16, 8
NK = N + 1
GU = TT * GH // 2
DEPTH, H, DH, WIN = 6, 16, 64, 32
INNER = H * DH
NG = 4
HG = H // NG
GC = HG * DH
PR = HG // 2
NW = P // WIN
ITERS = DEPTH * B
FI = int(D * 4 * 2 / 3)
FCH = [(0, 128), (128, 128), (256, FI - 256)]
QKV = 3 * INNER
PIECE = QKV // B
LN_EXP = "natural_log_exp_and_others"
NORM_G = 2.0 ** 10
NVEC = 9


def shape_constants():
    half = np.arange(0, DH, 2, dtype=np.float32)
    inv_freq = (1.0 / 10000.0 ** (half / DH)).astype(np.float32)
    t = np.arange(N, dtype=np.float32)
    freqs = t[:, None] * inv_freq[None, :]
    freqs = np.concatenate([freqs, freqs], -1).astype(np.float64)
    base = (half.astype(np.float64) + 0.4 * DH) / (1.4 * DH)
    power = (t.astype(np.float64) - N // 2) / (WIN // 2)
    scale = base[None, :] ** power[:, None]
    scale = np.concatenate([scale, scale], -1)
    sign = np.where(np.arange(DH) < DH // 2, -1.0, 1.0)
    cos, sin = np.cos(freqs), np.sin(freqs) * sign
    q_gain = 8.0
    rot = np.zeros((P, 2, TT, 2, DH))
    for k, trig in enumerate((cos, sin)):
        for tt in range(TT):
            rows = slice(tt * P, (tt + 1) * P)
            rot[:, k, tt, 0] = trig[rows] * scale[rows] * q_gain * NORM_G
            rot[:, k, tt, 1] = trig[rows] / scale[rows] * NORM_G
    mask = np.zeros((P, HG, TT, 2 * WIN))
    qi = (np.arange(P) % WIN)[:, None]
    w = (np.arange(P) // WIN)[:, None]
    j = np.arange(2 * WIN)[None, :]
    for tt in range(TT):
        bad = (j - WIN > qi) | (qi > j) | ((w + tt * NW == 0) & (j < WIN))
        mask[:, :, tt] = np.where(bad, -1e30, 0.0)[:, None, :]
    head_of = np.arange(P)[:, None] // GD == np.arange(GH)[None, :]
    return {
        "c_ident": np.eye(P, dtype=np.float32),
        "c_rot": rot.reshape(P, -1).astype(np.float32),
        "c_mask": mask.reshape(P, -1).astype(np.float32),
        "c_head": head_of.astype(np.float32),
        "c_spread": np.ascontiguousarray(head_of.T).astype(np.float32),
    }


def bass_dual_attention(nc: bass.Bass, A: dict, out: bass.AP):
    with ExitStack() as ctx:
        def sb(name, shape, dt=F32):
            return ctx.enter_context(nc.sbuf_tensor(name, shape, dt))

        PS = ctx.enter_context(nc.psum_tensor("PS", [P, 8, 512], F32))

        ident = sb("ident", [P, P])
        ident_bf = sb("ident_bf", [P, P], BF16)
        mask_bf = sb("mask_bf", [P, 512], BF16)
        head_col = sb("head_col", [P, GH])
        spread = sb("spread", [GH, P])
        mean_mat = sb("mean_mat", [P, P])
        rot = sb("rot", [P, DEPTH * 2 * TT * 2 * DH])
        vec_all = sb("vec_all", [P, DEPTH * NVEC])
        vec = sb("vec", [P, NVEC])
        x_tok = sb("x_tok", [P, TILES * D])
        xT = sb("xT", [P, B * (N + 1)])
        stat = sb("stat", [P, 4, TILES])
        temp = sb("temp", [GH, 6])
        qscale = sb("qscale", [P, 1])
        voidk = sb("voidk", [P, 1])
        voidv = sb("voidv", [P, GH, GD + 1])
        shared = sb("shared", [P, 4, N])
        gq, gk, xg, gattT = (shared[:, k, :] for k in range(4))
        gmx = sb("gmx", [P, 2, 2])
        gpv = sb("gpv", [P, 2 * TT * GH])
        gden = sb("gden", [P, TT * GH])
        gatt = sb("gatt", [P, TT, D])
        w_raw = sb("w_raw", [P, 2 * QKV])
        wh = sb("wh", [P, 2, 3, INNER], F32R)
        wl = sb("wl", [P, 2, 3, INNER], F32R)
        xh = sb("xh", [P, N], F32R)
        xl = sb("xl", [P, N], F32R)
        rmx = sb("rmx", [P, 2, TT * HG])
        rsum = sb("rsum", [P, 2, TT * HG])
        rinv = sb("rinv", [P, 2, TT * HG])
        ss = sb("ss", [P, 16])
        ssm = sb("ssm", [P, 2, 16])
        ssl = sb("ssl", [P, 2, 16])
        guess = sb("guess", [P, 2, 16])
        one_half = sb("one_half", [P, 16])
        newton = sb("newton", [P, 3, 16])
        rn = sb("rn", [P, 2, 16])
        wo = sb("wo", [P, INNER // P, D])
        w1 = sb("w1", [P, 2 * FI])
        w2 = sb("w2", [P, 3, D])
        x1 = shared[:, 0:2, :]
        xc, xc2 = shared[:, 2, :], shared[:, 3, :]
        xs2 = sb("xs2", [P, N])
        var = sb("var", [P, N])
        rs = sb("rs", [P, N])
        xn = sb("xn", [P, N])
        hT = sb("hT", [P, 3, N])

        arena = sb("arena", [P, 19328])
        taken = [0]

        def part(n):
            taken[0] += n
            return arena[:, taken[0] - n:taken[0]]

        gkz = part(2 * GH * NK)
        sq_tok = arena[:, taken[0]:taken[0] + TILES * D]
        gp = part(4 * 2 * NK).rearrange("p (u e k) -> p u e k", u=4, e=2)
        gpT = part(2 * 512).rearrange("p (u n) -> p u n", u=2)
        goT = part(2 * N).rearrange("p (u n) -> p u n", u=2)
        gtok = part(TT * GH * (GD + 1)).rearrange("p (h d) -> p h d", d=GD + 1)
        gacc = part(TT * GH * (GD + 1)).rearrange("p (h d) -> p h d", d=GD + 1)
        xc_tok = part(TILES * D)
        mask_f = part(512)
        rot_base = part(2 * TT * 2 * DH).rearrange("p (k t n) -> p k t n", k=2, t=TT)
        gains = part(DEPTH * 2 * DH).rearrange("p (l n) -> p l n", l=DEPTH)
        gains_sw = part(DEPTH * 2 * DH).rearrange("p (l n) -> p l n", l=DEPTH)
        wg, wgo, bo = part(3 * D), part(D), part(D)
        gv = part(TT * GH * 32).rearrange("p (t h d) -> p t h d", t=TT, h=GH)
        taken[0] = 0
        sq = part(1024)
        t1 = part(2048).rearrange("p (u n) -> p u n", u=2)
        t2 = part(1024)
        qn = part(2048).rearrange("p (u n) -> p u n", u=2)
        qT = part(1024).rearrange("p (u a n) -> p u a n", u=2, a=PR)
        kz = part(4 * PR * (N + WIN)).rearrange("p (u a e n) -> p u a e n", u=2, a=PR, e=2)
        v = part(2048).rearrange("p (g t n) -> p g t n", g=NG, t=TT)
        pr = part(1024).rearrange("p (u h t k) -> p u h t k", u=2, t=TT, h=HG)
        pT0 = part(HG * (P + WIN)).rearrange("p (h n) -> p h n", h=HG)
        pT1 = part(HG * P).rearrange("p (h n) -> p h n", h=HG)
        oT = part(4096).rearrange("p (u c n) -> p u c n", u=2, c=2 * NG)
        hg = part(3 * 512).rearrange("p (c n) -> p c n", c=3)

        wh_flat = wh[:, :, :, :].rearrange("p u a n -> p (u a n)")
        wl_flat = wl[:, :, :, :].rearrange("p u a n -> p (u a n)")

        names = """ld_x ld_const ld_gw ld_vec ld_raw ld_wo ld_w1 ld_w2 st_out
        vec_clear zeroed cleared ones_set mask_set temp_set spread_mm qscale_set voidk_set ln_step ln_guess ln_sq xn_t state_set rot_set
        g_k_mm g_k g_kz g_q_mm g_q g_x g_v_mm g_v g_s g_mx g_sub g_exp g_void g_pt g_pT g_o g_oT g_tok g_tokev g_num g_acc
        g_den g_att g_attT_mm g_attT g_y g_res
        split_hi split_lo xh_set xl_set s_qk s_v sq_set v_set ss_set ssm_set ssl_set guess_set nw1_set nw2_set nw3_set rn_set t1_set t2_set add_set qn_set
        tq_mm tk_mm qT_set kz_set s_mm mx_set sub_set exp_set sum_set inv_set pn_set pt_mm pT_set o_mm o_set
        f_y f_x1 f_xs2 f_mean f_xc f_sq f_var f_ve f_ln f_guess f_n1 f_n2 f_rs f_xr f_xn f_vec f_hg f_hgc f_gate f_h f_y2
        o_t o_add""".split()
        S = {n: ctx.enter_context(nc.semaphore(n)) for n in names}
        block = ctx.enter_context(nc.Block())

        def unit(i, g, back=0):
            return i + (g - back) // NG, (g - back) % NG

        def done(i, g, back=0):
            return i * NG + (g - back + 1)

        def live(i):
            return not isinstance(i, int) or 0 <= i < ITERS

        def layer_of(i):
            if isinstance(i, int):
                return i // B
            return nc.s_assert_within(i >> 3, 0, DEPTH - 1, skip_runtime_bounds_check_because="iterations end before ITERS")

        def wait(eng, name, value):
            if not isinstance(value, int) or value > 0:
                eng.wait_ge(S[name], value)

        def sweep(eng, body):
            for i in range(4):
                body(i)
            with eng.Fori(4, ITERS) as i:
                body(i)
            for i in range(ITERS, ITERS + 3):
                body(i)

        def gunit(b, c, back=0):
            return b + (c - back) // GU, (c - back) % GU

        def gdone(b, c, back=0):
            return b * GU + (c - back + 1)

        def glive(b):
            return not isinstance(b, int) or 0 <= b < B

        def gsweep(eng, body):
            body(0)
            body(1)
            with eng.Fori(2, B) as b:
                body(b)
            body(B)

        def state(rows, b, shift):
            return xT[rows, bass.ds(b * (N + 1) + 1 - shift, N)]

        lower, upper = slice(0, D // 2), slice(D // 2, D)

        @block.sync
        def _(sp):
            x_t = A["L0_attn_x"].rearrange("b (t p) d -> p (b t) d", p=P)
            xt3 = x_tok[:, :].rearrange("p (a d) -> p a d", d=D)
            sp.dma_start(xt3[:, :, :], x_t[:, :, :]).then_inc(S["ld_x"], 16)
            sp.dma_start(ident[:, :], A["c_ident"]).then_inc(S["ld_const"], 16)
            sp.dma_start(head_col[:, :], A["c_head"]).then_inc(S["ld_const"], 16)
            sp.dma_start(spread[:, :], A["c_spread"]).then_inc(S["ld_const"], 16)
            sp.dma_start(rot_base.rearrange("p a b c -> p (a b c)"), A["c_rot"]).then_inc(S["ld_const"], 16)
            sp.dma_start(mask_f, A["c_mask"]).then_inc(S["ld_const"], 16)
            sp.dma_start(wg, A["L0_attn_w_qkv"]).then_inc(S["ld_gw"], 16)
            sp.dma_start(wgo, A["L0_attn_w_out"]).then_inc(S["ld_gw"], 16)
            sp.dma_start(temp[:, 0:1], A["L0_attn_attention_trace"].rearrange("h a b -> h (a b)")).then_inc(S["ld_gw"], 16)
            sp.dma_start(temp[:, 1:2], A["L0_attn_temperature_factor"].rearrange("h a b -> h (a b)")).then_inc(S["ld_gw"], 16)
            sp.dma_start(voidk[:, :], A["L0_attn_void_k"].rearrange("a h b d -> (a h b d)").rearrange("(p o) -> p o", o=1)).then_inc(S["ld_gw"], 16)
            vv_src = A["L0_attn_void_v"].rearrange("a h b d -> (a b) h d")
            sp.dma_start(voidv[:, :, 0:GD], vv_src.to_broadcast([P, GH, GD])).then_inc(S["ld_gw"], 16)
            sp.dma_start(bo, A["L0_attn_b_out"].rearrange("(a d) -> a d", a=1).to_broadcast([P, D])).then_inc(S["ld_gw"], 16)
            sp.dma_start(w_raw[:, 0:QKV], A["L0_ffn_Wqkv"][0]).then_inc(S["ld_raw"], 16)
            hd = DH // 2
            for k, name in enumerate(("L0_ffn_q_scale", "L0_ffn_k_scale")):
                a = A[name].rearrange("(o l) d -> o l d", o=1)
                c = k * DH
                sp.dma_start(gains[:, :, c:c + DH], a.to_broadcast([P, DEPTH, DH])).then_inc(S["ld_vec"], 16)
                sp.dma_start(gains_sw[:, :, c:c + hd], a[:, :, hd:DH].to_broadcast([P, DEPTH, hd])).then_inc(S["ld_vec"], 16)
                sp.dma_start(gains_sw[:, :, c + hd:c + DH], a[:, :, 0:hd].to_broadcast([P, DEPTH, hd])).then_inc(S["ld_vec"], 16)
            vv = vec_all[:, :].rearrange("p (l v) -> p l v", v=NVEC)
            sp.wait_ge(S["vec_clear"], 1)
            with nc.allow_non_contiguous_dma(reason="small vectors"):
                def column(n, k, src):
                    sp.dma_start(vv[0:n, :, k:k + 1], src.rearrange("l (p o) -> p l o", o=1)).then_inc(S["ld_vec"], 16)

                column(P, 0, A["L0_ffn_ln_g"])
                column(P, 1, A["L0_ffn_ln_b"])
                for c, (c0, cn) in enumerate(FCH):
                    for half in range(2):
                        column(cn, 2 + 3 * half + c, A["L0_ffn_b1"][:, half * FI + c0:half * FI + c0 + cn])
                column(P, 8, A["L0_ffn_b2"])

            def load_wo(l):
                sp.dma_start(wo[:, :, :], A["L0_ffn_Wo"][l].rearrange("(c p) n -> p c n", p=P)).then_inc(S["ld_wo"], 16)

            def load_w1(l):
                sp.dma_start(w1[:, :], A["L0_ffn_W1"][l]).then_inc(S["ld_w1"], 16)

            def load_w2(l):
                sp.dma_start(w2[:, 0:2, :], A["L0_ffn_W2"][l][0:2 * P, :].rearrange("(c p) n -> p c n", p=P)).then_inc(S["ld_w2"], 16)
                sp.dma_start(w2[0:FCH[2][1], 2, :], A["L0_ffn_W2"][l][2 * P:FI, :]).then_inc(S["ld_w2"], 16)

            load_wo(0)
            load_w1(0)
            load_w2(0)
            sp.wait_ge(S["ld_raw"], 16)
            sp.dma_start(w_raw[:, QKV:2 * QKV], A["L0_ffn_Wqkv"][1]).then_inc(S["ld_raw"], 16)
            for l in range(1, DEPTH):
                c = (l + 1) % 2 * QKV
                sp.wait_ge(S["ld_raw"], 16 * (l + 1))
                sp.wait_ge(S["split_lo"], 1 + B * (l - 1))
                sp.dma_start(w_raw[:, c:c + QKV], A["L0_ffn_Wqkv"][(l + 1) % DEPTH]).then_inc(S["ld_raw"], 16)
                sp.wait_ge(S["f_y"], B * l)
                load_wo(l)
                sp.wait_ge(S["f_hg"], 3 * B * l)
                load_w1(l)
                sp.wait_ge(S["f_y2"], B * l)
                load_w2(l)
            o_t = out.rearrange("b (t p) d -> p (b t) d", p=P)
            for q in range(4):
                sp.wait_ge(S["o_add"], q + 1)
                sp.dma_start(o_t[:, 4 * q:4 * q + 4, :], xt3[:, 4 * q:4 * q + 4, :]).then_inc(S["st_out"], 16)
            sp.wait_ge(S["st_out"], 64)

        @block.gpsimd
        def _(pool):
            pool.memset(vec_all[:, :], 0.0).then_inc(S["vec_clear"], 1)
            pool.memset(mean_mat[:, :], 1.0 / D)
            pool.memset(one_half[:, :], 1.5)
            pool.memset(xT[:, :], 0.0)
            pool.memset(xs2[:, :], 0.0)
            pool.memset(gv[:, :, :, :], 0.0).then_inc(S["zeroed"], 1)
            pool.wait_ge(S["zeroed"], 1)
            pool.memset(gv[:, :, :, GD:GD + 1], 1.0)
            pool.memset(voidv[:, :, GD:GD + 1], 1.0).then_inc(S["ones_set"], 1)
            pool.wait_ge(S["ld_const"], 16 * 5)
            pool.wait_ge(S["ld_gw"], 16 * 7)
            gkz3 = gkz.rearrange("p (u k) -> p u k", k=NK)
            for u in range(2):
                last = pool.tensor_tensor(gkz3[:, u * GH:(u + 1) * GH, N], head_col[:, :],
                                          voidk[:, 0:1].to_broadcast([P, GH]), ALU.mult)
            last.then_inc(S["voidk_set"], 1)

            def spread_keys(b, h0):
                if h0 == 0:
                    pool.wait_ge(S["g_k"], b + 1)
                    wait(pool, "g_s", (b - 1) * GU)
                u = b & 1
                dst = gkz[:, bass.ds(u * (GH * NK) + h0 * NK, 4 * NK)].rearrange("p (h k) -> p h k", h=4)
                pool.tensor_tensor(
                    dst[:, :, 0:N], gk.unsqueeze(1).to_broadcast([P, 4, N]),
                    head_col[:, h0:h0 + 4].unsqueeze(2).to_broadcast([P, 4, N]), ALU.mult).then_inc(S["g_kz"], 1)

            for h0 in range(0, GH, 4):
                spread_keys(0, h0)

            def g_body(b, more=True):
                for c in range(GU):
                    j, cj = gunit(b, c, 1)
                    if glive(j):
                        pool.wait_ge(S["g_exp"], gdone(b, c, 1))
                        h0, t = cj // 2 * 2, cj % 2
                        wait(pool, "g_num", j - 1)
                        pool.tensor_copy(gpv[:, bass.ds((j & 1) * (TT * GH) + t * GH + h0, 2)], gp[:, cj % 4, :, N]).then_inc(S["g_void"], 1)
                    if 6 <= c < 10 and glive(b) and more:
                        spread_keys(b + 1, 4 * (c - 6))

            g_body(0)
            g_body(1)
            with pool.Fori(2, B - 1) as b:
                g_body(b)
            g_body(B - 1, more=False)
            g_body(B)

            pool.wait_ge(S["ld_vec"], 16 * 15)
            rot3 = rot[:, :].rearrange("p (l k t n) -> p l k t n", l=DEPTH, k=2, t=TT)
            for l in range(DEPTH):
                for k, gain in enumerate((gains, gains_sw)):
                    last = pool.tensor_tensor(rot3[:, l, k], rot_base[:, k, :, :],
                                              gain[:, l, :].unsqueeze(1).to_broadcast([P, TT, 2 * DH]), ALU.mult)
            last.then_inc(S["rot_set"], 1)
            pool.wait_ge(S["g_res"], B)
            pool.wait_ge(S["g_void"], GU * B)
            pool.memset(kz[:, :, :, :, :], 0.0)
            pool.memset(pT0[:, :, :], 0.0)
            pool.memset(pT1[:, :, :], 0.0).then_inc(S["cleared"], 1)

            def body(i):
                for g in range(NG):
                    j, gj = unit(i, g, 2)
                    if live(j):
                        k = gj % 2
                        p2 = pr[:, k].rearrange("p h t k -> p (h t) k")
                        pool.wait_ge(S["inv_set"], done(i, g, 2))
                        pool.tensor_tensor(p2, p2, rinv[:, k, :].unsqueeze(2).to_broadcast([P, TT * HG, 2 * WIN]),
                                           ALU.mult).then_inc(S["pn_set"], 1)
                    if g == 3 and live(i - 2):
                        f = i - 2
                        for c, (_, n) in enumerate(FCH):
                            pool.wait_ge(S["f_gate"], 3 * f + c + 1)
                            wait(pool, "f_y2", f)
                            pool.tensor_tensor(hT[0:n, c, :], hg[0:n, c, 0:N], hg[0:n, c, N:], ALU.mult).then_inc(S["f_h"], 1)
                    if live(i):
                        k = g % 2
                        pool.wait_ge(S["t2_set"], done(i, g))
                        pool.tensor_tensor(t1[:, k, :], t1[:, k, :], t2, ALU.add).then_inc(S["add_set"], 1)
                        pool.wait_ge(S["ssm_set"], done(i, g))
                        pool.wait_ge(S["guess_set"], done(i, g))
                        pool.tensor_tensor(newton[:, 0, :], guess[:, k, :], guess[:, k, :], ALU.mult).then_inc(S["nw1_set"], 1)
                        pool.wait_ge(S["nw1_set"], done(i, g))
                        pool.tensor_tensor(newton[:, 1, :], newton[:, 0, :], ssm[:, k, :], ALU.mult).then_inc(S["nw2_set"], 1)
                        pool.wait_ge(S["nw2_set"], done(i, g))
                        pool.tensor_tensor(newton[:, 2, :], newton[:, 1, :], one_half[:, :], ALU.add).then_inc(S["nw3_set"], 1)
                        pool.wait_ge(S["nw3_set"], done(i, g))
                        pool.tensor_tensor(rn[:, k, :], newton[:, 2, :], guess[:, k, :], ALU.mult).then_inc(S["rn_set"], 1)
                        pool.wait_ge(S["add_set"], done(i, g))
                        pool.wait_ge(S["rn_set"], done(i, g))
                        wait(pool, "tk_mm", done(i, g, 2))
                        for q in range(2):
                            dst, src = (a[:, k, :].rearrange("p (t u n) -> p t u n", t=TT, u=2)[:, :, q].rearrange("p t (h d) -> p t h d", d=DH)
                                        for a in (qn, t1))
                            norm = rn[:, k, :].rearrange("p (t u h) -> p t u h", t=TT, u=2)[:, :, q].unsqueeze(3)
                            pool.tensor_tensor(dst, src, norm.to_broadcast([P, TT, HG, DH]), ALU.mult).then_inc(S["qn_set"], 1)
                    if g == 2 and live(i):
                        c0 = (((i >> 3) + 1) & 1) * QKV + (i & 7) * PIECE
                        pool.wait_ge(S["split_hi"], i + 2)
                        pool.tensor_tensor(wl_flat[:, bass.ds(c0, PIECE)], w_raw[:, bass.ds(c0, PIECE)],
                                           wh_flat[:, bass.ds(c0, PIECE)].bitcast(F32), ALU.subtract).then_inc(S["split_lo"], 1)

            sweep(pool, body)

        @block.scalar
        def _(act):
            act.preload_act_table_set(LN_EXP)
            act.wait_ge(S["ln_step"], 3)
            act.activation(sq_tok, xc_tok, ACT.Square).then_inc(S["ln_sq"], 1)
            act.wait_ge(S["ln_step"], 6)
            act.activation(stat[:, 1, :], stat[:, 3, :], ACT.Ln).then_inc(S["ln_guess"], 1)
            act.wait_ge(S["ln_guess"], 1)
            act.activation(stat[:, 0, :], stat[:, 1, :], ACT.Exp, scale=-0.5).then_inc(S["ln_guess"], 1)
            act.wait_ge(S["ld_raw"], 16)
            act.activation(wh_flat[:, 0:QKV], w_raw[:, 0:QKV], ACT.Copy).then_inc(S["split_hi"], 1)
            act.wait_ge(S["zeroed"], 1)
            xT3 = xT[:, :].rearrange("p (b n) -> p b n", b=B)
            for b in range(B):
                act.wait_ge(S["xn_t"], b // 2 + 1)
                act.activation(xT3[:, b, 1:], PS[:, b // 2, (b % 2) * N:(b % 2 + 1) * N], ACT.Copy).then_inc(S["state_set"], 1)

            def take_keys(b):
                act.wait_ge(S["g_k_mm"], b + 1)
                wait(act, "g_kz", 4 * b)
                act.activation(gk, PS[:, 7, 0:N], ACT.Copy).then_inc(S["g_k"], 1)

            take_keys(0)

            def g_body(b, more=True):
                for c in range(GU):
                    if glive(b) and c == 0:
                        act.wait_ge(S["g_q_mm"], b + 1)
                        act.wait_ge(S["qscale_set"], 1)
                        act.activation(gq, PS[:, 7, 0:N], ACT.Copy, scale=qscale[:, 0:1]).then_inc(S["g_q"], 1)
                        wait(act, "g_v_mm", b)
                        act.activation(xg, state(slice(0, P), b, 0), ACT.Copy).then_inc(S["g_x"], 1)
                    if glive(b) and c == 3:
                        act.wait_ge(S["g_v_mm"], b + 1)
                        wait(act, "g_o", b * GU)
                        if isinstance(b, int) and b == 0:
                            act.wait_ge(S["ones_set"], 1)
                        act.activation(gv[:, :, :, 0:GD], PS[:, 7, 0:N].rearrange("p (t h d) -> p t h d", t=TT, h=GH), ACT.Copy).then_inc(S["g_v"], 1)
                    j, cj = gunit(b, c, 1)
                    if glive(j):
                        act.wait_ge(S["g_sub"], gdone(b, c, 1))
                        act.activation(gp[:, cj % 4], gp[:, cj % 4], ACT.Exp).then_inc(S["g_exp"], 1)
                    j, cj = gunit(b, c, 2)
                    if glive(j):
                        act.wait_ge(S["g_pt"], gdone(b, c, 2))
                        wait(act, "g_o", gdone(b, c, 4))
                        act.activation(gpT[:, cj % 2], PS[:, 4, :], ACT.Copy).then_inc(S["g_pT"], 1)
                    j, cj = gunit(b, c, 3)
                    if glive(j) and cj % 4 == 3:
                        n = cj // 4
                        act.wait_ge(S["g_o"], gdone(b, c, 3))
                        wait(act, "g_tok", 4 * j + n - 1)
                        act.activation(goT[:, n % 2, :], PS[:, 5, 0:N], ACT.Copy).then_inc(S["g_oT"], 1)
                    if c == 10 and glive(b - 1):
                        act.wait_ge(S["g_attT_mm"], b)
                        act.activation(gattT, PS[:, 7, 0:N], ACT.Copy).then_inc(S["g_attT"], 1)
                    if c == 5 and glive(b) and more:
                        take_keys(b + 1)

            g_body(0)
            g_body(1)
            with act.Fori(2, B - 1) as b:
                g_body(b)
            g_body(B - 1, more=False)
            g_body(B)

            act.wait_ge(S["cleared"], 1)

            def body(i):
                for g in range(NG):
                    if live(i):
                        wait(act, "ss_set", done(i, g, 1))
                        for t in range(TT):
                            act.wait_ge(S["s_qk"], TT * (done(i, g) - 1) + t + 1)
                            act.activation(sq[:, t * 512:(t + 1) * 512], PS[:, t, :], ACT.Square).then_inc(S["sq_set"], 1)
                        act.wait_ge(S["s_v"], done(i, g))
                        wait(act, "o_mm", done(i, g, 4))
                        act.activation(v[:, g].rearrange("p t n -> p (t n)"), PS[:, 2, :], ACT.Copy).then_inc(S["v_set"], 1)
                    j, gj = unit(i, g, 1)
                    if live(j):
                        k = gj % 2
                        act.wait_ge(S["tq_mm"], done(i, g, 1))
                        wait(act, "s_mm", done(i, g, 3))
                        act.activation(qT[:, k].rearrange("p a n -> p (a n)"), PS[:, 3, :], ACT.Copy).then_inc(S["qT_set"], 1)
                        act.wait_ge(S["tk_mm"], done(i, g, 1))
                        kt = PS[:, 4, :].rearrange("p (a n) -> p a n", a=PR)
                        act.activation(kz[0:DH, k, :, 0, WIN:], kt[0:DH], ACT.Copy)
                        act.activation(kz[DH:P, k, :, 1, WIN:], kt[DH:P], ACT.Copy).then_inc(S["kz_set"], 1)
                    j, gj = unit(i, g, 2)
                    if live(j):
                        act.wait_ge(S["pt_mm"], done(i, g, 2))
                        wait(act, "o_mm", done(i, g, 3))
                        src = PS[:, 6, :].rearrange("p (h n) -> p h n", h=HG)
                        for t in range(TT):
                            dst = (pT0, pT1)[t]
                            for w in range(NW):
                                k0, s0, q0 = (w - 1) * WIN, t * 2 * WIN, w * WIN
                                if w == 0:
                                    moves = [(s0 + WIN, WIN, dst, 0, 0)] + [(s0, WIN, pT0, P - WIN, P)] * t
                                elif k0 % (2 * WIN) == 0:
                                    moves = [(s0, 2 * WIN, dst, k0, q0)]
                                else:
                                    moves = [(s0, WIN, dst, k0, q0), (s0 + WIN, WIN, dst, k0 + WIN, q0)]
                                for r, n, to, d0, c0 in moves:
                                    last = act.activation(to[d0:d0 + n, :, c0:c0 + WIN], src[r:r + n, :, q0:q0 + WIN], ACT.Copy)
                        last.then_inc(S["pT_set"], 1)
                    if g == 0 and live(i - 2):
                        act.wait_ge(S["f_ve"], i - 1)
                        act.activation(rs[:, :], var[:, :], ACT.Ln).then_inc(S["f_ln"], 1)
                        act.wait_ge(S["f_ln"], i - 1)
                        act.activation(rs[:, :], rs[:, :], ACT.Exp, scale=-0.5).then_inc(S["f_guess"], 1)
                    if g == 3 and live(i - 1):
                        act.wait_ge(S["f_xc"], i)
                        act.activation(xc2, xc, ACT.Square).then_inc(S["f_sq"], 1)
                    if live(i):
                        act.wait_ge(S["ssm_set"], done(i, g))
                        act.activation(ssl[:, g % 2, :], ssm[:, g % 2, :], ACT.Ln, scale=-2.0).then_inc(S["ssl_set"], 1)
                        act.wait_ge(S["ssl_set"], done(i, g))
                        wait(act, "rn_set", done(i, g, 2))
                        act.activation(guess[:, g % 2, :], ssl[:, g % 2, :], ACT.Exp, scale=-0.5).then_inc(S["guess_set"], 1)
                    if g == 2 and live(i - 2):
                        for c, (_, n) in enumerate(FCH):
                            act.wait_ge(S["f_hgc"], 3 * (i - 2) + c + 1)
                            act.activation(hg[0:n, c, N:], hg[0:n, c, N:], ACT.Gelu, bias=vec[0:n, 5 + c:6 + c]).then_inc(S["f_gate"], 1)
                        act.preload_act_table_set(LN_EXP)
                    j, gj = unit(i, g, 2)
                    if live(j):
                        act.wait_ge(S["o_mm"], done(i, g, 2))
                        if gj == 0:
                            wait(act, "f_y", j - 1)
                        dst = oT[:, bass.ds(j & 1, 1), 2 * gj:2 * gj + 2, :].rearrange("p u c n -> p (u c n)")
                        act.activation(dst, PS[:, 2, :], ACT.Copy).then_inc(S["o_set"], 1)
                    j, gj = unit(i, g, 1)
                    if live(j):
                        k = gj % 2
                        act.wait_ge(S["sub_set"], done(i, g, 1))
                        act.activation(pr[:, k].rearrange("p h t k -> p (h t k)"), pr[:, k].rearrange("p h t k -> p (h t k)"),
                                       ACT.Exp).then_inc(S["exp_set"], 1)
                    if g == 1 and live(i):
                        c0 = (((i >> 3) + 1) & 1) * QKV + (i & 7) * PIECE
                        act.wait_ge(S["ld_raw"], 16 * ((i >> 3) + 2))
                        act.activation(wh_flat[:, bass.ds(c0, PIECE)], w_raw[:, bass.ds(c0, PIECE)], ACT.Copy).then_inc(S["split_hi"], 1)

            sweep(act, body)

        @block.vector
        def _(dve):
            dve.wait_ge(S["ld_gw"], 16 * 7)
            dve.tensor_scalar(temp[:, 3:4], temp[:, 0:1], -1.0, None, ALU.mult).then_inc(S["temp_set"], 1)
            dve.wait_ge(S["temp_set"], 1)
            dve.tensor_tensor(temp[:, 2:3], temp[:, 0:1], temp[:, 3:4], ALU.max).then_inc(S["temp_set"], 1)
            dve.wait_ge(S["temp_set"], 2)
            dve.tensor_tensor(temp[:, 3:4], temp[:, 2:3], temp[:, 1:2], ALU.mult).then_inc(S["temp_set"], 1)
            dve.wait_ge(S["temp_set"], 3)
            dve.tensor_scalar(temp[:, 4:5], temp[:, 3:4], 1.0, 1.0, ALU.add, ALU.max).then_inc(S["temp_set"], 1)
            dve.wait_ge(S["temp_set"], 4)
            dve.reciprocal(temp[:, 5:6], temp[:, 4:5]).then_inc(S["temp_set"], 1)
            x3 = x_tok[:, :].rearrange("p (a d) -> p a d", d=D)
            xc3 = xc_tok.rearrange("p (a d) -> p a d", d=D)
            dve.wait_ge(S["ld_x"], 16)
            dve.tensor_reduce(stat[:, 0, :], x3, AX_X, ALU.add).then_inc(S["ln_step"], 1)
            dve.wait_ge(S["ln_step"], 1)
            dve.tensor_scalar(stat[:, 1, :], stat[:, 0, :], 1.0 / D, None, ALU.mult).then_inc(S["ln_step"], 1)
            dve.wait_ge(S["ln_step"], 2)
            dve.tensor_tensor(xc3, x3, stat[:, 1, :].unsqueeze(2).to_broadcast([P, TILES, D]), ALU.subtract).then_inc(S["ln_step"], 1)
            dve.tensor_tensor(x3, x3, bo.unsqueeze(1).to_broadcast([P, TILES, D]), ALU.add).then_inc(S["ln_step"], 1)
            dve.wait_ge(S["ln_sq"], 1)
            dve.tensor_reduce(stat[:, 2, :], sq_tok.rearrange("p (a d) -> p a d", d=D), AX_X, ALU.add).then_inc(S["ln_step"], 1)
            dve.wait_ge(S["ln_step"], 5)
            dve.tensor_scalar(stat[:, 3, :], stat[:, 2, :], 1.0 / D, 1e-5, ALU.mult, ALU.add).then_inc(S["ln_step"], 1)
            dve.wait_ge(S["ln_guess"], 2)
            dve.scalar_tensor_tensor(out=stat[:, 1, :], in0=stat[:, 0, :], scalar=-0.5, in1=stat[:, 0, :], op0=ALU.mult, op1=ALU.mult).then_inc(S["ln_step"], 1)
            dve.wait_ge(S["ln_step"], 7)
            dve.tensor_tensor(stat[:, 2, :], stat[:, 1, :], stat[:, 3, :], ALU.mult).then_inc(S["ln_step"], 1)
            dve.wait_ge(S["ln_step"], 8)
            dve.scalar_tensor_tensor(out=stat[:, 1, :], in0=stat[:, 2, :], scalar=1.5, in1=stat[:, 0, :], op0=ALU.add, op1=ALU.mult).then_inc(S["ln_step"], 1)
            dve.wait_ge(S["ln_step"], 9)
            dve.tensor_tensor(xc3, xc3, stat[:, 1, :].unsqueeze(2).to_broadcast([P, TILES, D]), ALU.mult).then_inc(S["ln_step"], 1)
            dve.wait_ge(S["spread_mm"], 1)
            dve.tensor_scalar(qscale[:, :], PS[:, 7, 0:1], float(D) ** -0.5, None, ALU.mult).then_inc(S["qscale_set"], 1)
            dve.wait_ge(S["ld_const"], 16 * 5)
            dve.tensor_copy(ident_bf[:, :], ident[:, :])
            dve.tensor_copy(mask_bf[:, :], mask_f).then_inc(S["mask_set"], 1)
            dve.wait_ge(S["split_hi"], 1)
            dve.tensor_tensor(wl_flat[:, 0:QKV], w_raw[:, 0:QKV], wh_flat[:, 0:QKV].bitcast(F32), ALU.subtract).then_inc(S["split_lo"], 1)

            def g_body(b):
                for c in range(GU):
                    if glive(b):
                        bank = 2 * (c % 2)
                        dve.wait_ge(S["g_s"], gdone(b, c))
                        wait(dve, "g_sub", gdone(b, c, 2))
                        dve.tensor_reduce(gmx[:, c % 2, :], PS[:, bank:bank + 2, 0:NK], AX_X, ALU.max).then_inc(S["g_mx"], 1)
                        dve.wait_ge(S["g_mx"], gdone(b, c))
                        wait(dve, "g_pt", gdone(b, c, 4))
                        wait(dve, "g_void", gdone(b, c, 4))
                        dve.tensor_tensor(gp[:, c % 4], PS[:, bank:bank + 2, 0:NK],
                                          gmx[:, c % 2, :].unsqueeze(2).to_broadcast([P, 2, NK]), ALU.subtract).then_inc(S["g_sub"], 1)
                    j, cj = gunit(b, c, 6)
                    if glive(j) and cj % 4 == 3:
                        n = cj // 4
                        dve.wait_ge(S["g_tok"], 4 * j + n + 1)
                        if n == 0:
                            wait(dve, "g_acc", j)
                        dve.tensor_copy(gtok.rearrange("p (t h) d -> p t h d", t=TT)[:, :, 4 * n:4 * n + 4, :],
                                        PS[:, 6, 0:N].rearrange("p (t h d) -> p t h d", t=TT, h=4)[:, :, :, 0:GD + 1]).then_inc(S["g_tokev"], 1)
                    f = b - 1
                    if c == 5 and glive(f):
                        dve.wait_ge(S["g_void"], b * GU)
                        void = gpv[:, bass.ds((f & 1) * (TT * GH), TT * GH)]
                        dve.tensor_tensor(
                            gacc.rearrange("p (t h) d -> p t h d", t=TT),
                            void.rearrange("p (t h) -> p t h", t=TT).unsqueeze(3).to_broadcast([P, TT, GH, GD + 1]),
                            voidv[:, :, :].unsqueeze(1).to_broadcast([P, TT, GH, GD + 1]), ALU.mult).then_inc(S["g_num"], 1)
                    if c == 6 and glive(f):
                        dve.wait_ge(S["g_num"], b)
                        dve.wait_ge(S["g_tokev"], 4 * b)
                        dve.tensor_tensor(gacc[:, :, :], gacc[:, :, :], gtok[:, :, :], ALU.add).then_inc(S["g_acc"], 1)
                    if c == 7 and glive(f):
                        dve.wait_ge(S["g_acc"], b)
                        dve.reciprocal(gden[:, :], gacc[:, :, GD]).then_inc(S["g_den"], 1)
                    if c == 8 and glive(f):
                        dve.wait_ge(S["g_den"], b)
                        wait(dve, "g_attT_mm", b - 1)
                        dve.tensor_tensor(gatt[:, :, :].rearrange("p t (h d) -> p (t h) d", h=GH), gacc[:, :, 0:GD],
                                          gden[:, :].unsqueeze(2).to_broadcast([P, TT * GH, GD]), ALU.mult).then_inc(S["g_att"], 1)
                    if c == 12 and glive(f):
                        rows = x_tok[:, bass.ds((b - 1) * (TT * D), TT * D)]
                        dve.wait_ge(S["g_y"], b)
                        dve.tensor_tensor(rows, rows, PS[:, 7, 0:N], ALU.add).then_inc(S["g_res"], 1)

            gsweep(dve, g_body)

            def take_state(i):
                b = i & (B - 1)
                wait(dve, "s_v", NG * i)
                dve.wait_ge(S["state_set"], i + 1)
                dve.tensor_scalar(xh[lower, :], state(lower, b, 0), 1.0, None, ALU.mult)
                dve.tensor_scalar(xh[upper, :], state(upper, b, 1), 1.0, None, ALU.mult).then_inc(S["xh_set"], 1)
                dve.wait_ge(S["xh_set"], i + 1)
                dve.tensor_tensor(xl[lower, :], state(lower, b, 0), xh[lower, :].bitcast(F32), ALU.subtract)
                dve.tensor_tensor(xl[upper, :], state(upper, b, 1), xh[upper, :].bitcast(F32), ALU.subtract).then_inc(S["xl_set"], 1)

            take_state(0)
            dve.wait_ge(S["rot_set"], 1)
            ROT = TT * 2 * DH

            def inverse_deviations(f):
                dve.wait_ge(S["f_guess"], f + 1)
                wait(dve, "f_hg", 3 * f)
                dve.scalar_tensor_tensor(out=xn[:, :], in0=rs[:, :], scalar=-0.5, in1=rs[:, :], op0=ALU.mult, op1=ALU.mult).then_inc(S["f_n1"], 1)
                dve.wait_ge(S["f_n1"], f + 1)
                dve.tensor_tensor(var[:, :], xn[:, :], var[:, :], ALU.mult).then_inc(S["f_n2"], 1)
                dve.wait_ge(S["f_n2"], f + 1)
                dve.scalar_tensor_tensor(out=rs[:, :], in0=var[:, :], scalar=1.5, in1=rs[:, :], op0=ALU.add, op1=ALU.mult).then_inc(S["f_rs"], 1)

            def normalise(f):
                dve.wait_ge(S["f_rs"], f + 1)
                dve.tensor_tensor(var[:, :], xc, rs[:, :], ALU.mult).then_inc(S["f_xr"], 1)
                dve.wait_ge(S["f_xr"], f + 1)
                dve.wait_ge(S["f_vec"], f + 1)
                dve.tensor_scalar(xn[:, :], var[:, :], vec[:, 0:1], vec[:, 1:2], ALU.mult, ALU.add).then_inc(S["f_xn"], 1)

            def take_hidden(f, c):
                n = FCH[c][1]
                dve.wait_ge(S["f_hg"], 3 * f + c + 1)
                wait(dve, "f_h", 3 * f)
                dve.tensor_scalar(hg[0:n, c, 0:N], PS[0:n, 7, 0:N], vec[0:n, 2 + c:3 + c], None, ALU.add)
                dve.tensor_copy(hg[0:n, c, N:], PS[0:n, 7, N:]).then_inc(S["f_hgc"], 1)

            def body(i):
                for g in range(NG):
                    if g == 0 and live(i - 2):
                        dve.wait_ge(S["f_var"], i - 1)
                        dve.tensor_scalar(var[:, :], PS[:, 7, N:2 * N], 1e-5, None, ALU.add).then_inc(S["f_ve"], 1)
                    j, gj = unit(i, g, 2)
                    if live(j):
                        k = gj % 2
                        dve.wait_ge(S["exp_set"], done(i, g, 2))
                        dve.tensor_reduce(rsum[:, k, :], pr[:, k].rearrange("p h t k -> p (h t) k"), AX_X, ALU.add).then_inc(S["sum_set"], 1)
                        dve.wait_ge(S["sum_set"], done(i, g, 2))
                        dve.reciprocal(rinv[:, k, :], rsum[:, k, :]).then_inc(S["inv_set"], 1)
                    if g == 1 and live(i - 3):
                        f = i - 3
                        dve.wait_ge(S["f_y2"], f + 1)
                        new = xT[:, bass.ds((f & 7) * (N + 1) + 1, N)]
                        dve.scalar_tensor_tensor(out=new, in0=PS[:, 7, 0:N], scalar=vec[:, 8:9], in1=x1[:, bass.ds(f & 1, 1)].squeeze(1),
                                                 op0=ALU.add, op1=ALU.add).then_inc(S["state_set"], 1)
                    if g == 1 and live(i - 2):
                        if live(i - 3):
                            dve.wait_ge(S["state_set"], B + i - 2)
                            dve.wait_ge(S["f_gate"], 3 * (i - 2))
                        dve.tensor_copy(vec[:, :], vec_all[:, bass.ds(layer_of(i - 2) * NVEC, NVEC)]).then_inc(S["f_vec"], 1)
                        normalise(i - 2)
                    if g == 2 and live(i - 2):
                        take_hidden(i - 2, 1)
                    if g == 3 and live(i - 1):
                        f = i - 1
                        dve.wait_ge(S["f_y"], f + 1)
                        dve.wait_ge(S["state_set"], B - 1 + f)
                        own = bass.ds(f & 1, 1)
                        dve.tensor_tensor(x1[:, own].squeeze(1), PS[:, 7, N:2 * N],
                                          xT[:, bass.ds((f & 7) * (N + 1) + 1, N)], ALU.add).then_inc(S["f_x1"], 1)
                        dve.wait_ge(S["f_x1"], f + 1)
                        wait(dve, "f_xc", f)
                        dve.tensor_scalar(xs2[lower, :], x1[lower, own].squeeze(1), 1.0, None, ALU.mult)
                        dve.tensor_scalar(xs2[upper, 1:], x1[upper, own, 0:N - 1].squeeze(1), 1.0, None, ALU.mult).then_inc(S["f_xs2"], 1)
                    k = g % 2
                    if live(i):
                        wait(dve, "qn_set", 2 * done(i, g, 2))
                        qk4 = PS[:, 0:2, :].rearrange("p t (q h d) -> p (t q) h d", q=2, h=HG)
                        layer = layer_of(i)
                        cos = rot[:, bass.ds(layer * (2 * ROT), ROT)].rearrange("p (u d) -> p u d", d=DH)
                        sin = rot[:, bass.ds(layer * (2 * ROT) + ROT, ROT)].rearrange("p (u d) -> p u d", d=DH)
                        t4 = t1[:, k].rearrange("p (u h d) -> p u h d", u=4, h=HG)
                        for t in range(TT):
                            dve.wait_ge(S["sq_set"], TT * (done(i, g) - 1) + t + 1)
                            u2 = slice(2 * t, 2 * t + 2)
                            last = dve.tensor_tensor(t4[:, u2], qk4[:, u2], cos[:, u2].unsqueeze(2).to_broadcast([P, 2, HG, DH]), ALU.mult)
                        last.then_inc(S["t1_set"], 1)
                        hd = DH // 2
                        wait(dve, "add_set", done(i, g, 1))
                        o4 = t2.rearrange("p (u h d) -> p u h d", u=4, h=HG)
                        for lo, hi in ((0, hd), (hd, 0)):
                            last = dve.tensor_tensor(o4[:, :, :, lo:lo + hd], qk4[:, :, :, hi:hi + hd],
                                                     sin[:, :, lo:lo + hd].unsqueeze(2).to_broadcast([P, 4, HG, hd]), ALU.mult)
                        last.then_inc(S["t2_set"], 1)
                    if g == 3 and live(i - 1):
                        dve.wait_ge(S["f_mean"], i)
                        dve.wait_ge(S["f_xs2"], i)
                        dve.tensor_tensor(xc, xs2[:, :], PS[:, 7, 0:N], ALU.subtract).then_inc(S["f_xc"], 1)
                    if live(i):
                        dve.tensor_reduce(ss[:, :], sq.rearrange("p (u d) -> p u d", d=DH), AX_X, ALU.add).then_inc(S["ss_set"], 1)
                        dve.wait_ge(S["ss_set"], done(i, g))
                        wait(dve, "nw2_set", done(i, g, 2))
                        dve.tensor_scalar(ssm[:, k, :], ss[:, :], 1e-24, -0.5 * NORM_G ** 2, ALU.max, ALU.mult).then_inc(S["ssm_set"], 1)
                    if g == 3 and live(i) and (not isinstance(i, int) or i + 1 < ITERS):
                        take_state(i + 1)
                    if g == 1 and live(i - 2):
                        take_hidden(i - 2, 0)
                    if g == 2 and live(i - 2):
                        take_hidden(i - 2, 2)
                    j, gj = unit(i, g, 1)
                    if live(j):
                        k = gj % 2
                        s3 = PS[:, 5, :].rearrange("p (u k) -> p u k", k=2 * WIN)
                        dve.wait_ge(S["s_mm"], done(i, g, 1))
                        dve.tensor_reduce(rmx[:, k, :], s3, AX_X, ALU.max).then_inc(S["mx_set"], 1)
                        dve.wait_ge(S["mx_set"], done(i, g, 1))
                        wait(dve, "pt_mm", done(i, g, 3))
                        dve.tensor_tensor(pr[:, k].rearrange("p h t k -> p (h t) k"), s3,
                                          rmx[:, k, :].unsqueeze(2).to_broadcast([P, TT * HG, 2 * WIN]), ALU.subtract).then_inc(S["sub_set"], 1)
                    if g == 0 and live(i - 2):
                        inverse_deviations(i - 2)

            sweep(dve, body)
            for q in range(4):
                dve.wait_ge(S["o_t"], q + 1)
                rows = x_tok[:, 4 * q * D:4 * (q + 1) * D]
                dve.tensor_tensor(rows, rows, PS[:, q, :], ALU.add).then_inc(S["o_add"], 1)

        @block.tensor
        def _(pe):
            pe.wait_ge(S["ld_const"], 16 * 5)
            pe.wait_ge(S["temp_set"], 5)
            pe.matmul(PS[:, 7, 0:1], spread[:, :], temp[:, 5:6], start=True, stop=True).then_inc(S["spread_mm"], 1)
            pe.wait_ge(S["ln_step"], 10)
            for q in range(4):
                for a in range(4):
                    c = (4 * q + a) * D
                    last = pe.transpose(PS[:, q, a * P:(a + 1) * P], xc_tok[:, c:c + D], ident[:, :])
                last.then_inc(S["xn_t"], 1)
            misc = PS[:, 7, 0:N]

            def g_keys(b):
                pe.matmul(misc, wg[:, D:2 * D], state(slice(0, P), b, 0), start=True, stop=True).then_inc(S["g_k_mm"], 1)

            pe.wait_ge(S["state_set"], B)
            pe.wait_ge(S["ld_gw"], 16 * 7)
            pe.wait_ge(S["qscale_set"], 1)
            g_keys(0)

            def g_body(b, more=True):
                for c in range(GU):
                    if glive(b) and c == 0:
                        wait(pe, "g_k", b + 1)
                        wait(pe, "g_res", b - 1)
                        pe.matmul(misc, wg[:, 0:D], state(slice(0, P), b, 0), start=True, stop=True).then_inc(S["g_q_mm"], 1)
                        pe.wait_ge(S["g_q"], b + 1)
                        pe.wait_ge(S["g_kz"], 4 * (b + 1))
                        pe.wait_ge(S["voidk_set"], 1)
                    if glive(b):
                        wait(pe, "g_sub", gdone(b, c, 2))
                        for e in range(2):
                            h = c // 2 * 2 + e
                            keys = gkz[:, bass.ds((b & 1) * (GH * NK) + h * NK, NK)]
                            t = c % 2
                            last = pe.matmul(PS[:, 2 * (c % 2) + e, 0:NK], gq[:, t * P:(t + 1) * P], keys, start=True, stop=True)
                        last.then_inc(S["g_s"], 1)
                    if glive(b) and c == 1:
                        pe.wait_ge(S["g_x"], b + 1)
                        for t in range(TT):
                            last = pe.matmul(PS[:, 7, t * P:(t + 1) * P], xg[:, t * P:(t + 1) * P], wg[:, 2 * D:3 * D], start=True, stop=True)
                        last.then_inc(S["g_v_mm"], 1)
                    j, cj = gunit(b, c, 2)
                    if glive(j):
                        pe.wait_ge(S["g_exp"], gdone(b, c, 2))
                        wait(pe, "g_pT", gdone(b, c, 3))
                        for e in range(2):
                            for kt in range(TT):
                                n = 2 * e + kt
                                last = pe.transpose(PS[:, 4, n * P:(n + 1) * P], gp[:, cj % 4, e, kt * P:(kt + 1) * P], ident[:, :])
                        last.then_inc(S["g_pt"], 1)
                    j, cj = gunit(b, c, 3)
                    if glive(j):
                        n, pair, t = cj // 4, cj // 2 % 2, cj % 2
                        pe.wait_ge(S["g_pT"], gdone(b, c, 3))
                        if cj == 0:
                            pe.wait_ge(S["g_v"], j + 1)
                        if cj % 4 == 0:
                            wait(pe, "g_oT", 4 * j + n)
                        for kt in range(TT):
                            for e in range(2):
                                h = cj // 2 * 2 + e
                                r = 32 * (2 * pair + e)
                                last = pe.matmul(PS[r:r + 32, 5, t * P:(t + 1) * P], gv[:, kt, h, :],
                                                 gpT[:, cj % 2, (2 * e + kt) * P:(2 * e + kt + 1) * P],
                                                 start=(kt == 0), stop=(kt == 1), skip_group_check=True)
                        last.then_inc(S["g_o"], 1)
                    j, cj = gunit(b, c, 5)
                    if glive(j) and cj % 4 == 3:
                        n = cj // 4
                        pe.wait_ge(S["g_oT"], 4 * j + n + 1)
                        wait(pe, "g_tokev", 4 * j + n)
                        for t in range(TT):
                            last = pe.transpose(PS[:, 6, t * P:(t + 1) * P], goT[:, n % 2, t * P:(t + 1) * P], ident[:, :])
                        last.then_inc(S["g_tok"], 1)
                    if c == 5 and glive(b) and more:
                        wait(pe, "g_res", b - 1)
                        pe.wait_ge(S["g_v"], b + 1)
                        g_keys(b + 1)
                    if c == 10 and glive(b - 1):
                        pe.wait_ge(S["g_att"], b)
                        if glive(b):
                            pe.wait_ge(S["g_v"], b + 1)
                            if more:
                                pe.wait_ge(S["g_k"], b + 2)
                        for t in range(TT):
                            last = pe.transpose(PS[:, 7, t * P:(t + 1) * P], gatt[:, t, :], ident[:, :])
                        last.then_inc(S["g_attT_mm"], 1)
                    if c == 11 and glive(b - 1):
                        pe.wait_ge(S["g_attT"], b)
                        for t in range(TT):
                            last = pe.matmul(PS[:, 7, t * P:(t + 1) * P], gattT[:, t * P:(t + 1) * P], wgo, start=True, stop=True)
                        last.then_inc(S["g_y"], 1)

            g_body(0)
            g_body(1)
            with pe.Fori(2, B - 1) as b:
                g_body(b)
            g_body(B - 1, more=False)
            g_body(B)

            pe.wait_ge(S["mask_set"], 1)

            def body(i):
                for g in range(NG):
                    if live(i):
                        if g == 0:
                            pe.wait_ge(S["xl_set"], i + 1)
                            pe.wait_ge(S["split_lo"], 1 + (i >> 3) * B)
                        if isinstance(i, int) and i == 0 and g == 0:
                            pe.wait_ge(S["g_res"], B)
                            pe.wait_ge(S["g_void"], GU * B)
                        u = (i >> 3) & 1
                        parts = ((xh, wh), (xh, wl), (xl, wh))
                        wait(pe, "t2_set", done(i, g, 1))
                        for t in range(TT):
                            for n, (x, w) in enumerate(parts):
                                last = pe.matmul(PS[:, t, :], x[:, t * P:(t + 1) * P], w[:, bass.ds(u, 1), 0:2, g * GC:(g + 1) * GC].squeeze(1),
                                                 start=(n == 0), stop=(n == 2))
                            last.then_inc(S["s_qk"], 1)
                        wait(pe, "v_set", done(i, g, 1))
                        wait(pe, "o_set", done(i, g, 3))
                        for t in range(TT):
                            for n, (x, w) in enumerate(parts):
                                last = pe.matmul(PS[:, 2, t * GC:(t + 1) * GC], x[:, t * P:(t + 1) * P], w[:, bass.ds(u, 1), 2, g * GC:(g + 1) * GC].squeeze(1),
                                                 start=(n == 0), stop=(n == 2))
                        last.then_inc(S["s_v"], 1)
                    j, gj = unit(i, g, 1)
                    if live(j):
                        k = gj % 2
                        for q, (free, mm) in enumerate((("qT_set", "tq_mm"), ("kz_set", "tk_mm"))):
                            pe.wait_ge(S["qn_set"], 2 * done(i, g, 1) - 1 + q)
                            wait(pe, free, done(i, g, 2))
                            for a in range(PR):
                                for t in range(TT):
                                    c = (t * 2 + q) * GC + a * P
                                    last = pe.transpose(PS[:, 3 + q, a * N + t * P:a * N + (t + 1) * P], qn[:, k, c:c + P], ident[:, :])
                            last.then_inc(S[mm], 1)
                    if g == 0 and live(i - 3):
                        f = i - 3
                        pe.wait_ge(S["f_h"], 3 * (f + 1))
                        pe.wait_ge(S["ld_w2"], 32 * ((f >> 3) + 1))
                        if live(i - 2):
                            pe.wait_ge(S["f_ve"], f + 2)
                        for c, (_, n) in enumerate(FCH):
                            last = pe.matmul(PS[:, 7, 0:N], w2[0:n, c, :], hT[0:n, c, :], start=(c == 0), stop=(c == 2))
                        last.then_inc(S["f_y2"], 1)
                    j, gj = unit(i, g, 2)
                    if live(j):
                        k = gj % 2
                        pe.wait_ge(S["pn_set"], done(i, g, 2))
                        wait(pe, "pT_set", done(i, g, 3))
                        for h in range(HG):
                            last = pe.transpose(PS[:, 6, h * P:(h + 1) * P], pr[:, k, h].rearrange("p t k -> p (t k)"), ident[:, :])
                        last.then_inc(S["pt_mm"], 1)
                    if g == 1 and live(i - 2):
                        if live(i - 3):
                            pe.wait_ge(S["state_set"], B + i - 2)
                        hidden(i - 2, 0)
                    if g == 2 and live(i - 2):
                        hidden(i - 2, 2)
                    if g == 3 and live(i - 1):
                        pe.wait_ge(S["f_xs2"], i)
                        pe.matmul(PS[:, 7, 0:N], mean_mat[:, :], xs2[:, :], start=True, stop=True).then_inc(S["f_mean"], 1)
                    j, gj = unit(i, g, 1)
                    if live(j):
                        k = gj % 2
                        pe.wait_ge(S["qT_set"], done(i, g, 1))
                        pe.wait_ge(S["kz_set"], done(i, g, 1))
                        wait(pe, "sub_set", done(i, g, 2))
                        scores = PS[:, 5, :].rearrange("p (h t k) -> p h t k", h=HG, t=TT)
                        pe.matmul(PS[:, 5, :], ident_bf[:, :], mask_bf[:, :], start=True, stop=False, skip_group_check=True)
                        for t in range(TT):
                            for a in range(PR):
                                for w in range(NW):
                                    q0, k0 = t * P + w * WIN, (t * NW + w) * WIN
                                    last = pe.matmul(scores[w * WIN:(w + 1) * WIN, 2 * a:2 * a + 2, t, :], qT[:, k, a, q0:q0 + WIN],
                                                     kz[:, k, a, :, k0:k0 + 2 * WIN], start=False, stop=True, skip_group_check=True)
                        last.then_inc(S["s_mm"], 1)
                    j, gj = unit(i, g, 2)
                    if live(j):
                        pe.wait_ge(S["pT_set"], done(i, g, 2))
                        if live(i):
                            pe.wait_ge(S["v_set"], done(i, g))
                        wait(pe, "o_set", done(i, g, 3))
                        for a in range(PR):
                            for t, q0, probs in ((0, 0, pT0), (1, P, pT1)):
                                for e in range(2):
                                    h = 2 * a + e
                                    n = probs.shape[2]
                                    last = pe.matmul(PS[e * DH:(e + 1) * DH, 2, a * N + q0:a * N + q0 + n],
                                                     v[:, gj, t, h * DH:(h + 1) * DH], probs[:, h, :],
                                                     start=(t == 0), stop=(t == 1), skip_group_check=True)
                        last.then_inc(S["o_mm"], 1)
                    if g == 1 and live(i - 2):
                        hidden(i - 2, 1)
                    if g == 2 and live(i - 1):
                        f = i - 1
                        pe.wait_ge(S["o_set"], 4 * (f + 1))
                        pe.wait_ge(S["ld_wo"], 16 * ((f >> 3) + 1))
                        wait(pe, "f_hgc", 3 * f)
                        for c in range(2 * NG):
                            last = pe.matmul(PS[:, 7, N:2 * N], wo[:, c, :], oT[:, bass.ds(f & 1, 1), c, :].squeeze(1), start=(c == 0), stop=(c == 2 * NG - 1))
                        last.then_inc(S["f_y"], 1)
                    if g == 3 and live(i - 1):
                        pe.wait_ge(S["f_sq"], i)
                        pe.matmul(PS[:, 7, N:2 * N], mean_mat[:, :], xc2, start=True, stop=True).then_inc(S["f_var"], 1)

            def hidden(f, c):
                c0, n = FCH[c]
                pe.wait_ge(S["f_xn"], f + 1)
                pe.wait_ge(S["ld_w1"], 16 * ((f >> 3) + 1))
                wait(pe, "f_hgc", 3 * f + c)
                for half in range(2):
                    w0 = half * FI + c0
                    last = pe.matmul(PS[0:n, 7, half * N:(half + 1) * N], w1[:, w0:w0 + n], xn[:, :], start=True, stop=True)
                last.then_inc(S["f_hg"], 1)

            sweep(pe, body)
            pe.wait_ge(S["state_set"], B + ITERS)
            for q in range(4):
                for a in range(4):
                    b, t = (4 * q + a) // TT, a % TT
                    c = b * (N + 1) + 1 + t * P
                    last = pe.transpose(PS[:, q, a * P:(a + 1) * P], xT[:, c:c + P], ident[:, :])
                last.then_inc(S["o_t"], 1)


_INS = ["L0_attn_x", "L0_attn_w_qkv", "L0_attn_w_out", "L0_attn_b_out", "L0_attn_void_q", "L0_attn_void_k",
        "L0_attn_void_v", "L0_attn_attention_trace", "L0_attn_temperature_factor", "L0_ffn_Wqkv", "L0_ffn_q_scale",
        "L0_ffn_k_scale", "L0_ffn_Wo", "L0_ffn_ln_g", "L0_ffn_ln_b", "L0_ffn_W1", "L0_ffn_b1", "L0_ffn_W2", "L0_ffn_b2"]


def kernel(**inputs):
    import concourse.bacc as _bacc
    from concourse.bass_utils import run_bass_kernel_spmd as _run

    nc = _bacc.Bacc("TRN2", target_bir_lowering=False, num_devices=1)
    given = {name: np.ascontiguousarray(inputs[name]) for name in _INS if name != "L0_attn_void_q"}
    given.update(shape_constants())
    arrays, aps = {}, {}
    for name, a in given.items():
        arrays[f"in_{name}"] = a
        aps[name] = nc.dram_tensor(f"in_{name}", a.shape, mybir.dt.from_np(a.dtype), kind="ExternalInput").ap()
    result = nc.dram_tensor("result", (B, N, D), F32, kind="ExternalOutput").ap()
    bass_dual_attention(nc, aps, result)
    r = _run(nc, [arrays], core_ids=[0])
    return r.results[0]["result"]
```

```python
from contextlib import ExitStack

import numpy as np
import concourse.bass as bass
from concourse import mybir

F32 = mybir.dt.float32
F32R = mybir.dt.float32r
BF16 = mybir.dt.bfloat16
ALU = mybir.AluOpType
ACT = mybir.ActivationFunctionType
AX_X = mybir.AxisListType.X

P = 128
B, N, D = 8, 256, 128
TT = N // P
TILES = B * TT
GH, GD = 16, 8
NK = N + 1
GU = TT * GH // 2
DEPTH, H, DH, WIN = 6, 16, 64, 32
INNER = H * DH
NG = 4
HG = H // NG
GC = HG * DH
PR = HG // 2
NW = P // WIN
ITERS = DEPTH * B
FI = int(D * 4 * 2 / 3)
FCH = [(0, 128), (128, 128), (256, FI - 256)]
QKV = 3 * INNER
PIECE = QKV // B
LN_PARTS = ((0, TT), (TT, TILES))
LN_EXP = "natural_log_exp_and_others"
NORM_G = 2.0 ** 10
NVEC = 9


def shape_constants():
    half = np.arange(0, DH, 2, dtype=np.float32)
    inv_freq = (1.0 / 10000.0 ** (half / DH)).astype(np.float32)
    t = np.arange(N, dtype=np.float32)
    freqs = t[:, None] * inv_freq[None, :]
    freqs = np.concatenate([freqs, freqs], -1).astype(np.float64)
    base = (half.astype(np.float64) + 0.4 * DH) / (1.4 * DH)
    power = (t.astype(np.float64) - N // 2) / (WIN // 2)
    scale = base[None, :] ** power[:, None]
    scale = np.concatenate([scale, scale], -1)
    sign = np.where(np.arange(DH) < DH // 2, -1.0, 1.0)
    cos, sin = np.cos(freqs), np.sin(freqs) * sign
    q_gain = 8.0
    rot = np.zeros((P, 2, TT, 2, DH))
    for k, trig in enumerate((cos, sin)):
        for tt in range(TT):
            rows = slice(tt * P, (tt + 1) * P)
            rot[:, k, tt, 0] = trig[rows] * scale[rows] * q_gain * NORM_G
            rot[:, k, tt, 1] = trig[rows] / scale[rows] * NORM_G
    mask = np.zeros((P, HG, TT, 2 * WIN))
    qi = (np.arange(P) % WIN)[:, None]
    w = (np.arange(P) // WIN)[:, None]
    j = np.arange(2 * WIN)[None, :]
    for tt in range(TT):
        bad = (j - WIN > qi) | (qi > j) | ((w + tt * NW == 0) & (j < WIN))
        mask[:, :, tt] = np.where(bad, -1e30, 0.0)[:, None, :]
    head_of = np.arange(P)[:, None] // GD == np.arange(GH)[None, :]
    return {
        "c_ident": np.eye(P, dtype=np.float32),
        "c_rot": rot.reshape(P, -1).astype(np.float32),
        "c_mask": mask.reshape(P, -1).astype(np.float32),
        "c_head": head_of.astype(np.float32),
        "c_spread": np.ascontiguousarray(head_of.T).astype(np.float32),
    }


def bass_dual_attention(nc: bass.Bass, A: dict, out: bass.AP):
    with ExitStack() as ctx:
        def sb(name, shape, dt=F32):
            return ctx.enter_context(nc.sbuf_tensor(name, shape, dt))

        PS = ctx.enter_context(nc.psum_tensor("PS", [P, 8, 512], F32))

        ident = sb("ident", [P, P])
        ident_bf = sb("ident_bf", [P, P], BF16)
        mask_bf = sb("mask_bf", [P, 512], BF16)
        head_col = sb("head_col", [P, GH])
        mean_mat = sb("mean_mat", [P, P])
        rot = sb("rot", [P, DEPTH * 2 * TT * 2 * DH])
        vec_all = sb("vec_all", [P, DEPTH * NVEC])
        vec = sb("vec", [P, NVEC])
        x_tok = sb("x_tok", [P, TILES * D])
        xT = sb("xT", [P, B * (N + 1)])
        temp = sb("temp", [GH, 6])
        qscale = sb("qscale", [P, 1])
        voidk = sb("voidk", [P, 1])
        shared = sb("shared", [P, 4, N])
        gq, gk, xg, gattT = (shared[:, k, :] for k in range(4))
        gmx = sb("gmx", [P, 2, 2])
        w_raw = sb("w_raw", [P, 2 * QKV])
        wh = sb("wh", [P, 2, 3, INNER], F32R)
        wl = sb("wl", [P, 2, 3, INNER], F32R)
        xh = sb("xh", [P, N], F32R)
        xl = sb("xl", [P, N], F32R)
        rmx = sb("rmx", [P, 2, TT * HG])
        rsum = sb("rsum", [P, 2, TT * HG])
        rinv = sb("rinv", [P, 2, TT * HG])
        ss = sb("ss", [P, 16])
        ssm = sb("ssm", [P, 2, 16])
        ssl = sb("ssl", [P, 2, 16])
        guess = sb("guess", [P, 2, 16])
        one_half = sb("one_half", [P, 16])
        newton = sb("newton", [P, 3, 16])
        rn = sb("rn", [P, 2, 16])
        wo = sb("wo", [P, INNER // P, D])
        w1 = sb("w1", [P, 2 * FI])
        w2 = sb("w2", [P, 3, D])
        x1 = shared[:, 0:2, :]
        xc, rs = shared[:, 2, :], shared[:, 3, :]
        xs2 = sb("xs2", [P, N])
        var = sb("var", [P, N])
        xn = sb("xn", [P, N])
        hT = sb("hT", [P, 3, N])

        arena = sb("arena", [P, 21376])
        taken = [0]

        def part(n):
            taken[0] += n
            return arena[:, taken[0] - n:taken[0]]

        gkz = part(2 * GH * NK)
        sq_tok = arena[:, taken[0]:taken[0] + TILES * D]
        gp = part(4 * 2 * NK).rearrange("p (u e k) -> p u e k", u=4, e=2)
        gpT = part(2 * 512).rearrange("p (u n) -> p u n", u=2)
        goT = part(2 * N).rearrange("p (u n) -> p u n", u=2)
        gtok = part(TT * GH * (GD + 1)).rearrange("p (h d) -> p h d", d=GD + 1)
        gacc = part(TT * GH * (GD + 1)).rearrange("p (h d) -> p h d", d=GD + 1)
        xc_tok = part(TILES * D)
        mask_f = part(512)
        rot_base = part(2 * TT * 2 * DH).rearrange("p (k t n) -> p k t n", k=2, t=TT)
        gains = part(DEPTH * 2 * DH).rearrange("p (l n) -> p l n", l=DEPTH)
        gains_sw = part(DEPTH * 2 * DH).rearrange("p (l n) -> p l n", l=DEPTH)
        wg, wgo, bo = part(3 * D), part(D), part(D)
        spread = part(P)[0:GH]
        stat = part(4 * TILES).rearrange("p (k a) -> p k a", k=4)
        voidv = part(GH * (GD + 1)).rearrange("p (h d) -> p h d", h=GH)
        gpv, gden = part(2 * TT * GH), part(TT * GH)
        gatt = part(TT * D).rearrange("p (t d) -> p t d", t=TT)
        gv = part(TT * GH * 32).rearrange("p (t h d) -> p t h d", t=TT, h=GH)
        taken[0] = 0
        sq = part(1024)
        t1 = part(2048).rearrange("p (u n) -> p u n", u=2)
        t2 = part(1024)
        qn = part(2048).rearrange("p (u n) -> p u n", u=2)
        qT = part(1024).rearrange("p (u a n) -> p u a n", u=2, a=PR)
        kz = part(4 * PR * (N + WIN)).rearrange("p (u a e n) -> p u a e n", u=2, a=PR, e=2)
        v = part(4096).rearrange("p (u g t n) -> p u g t n", u=2, g=NG, t=TT)
        pr = part(1024).rearrange("p (u h t k) -> p u h t k", u=2, t=TT, h=HG)
        pT0 = part(HG * (P + WIN)).rearrange("p (h n) -> p h n", h=HG)
        pT1 = part(HG * P).rearrange("p (h n) -> p h n", h=HG)
        oT = part(4096).rearrange("p (u c n) -> p u c n", u=2, c=2 * NG)
        hg = part(3 * 512).rearrange("p (c n) -> p c n", c=3)

        wh_flat = wh[:, :, :, :].rearrange("p u a n -> p (u a n)")
        wl_flat = wl[:, :, :, :].rearrange("p u a n -> p (u a n)")

        names = """ld_x_first ld_x_rest ld_const ld_gw ld_tables ld_vec ld_raw ld_wo ld_w1 ld_w2 st_out
        vec_clear zeroed cleared ones_set mask_set temp_set spread_mm qscale_set voidk_set ln_step ln_guess g_bias ln_sq xn_t state_set rot_set
        g_k_mm g_k g_kz g_q_mm g_q g_x g_v_mm g_v g_s g_mx g_sub g_exp g_void g_pt g_pT g_o g_oT g_tok g_tokev g_num g_acc
        g_den g_att g_attT_mm g_attT g_y g_res
        split_hi split_lo xh_set xl_set s_qk s_v sq_set v_set ss_set ssm_set ssl_set guess_set nw1_set nw2_set nw3_set rn_set t2_set add_set qn_set
        tq_mm tk_mm qT_set kz_set s_mm mx_set sub_set exp_set sum_set inv_set pn_set pt_mm pT_set o_mm o_set
        f_y f_x1 f_xs2 f_mean f_xc f_sq f_var f_ve f_ln f_guess f_n1 f_n2 f_rs f_xr f_xn f_vec f_hg f_hgc f_gate f_h f_y2
        o_t o_add""".split()
        S = {n: ctx.enter_context(nc.semaphore(n)) for n in names}
        block = ctx.enter_context(nc.Block())

        def unit(i, g, back=0):
            return i + (g - back) // NG, (g - back) % NG

        def done(i, g, back=0):
            return i * NG + (g - back + 1)

        def live(i):
            return not isinstance(i, int) or 0 <= i < ITERS

        def layer_of(i):
            if isinstance(i, int):
                return i // B
            return nc.s_assert_within(i >> 3, 0, DEPTH - 1, skip_runtime_bounds_check_because="iterations end before ITERS")

        def wait(eng, name, value):
            if not isinstance(value, int) or value > 0:
                eng.wait_ge(S[name], value)

        def sweep(eng, body):
            for i in range(4):
                body(i)
            with eng.Fori(4, ITERS) as i:
                body(i)
            for i in range(ITERS, ITERS + 3):
                body(i)

        def sweep_pairs(eng, body):
            for i in range(4):
                body(i, i % 2)
            with eng.Fori(4, ITERS, 2) as i:
                body(i, 0)
                body(i + 1, 1)
            for i in range(ITERS, ITERS + 3):
                body(i, i % 2)

        def gunit(b, c, back=0):
            return b + (c - back) // GU, (c - back) % GU

        def gdone(b, c, back=0):
            return b * GU + (c - back + 1)

        def glive(b):
            return not isinstance(b, int) or 0 <= b < B

        def gsweep(eng, body):
            body(0)
            body(1)
            with eng.Fori(2, B) as b:
                body(b)
            body(B)

        def state(rows, b, shift):
            return xT[rows, bass.ds(b * (N + 1) + 1 - shift, N)]

        lower, upper = slice(0, D // 2), slice(D // 2, D)

        @block.sync
        def _(sp):
            x_t = A["L0_attn_x"].rearrange("b (t p) d -> p (b t) d", p=P)
            xt3 = x_tok[:, :].rearrange("p (a d) -> p a d", d=D)
            for loaded, (a0, a1) in zip(("ld_x_first", "ld_x_rest"), LN_PARTS):
                sp.dma_start(xt3[:, a0:a1, :], x_t[:, a0:a1, :]).then_inc(S[loaded], 16)
            sp.dma_start(ident[:, :], A["c_ident"]).then_inc(S["ld_const"], 16)
            sp.dma_start(head_col[:, :], A["c_head"]).then_inc(S["ld_const"], 16)
            sp.dma_start(spread, A["c_spread"]).then_inc(S["ld_const"], 16)
            sp.dma_start(wg, A["L0_attn_w_qkv"]).then_inc(S["ld_gw"], 16)
            sp.dma_start(wgo, A["L0_attn_w_out"]).then_inc(S["ld_gw"], 16)
            sp.dma_start(temp[:, 0:1], A["L0_attn_attention_trace"].rearrange("h a b -> h (a b)")).then_inc(S["ld_gw"], 16)
            sp.dma_start(temp[:, 1:2], A["L0_attn_temperature_factor"].rearrange("h a b -> h (a b)")).then_inc(S["ld_gw"], 16)
            sp.dma_start(voidk[:, :], A["L0_attn_void_k"].rearrange("a h b d -> (a h b d)").rearrange("(p o) -> p o", o=1)).then_inc(S["ld_gw"], 16)
            vv_src = A["L0_attn_void_v"].rearrange("a h b d -> (a b) h d")
            sp.dma_start(voidv[:, :, 0:GD], vv_src.to_broadcast([P, GH, GD])).then_inc(S["ld_gw"], 16)
            sp.dma_start(bo, A["L0_attn_b_out"].rearrange("(a d) -> a d", a=1).to_broadcast([P, D])).then_inc(S["ld_gw"], 16)
            sp.dma_start(rot_base.rearrange("p a b c -> p (a b c)"), A["c_rot"]).then_inc(S["ld_tables"], 16)
            sp.dma_start(mask_f, A["c_mask"]).then_inc(S["ld_tables"], 16)
            sp.dma_start(w_raw[:, 0:QKV], A["L0_ffn_Wqkv"][0]).then_inc(S["ld_raw"], 16)
            hd = DH // 2
            for k, name in enumerate(("L0_ffn_q_scale", "L0_ffn_k_scale")):
                a = A[name].rearrange("(o l) d -> o l d", o=1)
                c = k * DH
                sp.dma_start(gains[:, :, c:c + DH], a.to_broadcast([P, DEPTH, DH])).then_inc(S["ld_vec"], 16)
                sp.dma_start(gains_sw[:, :, c:c + hd], a[:, :, hd:DH].to_broadcast([P, DEPTH, hd])).then_inc(S["ld_vec"], 16)
                sp.dma_start(gains_sw[:, :, c + hd:c + DH], a[:, :, 0:hd].to_broadcast([P, DEPTH, hd])).then_inc(S["ld_vec"], 16)
            vv = vec_all[:, :].rearrange("p (l v) -> p l v", v=NVEC)
            sp.wait_ge(S["vec_clear"], 1)
            with nc.allow_non_contiguous_dma(reason="small vectors"):
                def column(n, k, src):
                    sp.dma_start(vv[0:n, :, k:k + 1], src.rearrange("l (p o) -> p l o", o=1)).then_inc(S["ld_vec"], 16)

                column(P, 0, A["L0_ffn_ln_g"])
                column(P, 1, A["L0_ffn_ln_b"])
                for c, (c0, cn) in enumerate(FCH):
                    for half in range(2):
                        column(cn, 2 + 3 * half + c, A["L0_ffn_b1"][:, half * FI + c0:half * FI + c0 + cn])
                column(P, 8, A["L0_ffn_b2"])

            def load_wo(l):
                sp.dma_start(wo[:, :, :], A["L0_ffn_Wo"][l].rearrange("(c p) n -> p c n", p=P)).then_inc(S["ld_wo"], 16)

            def load_w1(l):
                sp.dma_start(w1[:, :], A["L0_ffn_W1"][l]).then_inc(S["ld_w1"], 16)

            def load_w2(l):
                sp.dma_start(w2[:, 0:2, :], A["L0_ffn_W2"][l][0:2 * P, :].rearrange("(c p) n -> p c n", p=P)).then_inc(S["ld_w2"], 16)
                sp.dma_start(w2[0:FCH[2][1], 2, :], A["L0_ffn_W2"][l][2 * P:FI, :]).then_inc(S["ld_w2"], 16)

            load_wo(0)
            load_w1(0)
            load_w2(0)
            sp.wait_ge(S["ld_raw"], 16)
            sp.dma_start(w_raw[:, QKV:2 * QKV], A["L0_ffn_Wqkv"][1]).then_inc(S["ld_raw"], 16)
            for l in range(1, DEPTH):
                c = (l + 1) % 2 * QKV
                sp.wait_ge(S["ld_raw"], 16 * (l + 1))
                sp.wait_ge(S["split_lo"], B * l)
                sp.dma_start(w_raw[:, c:c + QKV], A["L0_ffn_Wqkv"][(l + 1) % DEPTH]).then_inc(S["ld_raw"], 16)
                sp.wait_ge(S["f_y"], B * l)
                load_wo(l)
                sp.wait_ge(S["f_hg"], 3 * B * l)
                load_w1(l)
                sp.wait_ge(S["f_y2"], B * l)
                load_w2(l)
            o_t = out.rearrange("b (t p) d -> p (b t) d", p=P)
            for q in range(4):
                sp.wait_ge(S["o_add"], q + 1)
                sp.dma_start(o_t[:, 4 * q:4 * q + 4, :], xt3[:, 4 * q:4 * q + 4, :]).then_inc(S["st_out"], 16)
            sp.wait_ge(S["st_out"], 64)

        @block.gpsimd
        def _(pool):
            pool.memset(vec_all[:, :], 0.0).then_inc(S["vec_clear"], 1)
            pool.memset(mean_mat[:, :], 1.0 / D)
            pool.memset(one_half[:, :], 1.5)
            pool.memset(xT[:, :], 0.0)
            pool.memset(xs2[:, :], 0.0)
            pool.memset(gv[:, :, :, :], 0.0).then_inc(S["zeroed"], 1)
            pool.wait_ge(S["zeroed"], 1)
            pool.memset(gv[:, :, :, GD:GD + 1], 1.0)
            pool.memset(voidv[:, :, GD:GD + 1], 1.0).then_inc(S["ones_set"], 1)
            pool.wait_ge(S["ld_const"], 16 * 3)
            pool.wait_ge(S["ld_gw"], 16 * 7)
            gkz3 = gkz.rearrange("p (u k) -> p u k", k=NK)
            for u in range(2):
                last = pool.tensor_tensor(gkz3[:, u * GH:(u + 1) * GH, N], head_col[:, :],
                                          voidk[:, 0:1].to_broadcast([P, GH]), ALU.mult)
            last.then_inc(S["voidk_set"], 1)

            def spread_keys(b, h0):
                if h0 == 0:
                    pool.wait_ge(S["g_k"], b + 1)
                    wait(pool, "g_s", (b - 1) * GU)
                u = b & 1
                dst = gkz[:, bass.ds(u * (GH * NK) + h0 * NK, 4 * NK)].rearrange("p (h k) -> p h k", h=4)
                pool.tensor_tensor(
                    dst[:, :, 0:N], gk.unsqueeze(1).to_broadcast([P, 4, N]),
                    head_col[:, h0:h0 + 4].unsqueeze(2).to_broadcast([P, 4, N]), ALU.mult).then_inc(S["g_kz"], 1)

            for h0 in range(0, GH, 4):
                spread_keys(0, h0)

            def g_body(b, more=True):
                for c in range(GU):
                    j, cj = gunit(b, c, 1)
                    if glive(j):
                        pool.wait_ge(S["g_exp"], gdone(b, c, 1))
                        h0, t = cj // 2 * 2, cj % 2
                        wait(pool, "g_num", j - 1)
                        pool.tensor_copy(gpv[:, bass.ds((j & 1) * (TT * GH) + t * GH + h0, 2)], gp[:, cj % 4, :, N]).then_inc(S["g_void"], 1)
                    if 6 <= c < 10 and glive(b) and more:
                        spread_keys(b + 1, 4 * (c - 6))

            g_body(0)
            g_body(1)
            with pool.Fori(2, B - 1) as b:
                g_body(b)
            g_body(B - 1, more=False)
            g_body(B)

            pool.wait_ge(S["ld_tables"], 16 * 2)
            pool.wait_ge(S["ld_vec"], 16 * 15)
            rot3 = rot[:, :].rearrange("p (l k t n) -> p l k t n", l=DEPTH, k=2, t=TT)
            for l in range(DEPTH):
                for k, gain in enumerate((gains, gains_sw)):
                    last = pool.tensor_tensor(rot3[:, l, k], rot_base[:, k, :, :],
                                              gain[:, l, :].unsqueeze(1).to_broadcast([P, TT, 2 * DH]), ALU.mult)
            last.then_inc(S["rot_set"], 1)
            pool.wait_ge(S["g_res"], B)
            pool.wait_ge(S["g_void"], GU * B)
            pool.wait_ge(S["rot_set"], 1)
            pool.memset(kz[:, :, :, :, :], 0.0)
            pool.memset(pT0[:, :, :], 0.0)
            pool.memset(pT1[:, :, :], 0.0).then_inc(S["cleared"], 1)

            def body(i):
                for g in range(NG):
                    j, gj = unit(i, g, 3)
                    if live(j):
                        k = gj % 2
                        p2 = pr[:, k].rearrange("p h t k -> p (h t) k")
                        pool.wait_ge(S["inv_set"], done(i, g, 3))
                        pool.tensor_tensor(p2, p2, rinv[:, k, :].unsqueeze(2).to_broadcast([P, TT * HG, 2 * WIN]),
                                           ALU.mult).then_inc(S["pn_set"], 1)
                    j, gj = unit(i, g, 1)
                    if live(j):
                        k, n = gj % 2, done(i, g, 1)
                        pool.wait_ge(S["ssm_set"], n)
                        pool.wait_ge(S["guess_set"], n)
                        pool.tensor_tensor(newton[:, 0, :], guess[:, k, :], guess[:, k, :], ALU.mult).then_inc(S["nw1_set"], 1)
                        pool.wait_ge(S["nw1_set"], n)
                        pool.tensor_tensor(newton[:, 1, :], newton[:, 0, :], ssm[:, k, :], ALU.mult).then_inc(S["nw2_set"], 1)
                        pool.wait_ge(S["nw2_set"], n)
                        pool.tensor_tensor(newton[:, 2, :], newton[:, 1, :], one_half[:, :], ALU.add).then_inc(S["nw3_set"], 1)
                        pool.wait_ge(S["nw3_set"], n)
                        pool.tensor_tensor(rn[:, k, :], newton[:, 2, :], guess[:, k, :], ALU.mult).then_inc(S["rn_set"], 1)
                    if live(j):
                        k = gj % 2
                        pool.wait_ge(S["add_set"], done(i, g, 1))
                        pool.wait_ge(S["rn_set"], done(i, g, 1))
                        wait(pool, "tk_mm", done(i, g, 3))
                        for q in range(2):
                            dst, src = (a[:, k, :].rearrange("p (t u n) -> p t u n", t=TT, u=2)[:, :, q].rearrange("p t (h d) -> p t h d", d=DH)
                                        for a in (qn, t1))
                            norm = rn[:, k, :].rearrange("p (t u h) -> p t u h", t=TT, u=2)[:, :, q].unsqueeze(3)
                            pool.tensor_tensor(dst, src, norm.to_broadcast([P, TT, HG, DH]), ALU.mult).then_inc(S["qn_set"], 1)
                    if live(i):
                        k = g % 2
                        pool.wait_ge(S["t2_set"], done(i, g))
                        pool.tensor_tensor(t1[:, k, :], t1[:, k, :], t2, ALU.add).then_inc(S["add_set"], 1)
                    if g == 3 and live(i - 2):
                        f = i - 2
                        for c, (_, n) in enumerate(FCH):
                            pool.wait_ge(S["f_gate"], 3 * f + c + 1)
                            wait(pool, "f_y2", f)
                            pool.tensor_tensor(hT[0:n, c, :], hg[0:n, c, 0:N], hg[0:n, c, N:], ALU.mult).then_inc(S["f_h"], 1)
                    if g == 2 and live(i):
                        c0 = (((i >> 3) + 1) & 1) * QKV + (i & 7) * PIECE
                        pool.wait_ge(S["split_hi"], i + B + 1)
                        pool.tensor_tensor(wl_flat[:, bass.ds(c0, PIECE)], w_raw[:, bass.ds(c0, PIECE)],
                                           wh_flat[:, bass.ds(c0, PIECE)].bitcast(F32), ALU.subtract).then_inc(S["split_lo"], 1)

            sweep(pool, body)

        @block.scalar
        def _(act):
            act.preload_act_table_set(LN_EXP)
            def take_state(b):
                act.wait_ge(S["xn_t"], b + 1)
                act.activation(xT[:, b * (N + 1) + 1:(b + 1) * (N + 1)], PS[:, b % 4, b // 4 * N:(b // 4 + 1) * N], ACT.Copy).then_inc(S["state_set"], 1)

            def take_keys(b):
                act.wait_ge(S["g_k_mm"], b + 1)
                wait(act, "g_kz", 4 * b)
                act.activation(gk, PS[:, 7, 0:N], ACT.Copy).then_inc(S["g_k"], 1)

            for n, (a0, a1) in enumerate(LN_PARTS):
                act.wait_ge(S["ln_step"], 9 * n + 3)
                act.activation(sq_tok[:, a0 * D:a1 * D], xc_tok[:, a0 * D:a1 * D], ACT.Square).then_inc(S["ln_sq"], 1)
                act.wait_ge(S["ln_step"], 9 * n + 5)
                act.activation(stat[:, 1, a0:a1], stat[:, 3, a0:a1], ACT.Ln).then_inc(S["ln_guess"], 1)
                act.wait_ge(S["ln_guess"], 2 * n + 1)
                act.activation(stat[:, 0, a0:a1], stat[:, 1, a0:a1], ACT.Exp, scale=-0.5).then_inc(S["ln_guess"], 1)
                act.wait_ge(S["zeroed"], 1)
                for b in range(a0 // TT, a1 // TT):
                    take_state(b)
                if n == 0:
                    take_keys(0)

            def g_body(b, more=True):
                for c in range(GU):
                    if glive(b) and c == 0:
                        act.wait_ge(S["g_q_mm"], b + 1)
                        act.wait_ge(S["qscale_set"], 1)
                        act.activation(gq, PS[:, 7, 0:N], ACT.Copy, scale=qscale[:, 0:1]).then_inc(S["g_q"], 1)
                        wait(act, "g_v_mm", b)
                        act.activation(xg, state(slice(0, P), b, 0), ACT.Copy).then_inc(S["g_x"], 1)
                    if glive(b) and c == 3:
                        act.wait_ge(S["g_v_mm"], b + 1)
                        wait(act, "g_o", b * GU)
                        if isinstance(b, int) and b == 0:
                            act.wait_ge(S["ones_set"], 1)
                        act.activation(gv[:, :, :, 0:GD], PS[:, 7, 0:N].rearrange("p (t h d) -> p t h d", t=TT, h=GH), ACT.Copy).then_inc(S["g_v"], 1)
                    j, cj = gunit(b, c, 1)
                    if glive(j):
                        act.wait_ge(S["g_sub"], gdone(b, c, 1))
                        act.activation(gp[:, cj % 4], gp[:, cj % 4], ACT.Exp).then_inc(S["g_exp"], 1)
                    j, cj = gunit(b, c, 2)
                    if glive(j):
                        act.wait_ge(S["g_pt"], gdone(b, c, 2))
                        wait(act, "g_o", gdone(b, c, 4))
                        act.activation(gpT[:, cj % 2], PS[:, 4, :], ACT.Copy).then_inc(S["g_pT"], 1)
                    j, cj = gunit(b, c, 3)
                    if glive(j) and cj % 4 == 3:
                        n = cj // 4
                        act.wait_ge(S["g_o"], gdone(b, c, 3))
                        wait(act, "g_tok", 4 * j + n - 1)
                        act.activation(goT[:, n % 2, :], PS[:, 5, 0:N], ACT.Copy).then_inc(S["g_oT"], 1)
                    if c == 10 and glive(b - 1):
                        act.wait_ge(S["g_attT_mm"], b)
                        act.activation(gattT, PS[:, 7, 0:N], ACT.Copy).then_inc(S["g_attT"], 1)
                    if c == 5 and glive(b) and more:
                        take_keys(b + 1)
                    if c == 13 and glive(b):
                        act.wait_ge(S["ld_raw"], 16)
                        act.activation(wh_flat[:, bass.ds(b * PIECE, PIECE)], w_raw[:, bass.ds(b * PIECE, PIECE)], ACT.Copy).then_inc(S["split_hi"], 1)

            g_body(0)
            g_body(1)
            with act.Fori(2, B - 1) as b:
                g_body(b)
            g_body(B - 1, more=False)
            g_body(B)

            def lead_state(i):
                b = i & (B - 1)
                act.wait_ge(S["state_set"], i + 1)
                act.activation(xh[lower, :], state(lower, b, 0), ACT.Copy)
                act.activation(xh[upper, :], state(upper, b, 1), ACT.Copy).then_inc(S["xh_set"], 1)

            lead_state(0)
            act.wait_ge(S["cleared"], 1)

            def body(i, parity):
                for g in range(NG):
                    if live(i):
                        wait(act, "ss_set", done(i, g, 1))
                        for t in range(TT):
                            act.wait_ge(S["s_qk"], TT * (done(i, g) - 1) + t + 1)
                            act.activation(sq[:, t * 512:(t + 1) * 512], PS[:, t, :], ACT.Square).then_inc(S["sq_set"], 1)
                        act.wait_ge(S["s_v"], done(i, g))
                        wait(act, "o_mm", done(i, g, 8))
                        act.activation(v[:, parity, g].rearrange("p t n -> p (t n)"), PS[:, 2, :], ACT.Copy).then_inc(S["v_set"], 1)
                    j, gj = unit(i, g, 3)
                    if live(j):
                        k = gj % 2
                        act.wait_ge(S["sub_set"], done(i, g, 3))
                        act.activation(pr[:, k].rearrange("p h t k -> p (h t k)"), pr[:, k].rearrange("p h t k -> p (h t k)"),
                                       ACT.Exp).then_inc(S["exp_set"], 1)
                    j, gj = unit(i, g, 2)
                    if live(j):
                        k = gj % 2
                        act.wait_ge(S["tq_mm"], done(i, g, 2))
                        wait(act, "s_mm", done(i, g, 4))
                        act.activation(qT[:, k].rearrange("p a n -> p (a n)"), PS[:, 3, :], ACT.Copy).then_inc(S["qT_set"], 1)
                        act.wait_ge(S["tk_mm"], done(i, g, 2))
                        kt = PS[:, 4, :].rearrange("p (a n) -> p a n", a=PR)
                        act.activation(kz[0:DH, k, :, 0, WIN:], kt[0:DH], ACT.Copy)
                        act.activation(kz[DH:P, k, :, 1, WIN:], kt[DH:P], ACT.Copy).then_inc(S["kz_set"], 1)
                    j, gj = unit(i, g, 4)
                    if live(j):
                        act.wait_ge(S["o_mm"], done(i, g, 4))
                        if gj == 0:
                            wait(act, "f_y", j - 1)
                        dst = oT[:, bass.ds(j & 1, 1), 2 * gj:2 * gj + 2, :].rearrange("p u c n -> p (u c n)")
                        act.activation(dst, PS[:, 2, :], ACT.Copy).then_inc(S["o_set"], 1)
                    j, gj = unit(i, g, 1)
                    if live(j):
                        k, n = gj % 2, done(i, g, 1)
                        act.wait_ge(S["ssm_set"], n)
                        act.activation(ssl[:, k, :], ssm[:, k, :], ACT.Ln, scale=-2.0).then_inc(S["ssl_set"], 1)
                        act.wait_ge(S["ssl_set"], n)
                        wait(act, "rn_set", done(i, g, 3))
                        act.activation(guess[:, k, :], ssl[:, k, :], ACT.Exp, scale=-0.5).then_inc(S["guess_set"], 1)
                    if g == 1 and live(i):
                        c0 = (((i >> 3) + 1) & 1) * QKV + (i & 7) * PIECE
                        act.wait_ge(S["ld_raw"], 16 * ((i >> 3) + 2))
                        act.activation(wh_flat[:, bass.ds(c0, PIECE)], w_raw[:, bass.ds(c0, PIECE)], ACT.Copy).then_inc(S["split_hi"], 1)
                    if g == 1 and live(i - 2):
                        act.wait_ge(S["f_ve"], i - 1)
                        act.activation(rs, var[:, :], ACT.Ln).then_inc(S["f_ln"], 1)
                        act.wait_ge(S["f_ln"], i - 1)
                        act.activation(rs, rs, ACT.Exp, scale=-0.5).then_inc(S["f_guess"], 1)
                    if g == 3 and live(i) and (not isinstance(i, int) or i + 1 < ITERS):
                        act.wait_ge(S["s_v"], done(i, 3))
                        lead_state(i + 1)
                    if g == 0 and live(i - 2):
                        act.wait_ge(S["f_xc"], i - 1)
                        act.activation(var[:, :], xc, ACT.Square).then_inc(S["f_sq"], 1)
                    if g == 3 and live(i - 2):
                        for c, (_, n) in enumerate(FCH):
                            act.wait_ge(S["f_hgc"], 3 * (i - 2) + c + 1)
                            act.activation(hg[0:n, c, N:], hg[0:n, c, N:], ACT.Gelu, bias=vec[0:n, 5 + c:6 + c]).then_inc(S["f_gate"], 1)
                        act.preload_act_table_set(LN_EXP)
                    j, gj = unit(i, g, 3)
                    if live(j):
                        act.wait_ge(S["pt_mm"], done(i, g, 3))
                        wait(act, "o_mm", done(i, g, 4))
                        src = PS[:, 6, :].rearrange("p (h n) -> p h n", h=HG)
                        for t in range(TT):
                            dst = (pT0, pT1)[t]
                            for w in range(NW):
                                k0, s0, q0 = (w - 1) * WIN, t * 2 * WIN, w * WIN
                                if w == 0:
                                    moves = [(s0 + WIN, WIN, dst, 0, 0)] + [(s0, WIN, pT0, P - WIN, P)] * t
                                elif k0 % (2 * WIN) == 0:
                                    moves = [(s0, 2 * WIN, dst, k0, q0)]
                                else:
                                    moves = [(s0, WIN, dst, k0, q0), (s0 + WIN, WIN, dst, k0 + WIN, q0)]
                                for r, n, to, d0, c0 in moves:
                                    last = act.activation(to[d0:d0 + n, :, c0:c0 + WIN], src[r:r + n, :, q0:q0 + WIN], ACT.Copy)
                        last.then_inc(S["pT_set"], 1)

            sweep_pairs(act, body)

        @block.vector
        def _(dve):
            x3 = x_tok[:, :].rearrange("p (a d) -> p a d", d=D)
            xc3 = xc_tok.rearrange("p (a d) -> p a d", d=D)
            for n, (a0, a1) in enumerate(LN_PARTS):
                tiles = slice(a0, a1)
                x, xc_part, shape = x3[:, tiles], xc3[:, tiles], [P, a1 - a0, D]
                dve.wait_ge(S[("ld_x_first", "ld_x_rest")[n]], 16)
                dve.tensor_reduce(stat[:, 0, tiles], x, AX_X, ALU.add).then_inc(S["ln_step"], 1)
                dve.wait_ge(S["ln_step"], 9 * n + 1)
                dve.tensor_scalar(stat[:, 1, tiles], stat[:, 0, tiles], 1.0 / D, None, ALU.mult).then_inc(S["ln_step"], 1)
                dve.wait_ge(S["ln_step"], 9 * n + 2)
                dve.tensor_tensor(xc_part, x, stat[:, 1, tiles].unsqueeze(2).to_broadcast(shape), ALU.subtract).then_inc(S["ln_step"], 1)
                dve.wait_ge(S["ln_sq"], n + 1)
                dve.tensor_reduce(stat[:, 2, tiles], sq_tok[:, a0 * D:a1 * D].rearrange("p (a d) -> p a d", d=D), AX_X, ALU.add).then_inc(S["ln_step"], 1)
                dve.wait_ge(S["ln_step"], 9 * n + 4)
                dve.tensor_scalar(stat[:, 3, tiles], stat[:, 2, tiles], 1.0 / D, 1e-5, ALU.mult, ALU.add).then_inc(S["ln_step"], 1)
                dve.wait_ge(S["ln_guess"], 2 * (n + 1))
                dve.scalar_tensor_tensor(out=stat[:, 1, tiles], in0=stat[:, 0, tiles], scalar=-0.5, in1=stat[:, 0, tiles], op0=ALU.mult, op1=ALU.mult).then_inc(S["ln_step"], 1)
                dve.wait_ge(S["ln_step"], 9 * n + 6)
                dve.tensor_tensor(stat[:, 2, tiles], stat[:, 1, tiles], stat[:, 3, tiles], ALU.mult).then_inc(S["ln_step"], 1)
                dve.wait_ge(S["ln_step"], 9 * n + 7)
                dve.scalar_tensor_tensor(out=stat[:, 1, tiles], in0=stat[:, 2, tiles], scalar=1.5, in1=stat[:, 0, tiles], op0=ALU.add, op1=ALU.mult).then_inc(S["ln_step"], 1)
                dve.wait_ge(S["ln_step"], 9 * n + 8)
                dve.tensor_tensor(xc_part, xc_part, stat[:, 1, tiles].unsqueeze(2).to_broadcast(shape), ALU.mult).then_inc(S["ln_step"], 1)
                if n == 0:
                    dve.wait_ge(S["ld_gw"], 16 * 7)
                    dve.tensor_scalar(temp[:, 3:4], temp[:, 0:1], -1.0, None, ALU.mult).then_inc(S["temp_set"], 1)
                    dve.wait_ge(S["temp_set"], 1)
                    dve.tensor_tensor(temp[:, 2:3], temp[:, 0:1], temp[:, 3:4], ALU.max).then_inc(S["temp_set"], 1)
                    dve.wait_ge(S["temp_set"], 2)
                    dve.tensor_tensor(temp[:, 3:4], temp[:, 2:3], temp[:, 1:2], ALU.mult).then_inc(S["temp_set"], 1)
                    dve.wait_ge(S["temp_set"], 3)
                    dve.tensor_scalar(temp[:, 4:5], temp[:, 3:4], 1.0, 1.0, ALU.add, ALU.max).then_inc(S["temp_set"], 1)
                    dve.wait_ge(S["temp_set"], 4)
                    dve.reciprocal(temp[:, 5:6], temp[:, 4:5]).then_inc(S["temp_set"], 1)
                    dve.wait_ge(S["spread_mm"], 1)
                    dve.tensor_scalar(qscale[:, :], PS[:, 6, 0:1], float(D) ** -0.5, None, ALU.mult).then_inc(S["qscale_set"], 1)
            dve.wait_ge(S["ld_const"], 16 * 3)
            dve.wait_ge(S["ld_tables"], 16 * 2)
            dve.tensor_copy(ident_bf[:, :], ident[:, :])
            dve.tensor_copy(mask_bf[:, :], mask_f).then_inc(S["mask_set"], 1)
            def g_body(b):
                for c in range(GU):
                    if glive(b):
                        bank = 2 * (c % 2)
                        dve.wait_ge(S["g_s"], gdone(b, c))
                        wait(dve, "g_sub", gdone(b, c, 2))
                        dve.tensor_reduce(gmx[:, c % 2, :], PS[:, bank:bank + 2, 0:NK], AX_X, ALU.max).then_inc(S["g_mx"], 1)
                        dve.wait_ge(S["g_mx"], gdone(b, c))
                        wait(dve, "g_pt", gdone(b, c, 4))
                        wait(dve, "g_void", gdone(b, c, 4))
                        dve.tensor_tensor(gp[:, c % 4], PS[:, bank:bank + 2, 0:NK],
                                          gmx[:, c % 2, :].unsqueeze(2).to_broadcast([P, 2, NK]), ALU.subtract).then_inc(S["g_sub"], 1)
                    j, cj = gunit(b, c, 6)
                    if glive(j) and cj % 4 == 3:
                        n = cj // 4
                        dve.wait_ge(S["g_tok"], 4 * j + n + 1)
                        if n == 0:
                            wait(dve, "g_acc", j)
                        dve.tensor_copy(gtok.rearrange("p (t h) d -> p t h d", t=TT)[:, :, 4 * n:4 * n + 4, :],
                                        PS[:, 6, 0:N].rearrange("p (t h d) -> p t h d", t=TT, h=4)[:, :, :, 0:GD + 1]).then_inc(S["g_tokev"], 1)
                    f = b - 1
                    if c == 5 and glive(f):
                        dve.wait_ge(S["g_void"], b * GU)
                        void = gpv[:, bass.ds((f & 1) * (TT * GH), TT * GH)]
                        dve.tensor_tensor(
                            gacc.rearrange("p (t h) d -> p t h d", t=TT),
                            void.rearrange("p (t h) -> p t h", t=TT).unsqueeze(3).to_broadcast([P, TT, GH, GD + 1]),
                            voidv[:, :, :].unsqueeze(1).to_broadcast([P, TT, GH, GD + 1]), ALU.mult).then_inc(S["g_num"], 1)
                    if c == 6 and glive(f):
                        dve.wait_ge(S["g_num"], b)
                        dve.wait_ge(S["g_tokev"], 4 * b)
                        dve.tensor_tensor(gacc[:, :, :], gacc[:, :, :], gtok[:, :, :], ALU.add).then_inc(S["g_acc"], 1)
                    if c == 7 and glive(f):
                        dve.wait_ge(S["g_acc"], b)
                        dve.reciprocal(gden, gacc[:, :, GD]).then_inc(S["g_den"], 1)
                    if c == 8 and glive(f):
                        dve.wait_ge(S["g_den"], b)
                        wait(dve, "g_attT_mm", b - 1)
                        dve.tensor_tensor(gatt[:, :, :].rearrange("p t (h d) -> p (t h) d", h=GH), gacc[:, :, 0:GD],
                                          gden.unsqueeze(2).to_broadcast([P, TT * GH, GD]), ALU.mult).then_inc(S["g_att"], 1)
                    if c == 12 and glive(f):
                        rows = x_tok[:, bass.ds((b - 1) * (TT * D), TT * D)]
                        dve.wait_ge(S["g_bias"], b)
                        dve.wait_ge(S["g_y"], b)
                        dve.tensor_tensor(rows, rows, PS[:, 7, 0:N], ALU.add).then_inc(S["g_res"], 1)
                    if c == 13 and glive(b):
                        rows = x_tok[:, bass.ds(b * (TT * D), TT * D)].rearrange("p (t d) -> p t d", t=TT)
                        dve.tensor_tensor(rows, rows, bo.unsqueeze(1).to_broadcast([P, TT, D]), ALU.add).then_inc(S["g_bias"], 1)
                    if c == 14 and glive(b):
                        dve.wait_ge(S["split_hi"], b + 1)
                        dve.tensor_tensor(wl_flat[:, bass.ds(b * PIECE, PIECE)], w_raw[:, bass.ds(b * PIECE, PIECE)],
                                          wh_flat[:, bass.ds(b * PIECE, PIECE)].bitcast(F32), ALU.subtract).then_inc(S["split_lo"], 1)

            gsweep(dve, g_body)

            def trail_state(i):
                b = i & (B - 1)
                dve.wait_ge(S["xh_set"], i + 1)
                dve.tensor_tensor(xl[lower, :], state(lower, b, 0), xh[lower, :].bitcast(F32), ALU.subtract)
                dve.tensor_tensor(xl[upper, :], state(upper, b, 1), xh[upper, :].bitcast(F32), ALU.subtract).then_inc(S["xl_set"], 1)

            trail_state(0)
            dve.wait_ge(S["rot_set"], 1)
            ROT = TT * 2 * DH

            def inverse_deviations(f):
                dve.wait_ge(S["f_guess"], f + 1)
                wait(dve, "f_hg", 3 * f)
                dve.scalar_tensor_tensor(out=xn[:, :], in0=rs, scalar=-0.5, in1=rs, op0=ALU.mult, op1=ALU.mult).then_inc(S["f_n1"], 1)
                dve.wait_ge(S["f_n1"], f + 1)
                dve.tensor_tensor(var[:, :], xn[:, :], var[:, :], ALU.mult).then_inc(S["f_n2"], 1)
                dve.wait_ge(S["f_n2"], f + 1)
                dve.scalar_tensor_tensor(out=rs, in0=var[:, :], scalar=1.5, in1=rs, op0=ALU.add, op1=ALU.mult).then_inc(S["f_rs"], 1)

            def normalise(f):
                dve.wait_ge(S["f_rs"], f + 1)
                dve.tensor_tensor(var[:, :], xc, rs, ALU.mult).then_inc(S["f_xr"], 1)
                dve.wait_ge(S["f_xr"], f + 1)
                dve.wait_ge(S["f_vec"], f + 1)
                dve.tensor_scalar(xn[:, :], var[:, :], vec[:, 0:1], vec[:, 1:2], ALU.mult, ALU.add).then_inc(S["f_xn"], 1)

            def take_hidden(f, c):
                n = FCH[c][1]
                dve.wait_ge(S["f_hg"], 3 * f + c + 1)
                wait(dve, "f_h", 3 * f)
                dve.tensor_scalar(hg[0:n, c, 0:N], PS[0:n, 7, 0:N], vec[0:n, 2 + c:3 + c], None, ALU.add)
                dve.tensor_copy(hg[0:n, c, N:], PS[0:n, 7, N:]).then_inc(S["f_hgc"], 1)

            def body(i):
                for g in range(NG):
                    if g == 1 and live(i - 2):
                        dve.wait_ge(S["f_var"], i - 1)
                        dve.tensor_scalar(var[:, :], PS[:, 7, N:2 * N], 1e-5, None, ALU.add).then_inc(S["f_ve"], 1)
                    if g == 2 and live(i - 3):
                        f = i - 3
                        dve.wait_ge(S["f_y2"], f + 1)
                        new = xT[:, bass.ds((f & 7) * (N + 1) + 1, N)]
                        dve.scalar_tensor_tensor(out=new, in0=PS[:, 7, 0:N], scalar=vec[:, 8:9], in1=x1[:, bass.ds(f & 1, 1)].squeeze(1),
                                                 op0=ALU.add, op1=ALU.add).then_inc(S["state_set"], 1)
                    if g == 2 and live(i - 2):
                        if live(i - 3):
                            dve.wait_ge(S["state_set"], B + i - 2)
                            dve.wait_ge(S["f_gate"], 3 * (i - 2))
                        dve.tensor_copy(vec[:, :], vec_all[:, bass.ds(layer_of(i - 2) * NVEC, NVEC)]).then_inc(S["f_vec"], 1)
                        normalise(i - 2)
                    if g == 3 and live(i - 2):
                        take_hidden(i - 2, 1)
                    if g == 0 and live(i - 2):
                        f = i - 2
                        dve.wait_ge(S["f_y"], f + 1)
                        dve.wait_ge(S["state_set"], B - 1 + f)
                        own = bass.ds(f & 1, 1)
                        dve.tensor_tensor(x1[:, own].squeeze(1), PS[:, 7, N:2 * N],
                                          xT[:, bass.ds((f & 7) * (N + 1) + 1, N)], ALU.add).then_inc(S["f_x1"], 1)
                        dve.wait_ge(S["f_x1"], f + 1)
                        wait(dve, "f_xc", f)
                        dve.tensor_scalar(xs2[lower, :], x1[lower, own].squeeze(1), 1.0, None, ALU.mult)
                        dve.tensor_scalar(xs2[upper, 1:], x1[upper, own, 0:N - 1].squeeze(1), 1.0, None, ALU.mult).then_inc(S["f_xs2"], 1)
                    k = g % 2
                    if live(i):
                        wait(dve, "qn_set", 2 * done(i, g, 2))
                        qk4 = PS[:, 0:2, :].rearrange("p t (q h d) -> p (t q) h d", q=2, h=HG)
                        layer = layer_of(i)
                        cos = rot[:, bass.ds(layer * (2 * ROT), ROT)].rearrange("p (u d) -> p u d", d=DH)
                        sin = rot[:, bass.ds(layer * (2 * ROT) + ROT, ROT)].rearrange("p (u d) -> p u d", d=DH)
                        t4 = t1[:, k].rearrange("p (u h d) -> p u h d", u=4, h=HG)
                        for t in range(TT):
                            dve.wait_ge(S["sq_set"], TT * (done(i, g) - 1) + t + 1)
                            u2 = slice(2 * t, 2 * t + 2)
                            dve.tensor_tensor(t4[:, u2], qk4[:, u2], cos[:, u2].unsqueeze(2).to_broadcast([P, 2, HG, DH]), ALU.mult)
                    j, gj = unit(i, g, 3)
                    if live(j):
                        kj = gj % 2
                        dve.wait_ge(S["exp_set"], done(i, g, 3))
                        dve.tensor_reduce(rsum[:, kj, :], pr[:, kj].rearrange("p h t k -> p (h t) k"), AX_X, ALU.add).then_inc(S["sum_set"], 1)
                        dve.wait_ge(S["sum_set"], done(i, g, 3))
                        dve.reciprocal(rinv[:, kj, :], rsum[:, kj, :]).then_inc(S["inv_set"], 1)
                    if live(i):
                        hd = DH // 2
                        wait(dve, "add_set", done(i, g, 1))
                        o4 = t2.rearrange("p (u h d) -> p u h d", u=4, h=HG)
                        for lo, hi in ((0, hd), (hd, 0)):
                            last = dve.tensor_tensor(o4[:, :, :, lo:lo + hd], qk4[:, :, :, hi:hi + hd],
                                                     sin[:, :, lo:lo + hd].unsqueeze(2).to_broadcast([P, 4, HG, hd]), ALU.mult)
                        last.then_inc(S["t2_set"], 1)
                    if g == 3 and live(i - 2):
                        take_hidden(i - 2, 2)
                    if g == 2 and live(i - 2):
                        take_hidden(i - 2, 0)
                    if g == 0 and live(i - 2):
                        dve.wait_ge(S["f_mean"], i - 1)
                        dve.wait_ge(S["f_xs2"], i - 1)
                        dve.tensor_tensor(xc, xs2[:, :], PS[:, 7, 0:N], ALU.subtract).then_inc(S["f_xc"], 1)
                    if live(i):
                        wait(dve, "ssm_set", done(i, g, 1))
                        dve.tensor_reduce(ss[:, :], sq.rearrange("p (u d) -> p u d", d=DH), AX_X, ALU.add).then_inc(S["ss_set"], 1)
                        dve.wait_ge(S["ss_set"], done(i, g))
                        wait(dve, "nw2_set", done(i, g, 2))
                        dve.tensor_scalar(ssm[:, k, :], ss[:, :], 1e-24, -0.5 * NORM_G ** 2, ALU.max, ALU.mult).then_inc(S["ssm_set"], 1)
                    if g == 3 and live(i) and (not isinstance(i, int) or i + 1 < ITERS):
                        trail_state(i + 1)
                    j, gj = unit(i, g, 2)
                    if live(j):
                        k = gj % 2
                        s3 = PS[:, 5, :].rearrange("p (u k) -> p u k", k=2 * WIN)
                        dve.wait_ge(S["s_mm"], done(i, g, 2))
                        dve.tensor_reduce(rmx[:, k, :], s3, AX_X, ALU.max).then_inc(S["mx_set"], 1)
                        dve.wait_ge(S["mx_set"], done(i, g, 2))
                        wait(dve, "pt_mm", done(i, g, 4))
                        dve.tensor_tensor(pr[:, k].rearrange("p h t k -> p (h t) k"), s3,
                                          rmx[:, k, :].unsqueeze(2).to_broadcast([P, TT * HG, 2 * WIN]), ALU.subtract).then_inc(S["sub_set"], 1)
                    if g == 1 and live(i - 2):
                        inverse_deviations(i - 2)

            sweep(dve, body)
            for q in range(4):
                dve.wait_ge(S["o_t"], q + 1)
                rows = x_tok[:, 4 * q * D:4 * (q + 1) * D]
                dve.tensor_tensor(rows, rows, PS[:, q, :], ALU.add).then_inc(S["o_add"], 1)

        @block.tensor
        def _(pe):
            pe.wait_ge(S["ld_const"], 16 * 3)
            misc = PS[:, 7, 0:N]

            def g_keys(b):
                pe.matmul(misc, wg[:, D:2 * D], state(slice(0, P), b, 0), start=True, stop=True).then_inc(S["g_k_mm"], 1)

            for n, (a0, a1) in enumerate(LN_PARTS):
                pe.wait_ge(S["ln_step"], 9 * (n + 1))
                for b in range(a0 // TT, a1 // TT):
                    wait(pe, "state_set", b - 3)
                    for t in range(TT):
                        c, c0 = (b * TT + t) * D, b // 4 * N + t * P
                        last = pe.transpose(PS[:, b % 4, c0:c0 + P], xc_tok[:, c:c + D], ident[:, :])
                    last.then_inc(S["xn_t"], 1)
                if n == 0:
                    pe.wait_ge(S["state_set"], 1)
                    pe.wait_ge(S["ld_gw"], 16 * 7)
                    g_keys(0)
                    pe.wait_ge(S["temp_set"], 5)
                    pe.matmul(PS[:, 6, 0:1], spread, temp[:, 5:6], start=True, stop=True).then_inc(S["spread_mm"], 1)
            pe.wait_ge(S["state_set"], B)
            pe.wait_ge(S["qscale_set"], 1)

            def g_body(b, more=True):
                for c in range(GU):
                    if glive(b) and c == 0:
                        wait(pe, "g_k", b + 1)
                        wait(pe, "g_res", b - 1)
                        pe.matmul(misc, wg[:, 0:D], state(slice(0, P), b, 0), start=True, stop=True).then_inc(S["g_q_mm"], 1)
                        pe.wait_ge(S["g_q"], b + 1)
                        pe.wait_ge(S["voidk_set"], 1)
                    if glive(b):
                        if c % 4 == 0:
                            pe.wait_ge(S["g_kz"], 4 * b + c // 4 + 1)
                        wait(pe, "g_sub", gdone(b, c, 2))
                        for e in range(2):
                            h = c // 2 * 2 + e
                            keys = gkz[:, bass.ds((b & 1) * (GH * NK) + h * NK, NK)]
                            t = c % 2
                            last = pe.matmul(PS[:, 2 * (c % 2) + e, 0:NK], gq[:, t * P:(t + 1) * P], keys, start=True, stop=True)
                        last.then_inc(S["g_s"], 1)
                    if glive(b) and c == 1:
                        pe.wait_ge(S["g_x"], b + 1)
                        for t in range(TT):
                            last = pe.matmul(PS[:, 7, t * P:(t + 1) * P], xg[:, t * P:(t + 1) * P], wg[:, 2 * D:3 * D], start=True, stop=True)
                        last.then_inc(S["g_v_mm"], 1)
                    j, cj = gunit(b, c, 2)
                    if glive(j):
                        pe.wait_ge(S["g_exp"], gdone(b, c, 2))
                        wait(pe, "g_pT", gdone(b, c, 3))
                        for e in range(2):
                            for kt in range(TT):
                                n = 2 * e + kt
                                last = pe.transpose(PS[:, 4, n * P:(n + 1) * P], gp[:, cj % 4, e, kt * P:(kt + 1) * P], ident[:, :])
                        last.then_inc(S["g_pt"], 1)
                    j, cj = gunit(b, c, 3)
                    if glive(j):
                        n, pair, t = cj // 4, cj // 2 % 2, cj % 2
                        pe.wait_ge(S["g_pT"], gdone(b, c, 3))
                        if cj == 0:
                            pe.wait_ge(S["g_v"], j + 1)
                        if cj % 4 == 0:
                            wait(pe, "g_oT", 4 * j + n)
                        for kt in range(TT):
                            for e in range(2):
                                h = cj // 2 * 2 + e
                                r = 32 * (2 * pair + e)
                                last = pe.matmul(PS[r:r + 32, 5, t * P:(t + 1) * P], gv[:, kt, h, :],
                                                 gpT[:, cj % 2, (2 * e + kt) * P:(2 * e + kt + 1) * P],
                                                 start=(kt == 0), stop=(kt == 1), skip_group_check=True)
                        last.then_inc(S["g_o"], 1)
                    j, cj = gunit(b, c, 5)
                    if glive(j) and cj % 4 == 3:
                        n = cj // 4
                        pe.wait_ge(S["g_oT"], 4 * j + n + 1)
                        wait(pe, "g_tokev", 4 * j + n)
                        for t in range(TT):
                            last = pe.transpose(PS[:, 6, t * P:(t + 1) * P], goT[:, n % 2, t * P:(t + 1) * P], ident[:, :])
                        last.then_inc(S["g_tok"], 1)
                    if c == 5 and glive(b) and more:
                        wait(pe, "g_res", b - 1)
                        pe.wait_ge(S["g_v"], b + 1)
                        g_keys(b + 1)
                    if c == 10 and glive(b - 1):
                        pe.wait_ge(S["g_att"], b)
                        if glive(b):
                            pe.wait_ge(S["g_v"], b + 1)
                            if more:
                                pe.wait_ge(S["g_k"], b + 2)
                        for t in range(TT):
                            last = pe.transpose(PS[:, 7, t * P:(t + 1) * P], gatt[:, t, :], ident[:, :])
                        last.then_inc(S["g_attT_mm"], 1)
                    if c == 11 and glive(b - 1):
                        pe.wait_ge(S["g_attT"], b)
                        for t in range(TT):
                            last = pe.matmul(PS[:, 7, t * P:(t + 1) * P], gattT[:, t * P:(t + 1) * P], wgo, start=True, stop=True)
                        last.then_inc(S["g_y"], 1)

            g_body(0)
            g_body(1)
            with pe.Fori(2, B - 1) as b:
                g_body(b)
            g_body(B - 1, more=False)
            g_body(B)

            pe.wait_ge(S["mask_set"], 1)

            def body(i, parity):
                for g in range(NG):
                    if live(i):
                        if g == 0:
                            pe.wait_ge(S["xl_set"], i + 1)
                            pe.wait_ge(S["split_lo"], B + (i >> 3) * B)
                        if isinstance(i, int) and i == 0 and g == 0:
                            pe.wait_ge(S["g_res"], B)
                            pe.wait_ge(S["g_void"], GU * B)
                        u = (i >> 3) & 1
                        parts = ((xh, wh), (xh, wl), (xl, wh))
                        wait(pe, "t2_set", done(i, g, 1))
                        for t in range(TT):
                            for n, (x, w) in enumerate(parts):
                                last = pe.matmul(PS[:, t, :], x[:, t * P:(t + 1) * P], w[:, bass.ds(u, 1), 0:2, g * GC:(g + 1) * GC].squeeze(1),
                                                 start=(n == 0), stop=(n == 2))
                            last.then_inc(S["s_qk"], 1)
                        wait(pe, "v_set", done(i, g, 1))
                        wait(pe, "o_set", done(i, g, 5))
                        for t in range(TT):
                            for n, (x, w) in enumerate(parts):
                                last = pe.matmul(PS[:, 2, t * GC:(t + 1) * GC], x[:, t * P:(t + 1) * P], w[:, bass.ds(u, 1), 2, g * GC:(g + 1) * GC].squeeze(1),
                                                 start=(n == 0), stop=(n == 2))
                        last.then_inc(S["s_v"], 1)
                    j, gj = unit(i, g, 2)
                    if live(j):
                        k = gj % 2
                        for q, (free, mm) in enumerate((("qT_set", "tq_mm"), ("kz_set", "tk_mm"))):
                            pe.wait_ge(S["qn_set"], 2 * done(i, g, 2) - 1 + q)
                            wait(pe, free, done(i, g, 3))
                            for a in range(PR):
                                for t in range(TT):
                                    c = (t * 2 + q) * GC + a * P
                                    last = pe.transpose(PS[:, 3 + q, a * N + t * P:a * N + (t + 1) * P], qn[:, k, c:c + P], ident[:, :])
                            last.then_inc(S[mm], 1)
                    j, gj = unit(i, g, 4)
                    if live(j):
                        pe.wait_ge(S["pT_set"], done(i, g, 4))
                        if live(i):
                            pe.wait_ge(S["v_set"], done(i, g))
                        wait(pe, "o_set", done(i, g, 5))
                        for a in range(PR):
                            for t, q0, probs in ((0, 0, pT0), (1, P, pT1)):
                                for e in range(2):
                                    h = 2 * a + e
                                    n = probs.shape[2]
                                    last = pe.matmul(PS[e * DH:(e + 1) * DH, 2, a * N + q0:a * N + q0 + n],
                                                     v[:, 1 - parity, gj, t, h * DH:(h + 1) * DH], probs[:, h, :],
                                                     start=(t == 0), stop=(t == 1), skip_group_check=True)
                        last.then_inc(S["o_mm"], 1)
                    if g == 2 and live(i - 2):
                        if live(i - 3):
                            pe.wait_ge(S["state_set"], B + i - 2)
                        hidden(i - 2, 0)
                    if g == 3 and live(i - 2):
                        hidden(i - 2, 2)
                    if g == 0 and live(i - 2):
                        pe.wait_ge(S["f_xs2"], i - 1)
                        pe.matmul(PS[:, 7, 0:N], mean_mat[:, :], xs2[:, :], start=True, stop=True).then_inc(S["f_mean"], 1)
                    j, gj = unit(i, g, 2)
                    if live(j):
                        k = gj % 2
                        pe.wait_ge(S["qT_set"], done(i, g, 2))
                        pe.wait_ge(S["kz_set"], done(i, g, 2))
                        wait(pe, "sub_set", done(i, g, 3))
                        scores = PS[:, 5, :].rearrange("p (h t k) -> p h t k", h=HG, t=TT)
                        pe.matmul(PS[:, 5, :], ident_bf[:, :], mask_bf[:, :], start=True, stop=False, skip_group_check=True)
                        for t in range(TT):
                            for a in range(PR):
                                for w in range(NW):
                                    q0, k0 = t * P + w * WIN, (t * NW + w) * WIN
                                    last = pe.matmul(scores[w * WIN:(w + 1) * WIN, 2 * a:2 * a + 2, t, :], qT[:, k, a, q0:q0 + WIN],
                                                     kz[:, k, a, :, k0:k0 + 2 * WIN], start=False, stop=True, skip_group_check=True)
                        last.then_inc(S["s_mm"], 1)
                    j, gj = unit(i, g, 3)
                    if live(j):
                        k = gj % 2
                        pe.wait_ge(S["pn_set"], done(i, g, 3))
                        wait(pe, "pT_set", done(i, g, 4))
                        for h in range(HG):
                            last = pe.transpose(PS[:, 6, h * P:(h + 1) * P], pr[:, k, h].rearrange("p t k -> p (t k)"), ident[:, :])
                        last.then_inc(S["pt_mm"], 1)
                    if g == 1 and live(i - 3):
                        f = i - 3
                        pe.wait_ge(S["f_h"], 3 * (f + 1))
                        pe.wait_ge(S["ld_w2"], 32 * ((f >> 3) + 1))
                        if live(i - 2):
                            pe.wait_ge(S["f_ve"], f + 2)
                        for c, (_, n) in enumerate(FCH):
                            last = pe.matmul(PS[:, 7, 0:N], w2[0:n, c, :], hT[0:n, c, :], start=(c == 0), stop=(c == 2))
                        last.then_inc(S["f_y2"], 1)
                    if g == 2 and live(i - 2):
                        hidden(i - 2, 1)
                    if g == 3 and live(i - 1):
                        f = i - 1
                        pe.wait_ge(S["o_set"], 4 * (f + 1))
                        pe.wait_ge(S["ld_wo"], 16 * ((f >> 3) + 1))
                        wait(pe, "f_hgc", 3 * f)
                        for c in range(2 * NG):
                            last = pe.matmul(PS[:, 7, N:2 * N], wo[:, c, :], oT[:, bass.ds(f & 1, 1), c, :].squeeze(1), start=(c == 0), stop=(c == 2 * NG - 1))
                        last.then_inc(S["f_y"], 1)
                    if g == 0 and live(i - 2):
                        pe.wait_ge(S["f_sq"], i - 1)
                        pe.matmul(PS[:, 7, N:2 * N], mean_mat[:, :], var[:, :], start=True, stop=True).then_inc(S["f_var"], 1)

            def hidden(f, c):
                c0, n = FCH[c]
                pe.wait_ge(S["f_xn"], f + 1)
                pe.wait_ge(S["ld_w1"], 16 * ((f >> 3) + 1))
                wait(pe, "f_hgc", 3 * f + c)
                for half in range(2):
                    w0 = half * FI + c0
                    last = pe.matmul(PS[0:n, 7, half * N:(half + 1) * N], w1[:, w0:w0 + n], xn[:, :], start=True, stop=True)
                last.then_inc(S["f_hg"], 1)

            sweep_pairs(pe, body)
            pe.wait_ge(S["state_set"], B + ITERS)
            for q in range(4):
                for a in range(4):
                    b, t = (4 * q + a) // TT, a % TT
                    c = b * (N + 1) + 1 + t * P
                    last = pe.transpose(PS[:, q, a * P:(a + 1) * P], xT[:, c:c + P], ident[:, :])
                last.then_inc(S["o_t"], 1)


_INS = ["L0_attn_x", "L0_attn_w_qkv", "L0_attn_w_out", "L0_attn_b_out", "L0_attn_void_q", "L0_attn_void_k",
        "L0_attn_void_v", "L0_attn_attention_trace", "L0_attn_temperature_factor", "L0_ffn_Wqkv", "L0_ffn_q_scale",
        "L0_ffn_k_scale", "L0_ffn_Wo", "L0_ffn_ln_g", "L0_ffn_ln_b", "L0_ffn_W1", "L0_ffn_b1", "L0_ffn_W2", "L0_ffn_b2"]


def kernel(**inputs):
    import concourse.bacc as _bacc
    from concourse.bass_utils import run_bass_kernel_spmd as _run

    nc = _bacc.Bacc("TRN2", target_bir_lowering=False, num_devices=1)
    given = {name: np.ascontiguousarray(inputs[name]) for name in _INS if name != "L0_attn_void_q"}
    given.update(shape_constants())
    arrays, aps = {}, {}
    for name, a in given.items():
        arrays[f"in_{name}"] = a
        aps[name] = nc.dram_tensor(f"in_{name}", a.shape, mybir.dt.from_np(a.dtype), kind="ExternalInput").ap()
    result = nc.dram_tensor("result", (B, N, D), F32, kind="ExternalOutput").ap()
    bass_dual_attention(nc, aps, result)
    r = _run(nc, [arrays], core_ids=[0])
    return r.results[0]["result"]
```
